# Optimizing a Trainium2 kernel written in Bass

```python
import numpy as np
import jax
import jax.numpy as jnp

def _softmax(x, axis=-1):
    return jax.nn.softmax(x, axis=axis)

def _gelu(x):
    return jax.nn.gelu(x, approximate=True)

def _silu(x):
    return jax.nn.silu(x)

def _sigmoid(x):
    return jax.nn.sigmoid(x)

def _layernorm(x, axis=-1, eps=1e-05):
    m = jnp.mean(x, axis=axis, keepdims=True)
    v = jnp.var(x, axis=axis, keepdims=True)
    return (x - m) / jnp.sqrt(v + eps)

def _scatter_add(tgt, idx, src, axis=0):
    return tgt.at[idx].add(src)

def _segment_sum(src, seg, n):
    return jax.ops.segment_sum(src, seg, n)
kernel_name = 'mk_decoder_postln_d2_seqx_r8_ca2f4a'

def setup_inputs(seed: int=0):
    np.random.seed(seed)
    _w = jnp.asarray

    def _rec_inputs():
        import jax
        import jax.numpy as jnp
        _rk = jax.random.key(seed)
        x = -0.0002928 + 1 * jax.random.normal(jax.random.fold_in(_rk, 1), (4, 512, 128), jnp.float32)
        _lenS = 512 - jax.random.randint(jax.random.fold_in(_rk, 7), (4,), 0, max(1, 512 // 4) + 1, jnp.int32)
        _lenS2 = 154 - jax.random.randint(jax.random.fold_in(_rk, 8), (4,), 0, max(1, 154 // 4) + 1, jnp.int32)
        _ctx_1024P = jax.random.normal(jax.random.fold_in(_rk, 11), (4, 16, 128), jnp.float32)
        _ctx_1024c = jax.random.dirichlet(jax.random.fold_in(_rk, 511), 0.3 * jnp.ones((16,), jnp.float32), (4, 154))
        _ctx_1024t = jnp.einsum('bsk,bkd->bsd', _ctx_1024c, _ctx_1024P)
        _ctx_1024t = _ctx_1024t * jax.lax.rsqrt(jnp.mean(jnp.square(_ctx_1024t)) + 1e-12) * 0.953939
        ctx_1024 = -8.57375e-05 + 0.999917 * (_ctx_1024t + 0.3 * jax.random.normal(jax.random.fold_in(_rk, 611), (4, 154, 128), jnp.float32))
        _validS = jnp.arange(512)[None, :] < _lenS[:, None]
        _validS2 = jnp.arange(154)[None, :] < _lenS2[:, None]
        _causal = jnp.tril(jnp.ones((512, 512), dtype=bool))
        mask_Bx1xS2_if1 = jnp.where(jnp.ones((4, 1, 154), dtype=bool), 1, 0).astype(jnp.int32)
        mask_1x1xSxS2_ik0 = jnp.where(jnp.broadcast_to(_validS2[0:1, None, None, :], (1, 1, 512, 154)), 0, 1).astype(jnp.int32)
        return (x, ctx_1024, mask_Bx1xS2_if1, mask_1x1xSxS2_ik0)
    x, ctx_1024, mask_Bx1xS2_if1, mask_1x1xSxS2_ik0 = _rec_inputs()

    def _L0_attn_setup():
        import jax, jax.numpy as jnp
        import numpy as np
        EMBED_DIM = 128
        NUM_HEADS = 16
        HEAD_DIM = EMBED_DIM // NUM_HEADS
        FEATURE_EPS = 1e-06
        DEN_EPS = 1e-06
        key = jax.random.key(seed)
        k_x, k_qw, k_qb, k_ow, k_ob = jax.random.split(key, 5)
        b, l = (2, 256)
        x = jax.random.normal(k_x, (b, l, EMBED_DIM), dtype=jnp.float32)
        s = 1.0 / np.sqrt(EMBED_DIM)
        qkv_w = jax.random.uniform(k_qw, (3 * EMBED_DIM, EMBED_DIM), minval=-s, maxval=s, dtype=jnp.float32)
        qkv_b = jax.random.uniform(k_qb, (3 * EMBED_DIM,), minval=-s, maxval=s, dtype=jnp.float32)
        out_w = jax.random.uniform(k_ow, (EMBED_DIM, EMBED_DIM), minval=-s, maxval=s, dtype=jnp.float32)
        out_b = jax.random.uniform(k_ob, (EMBED_DIM,), minval=-s, maxval=s, dtype=jnp.float32)
        return {'x': x, 'qkv_w': qkv_w, 'qkv_b': qkv_b, 'out_w': out_w, 'out_b': out_b}
    _L0_attn_all = _L0_attn_setup()
    _L0_attn_in = {k: v for k, v in _L0_attn_all.items() if k in ('qkv_w', 'qkv_b', 'out_w', 'out_b')}
    del _L0_attn_all

    def _L0_xattn_setup():
        import jax, jax.numpy as jnp
        import numpy as np
        B, T1, T2, NFEAT, H = (8, 64, 1500, 128, 16)
        DK = NFEAT // H
        key = jax.random.key(seed)
        ks = jax.random.split(key, 8)
        s = 0.02
        return {'x': jax.random.normal(ks[0], (B, T1, NFEAT), dtype=jnp.float32), 'memory': jax.random.normal(ks[1], (B, T2, NFEAT), dtype=jnp.float32), 'memory_mask': jnp.ones((B, 1, T2), dtype=jnp.int32), 'Wq': jax.random.normal(ks[2], (NFEAT, NFEAT), dtype=jnp.float32) * s, 'bq': jnp.zeros((NFEAT,), dtype=jnp.float32), 'Wkv': jax.random.normal(ks[3], (NFEAT, 2 * NFEAT), dtype=jnp.float32) * s, 'bkv': jnp.zeros((2 * NFEAT,), dtype=jnp.float32), 'Wout': jax.random.normal(ks[4], (NFEAT, NFEAT), dtype=jnp.float32) * s, 'bout': jnp.zeros((NFEAT,), dtype=jnp.float32)}
    _L0_xattn_all = _L0_xattn_setup()
    _L0_xattn_in = {k: v for k, v in _L0_xattn_all.items() if k in ('Wq', 'bq', 'Wkv', 'bkv', 'Wout', 'bout')}
    del _L0_xattn_all

    def _L0_ffn_setup():
        import jax, jax.numpy as jnp
        import numpy as np
        EPS = 1e-12

        def rms_norm(t, gamma):
            n = jnp.maximum(jnp.linalg.norm(t, axis=-1, keepdims=True), EPS)
            scale = jnp.sqrt(jnp.asarray(t.shape[-1], t.dtype))
            return t / n * scale * gamma
        key = jax.random.key(seed)
        ks = jax.random.split(key, 4)
        b, s, d = (4, 512, 128)
        e, t = (8, 64)
        hidden = 4 * d
        return {'x': jax.random.normal(ks[0], (b, s, d), dtype=jnp.float32), 'gamma_x': jnp.ones((d,), dtype=jnp.float32), 'gamma_slot': jnp.ones((d,), dtype=jnp.float32), 'slot_embeds': jax.random.normal(ks[1], (e, t, d), dtype=jnp.float32), 'w1': jax.random.normal(ks[2], (d, hidden), dtype=jnp.float32) * (1.0 / np.sqrt(d)), 'w2': jax.random.normal(ks[3], (hidden, d), dtype=jnp.float32) * (1.0 / np.sqrt(hidden))}
    _L0_ffn_all = _L0_ffn_setup()
    _L0_ffn_in = {k: v for k, v in _L0_ffn_all.items() if k in ('gamma_x', 'gamma_slot', 'slot_embeds', 'w1', 'w2')}
    del _L0_ffn_all

    def _L1_attn_setup():
        import jax, jax.numpy as jnp
        import numpy as np
        B, N, DIM = (2, 512, 128)
        H, DH, F = (16, 64, 32)
        key = jax.random.key(seed)
        ks = jax.random.split(key, 12)
        s = 1.0 / np.sqrt(DIM)
        inp = {'x': jax.random.normal(ks[0], (B, N, DIM), jnp.float32), 'Wq': jax.random.normal(ks[1], (DIM, H * DH), jnp.float32) * s, 'bq': jax.random.normal(ks[2], (H * DH,), jnp.float32) * 0.02, 'Wk': jax.random.normal(ks[3], (DIM, H * DH), jnp.float32) * s, 'bk': jax.random.normal(ks[4], (H * DH,), jnp.float32) * 0.02, 'Wv': jax.random.normal(ks[5], (DIM, H * DH), jnp.float32) * s, 'bv': jax.random.normal(ks[6], (H * DH,), jnp.float32) * 0.02, 'Wproj': jax.random.normal(ks[7], (H * DH, DIM), jnp.float32) * s, 'bproj': jax.random.normal(ks[8], (DIM,), jnp.float32) * 0.02, 'wq_feat': jax.random.normal(ks[9], (DH, F), jnp.float32) / np.sqrt(DH), 'wk_feat': jax.random.normal(ks[10], (DH, F), jnp.float32) / np.sqrt(DH)}
        return inp
    _L1_attn_all = _L1_attn_setup()
    _L1_attn_in = {k: v for k, v in _L1_attn_all.items() if k in ('Wq', 'bq', 'Wk', 'bk', 'Wv', 'bv', 'Wproj', 'bproj', 'wq_feat', 'wk_feat')}
    del _L1_attn_all

    def _L1_xattn_setup():
        import jax, jax.numpy as jnp
        import numpy as np
        B, S, D, H = (2, 256, 128, 16)
        DK = D // H
        key = jax.random.key(seed)
        ks = jax.random.split(key, 12)
        std = 1.0 / np.sqrt(D)
        inp = {'query': jax.random.normal(ks[0], (B, S, D), jnp.float32), 'key': jax.random.normal(ks[1], (B, S, D), jnp.float32), 'value': jax.random.normal(ks[2], (B, S, D), jnp.float32), 'mask': jnp.tril(jnp.ones((S, S), jnp.int32))[None, None, :, :], 'Wq': jax.random.normal(ks[3], (D, D), jnp.float32) * std, 'bq': jax.random.normal(ks[4], (D,), jnp.float32) * std, 'Wk': jax.random.normal(ks[5], (D, D), jnp.float32) * std, 'bk': jax.random.normal(ks[6], (D,), jnp.float32) * std, 'Wv': jax.random.normal(ks[7], (D, D), jnp.float32) * std, 'bv': jax.random.normal(ks[8], (D,), jnp.float32) * std, 'Wo': jax.random.normal(ks[9], (D, D), jnp.float32) * std, 'bo': jax.random.normal(ks[10], (D,), jnp.float32) * std}
        return inp
    _L1_xattn_all = _L1_xattn_setup()
    _L1_xattn_in = {k: v for k, v in _L1_xattn_all.items() if k in ('Wq', 'bq', 'Wk', 'bk', 'Wv', 'bv', 'Wo', 'bo')}
    del _L1_xattn_all

    def _L1_ffn_setup():
        import jax, jax.numpy as jnp
        import numpy as np
        B, S, D = (8, 64, 128)
        H = 16
        DFF = 512
        E = 4
        K = 2
        EPS = 1e-05

        def _layernorm(x, w, b):
            m = x.mean(-1, keepdims=True)
            v = ((x - m) ** 2).mean(-1, keepdims=True)
            return (x - m) / jnp.sqrt(v + EPS) * w + b

        def _encoder_layer(x, iw, ib, ow, ob, l1w, l1b, l2w, l2b, n1w, n1b, n2w, n2b):
            b, s, d = x.shape
            hd = d // H
            qkv = x @ iw.T + ib
            q, k, v = jnp.split(qkv, 3, axis=-1)
            rs = lambda t: t.reshape(b, s, H, hd).transpose(0, 2, 1, 3)
            q, k, v = (rs(q), rs(k), rs(v))
            scale = jnp.asarray(hd, x.dtype) ** 0.5
            scores = jnp.einsum('bhqd,bhkd->bhqk', q, k) / scale
            attn = jax.nn.softmax(scores, axis=-1)
            o = jnp.einsum('bhqk,bhkd->bhqd', attn, v).transpose(0, 2, 1, 3).reshape(b, s, d)
            o = o @ ow.T + ob
            x = _layernorm(x + o, n1w, n1b)
            ff = jax.nn.relu(x @ l1w.T + l1b) @ l2w.T + l2b
            return _layernorm(x + ff, n2w, n2b)
        key = jax.random.key(seed)
        ks = jax.random.split(key, 12)
        g = lambda k, shape: jax.random.normal(k, shape, dtype=jnp.float32) * 0.02
        return {'x': jax.random.normal(ks[0], (B, S, D), dtype=jnp.float32), 'in_proj_w': g(ks[1], (E, 3 * D, D)), 'in_proj_b': g(ks[2], (E, 3 * D)), 'out_proj_w': g(ks[3], (E, D, D)), 'out_proj_b': g(ks[4], (E, D)), 'ln1_w': jnp.ones((E, D), jnp.float32), 'ln1_b': jnp.zeros((E, D), jnp.float32), 'lin1_w': g(ks[5], (E, DFF, D)), 'lin1_b': g(ks[6], (E, DFF)), 'lin2_w': g(ks[7], (E, D, DFF)), 'lin2_b': g(ks[8], (E, D)), 'ln2_w': jnp.ones((E, D), jnp.float32), 'ln2_b': jnp.zeros((E, D), jnp.float32), 'gate_w': g(ks[9], (E, D)), 'gate_b': g(ks[10], (E,))}
    _L1_ffn_all = _L1_ffn_setup()
    _L1_ffn_in = {k: v for k, v in _L1_ffn_all.items() if k in ('in_proj_w', 'in_proj_b', 'out_proj_w', 'out_proj_b', 'ln1_w', 'ln1_b', 'lin1_w', 'lin1_b', 'lin2_w', 'lin2_b', 'ln2_w', 'ln2_b', 'gate_w', 'gate_b')}
    del _L1_ffn_all
    return {'x': x, 'ctx_1024': ctx_1024, 'mask_Bx1xS2_if1': mask_Bx1xS2_if1, 'mask_1x1xSxS2_ik0': mask_1x1xSxS2_ik0, 'L0_attn_qkv_w': _L0_attn_in['qkv_w'], 'L0_attn_qkv_b': _L0_attn_in['qkv_b'], 'L0_attn_out_w': _L0_attn_in['out_w'], 'L0_attn_out_b': _L0_attn_in['out_b'], 'L0_xattn_Wq': _L0_xattn_in['Wq'], 'L0_xattn_bq': _L0_xattn_in['bq'], 'L0_xattn_Wkv': _L0_xattn_in['Wkv'], 'L0_xattn_bkv': _L0_xattn_in['bkv'], 'L0_xattn_Wout': _L0_xattn_in['Wout'], 'L0_xattn_bout': _L0_xattn_in['bout'], 'L0_ffn_gamma_x': _L0_ffn_in['gamma_x'], 'L0_ffn_gamma_slot': _L0_ffn_in['gamma_slot'], 'L0_ffn_slot_embeds': _L0_ffn_in['slot_embeds'], 'L0_ffn_w1': _L0_ffn_in['w1'], 'L0_ffn_w2': _L0_ffn_in['w2'], 'L1_attn_Wq': _L1_attn_in['Wq'], 'L1_attn_bq': _L1_attn_in['bq'], 'L1_attn_Wk': _L1_attn_in['Wk'], 'L1_attn_bk': _L1_attn_in['bk'], 'L1_attn_Wv': _L1_attn_in['Wv'], 'L1_attn_bv': _L1_attn_in['bv'], 'L1_attn_Wproj': _L1_attn_in['Wproj'], 'L1_attn_bproj': _L1_attn_in['bproj'], 'L1_attn_wq_feat': _L1_attn_in['wq_feat'], 'L1_attn_wk_feat': _L1_attn_in['wk_feat'], 'L1_xattn_Wq': _L1_xattn_in['Wq'], 'L1_xattn_bq': _L1_xattn_in['bq'], 'L1_xattn_Wk': _L1_xattn_in['Wk'], 'L1_xattn_bk': _L1_xattn_in['bk'], 'L1_xattn_Wv': _L1_xattn_in['Wv'], 'L1_xattn_bv': _L1_xattn_in['bv'], 'L1_xattn_Wo': _L1_xattn_in['Wo'], 'L1_xattn_bo': _L1_xattn_in['bo'], 'L1_ffn_in_proj_w': _L1_ffn_in['in_proj_w'], 'L1_ffn_in_proj_b': _L1_ffn_in['in_proj_b'], 'L1_ffn_out_proj_w': _L1_ffn_in['out_proj_w'], 'L1_ffn_out_proj_b': _L1_ffn_in['out_proj_b'], 'L1_ffn_ln1_w': _L1_ffn_in['ln1_w'], 'L1_ffn_ln1_b': _L1_ffn_in['ln1_b'], 'L1_ffn_lin1_w': _L1_ffn_in['lin1_w'], 'L1_ffn_lin1_b': _L1_ffn_in['lin1_b'], 'L1_ffn_lin2_w': _L1_ffn_in['lin2_w'], 'L1_ffn_lin2_b': _L1_ffn_in['lin2_b'], 'L1_ffn_ln2_w': _L1_ffn_in['ln2_w'], 'L1_ffn_ln2_b': _L1_ffn_in['ln2_b'], 'L1_ffn_gate_w': _L1_ffn_in['gate_w'], 'L1_ffn_gate_b': _L1_ffn_in['gate_b']}

def reference(x, ctx_1024, mask_Bx1xS2_if1, mask_1x1xSxS2_ik0, L0_attn_qkv_w, L0_attn_qkv_b, L0_attn_out_w, L0_attn_out_b, L0_xattn_Wq, L0_xattn_bq, L0_xattn_Wkv, L0_xattn_bkv, L0_xattn_Wout, L0_xattn_bout, L0_ffn_gamma_x, L0_ffn_gamma_slot, L0_ffn_slot_embeds, L0_ffn_w1, L0_ffn_w2, L1_attn_Wq, L1_attn_bq, L1_attn_Wk, L1_attn_bk, L1_attn_Wv, L1_attn_bv, L1_attn_Wproj, L1_attn_bproj, L1_attn_wq_feat, L1_attn_wk_feat, L1_xattn_Wq, L1_xattn_bq, L1_xattn_Wk, L1_xattn_bk, L1_xattn_Wv, L1_xattn_bv, L1_xattn_Wo, L1_xattn_bo, L1_ffn_in_proj_w, L1_ffn_in_proj_b, L1_ffn_out_proj_w, L1_ffn_out_proj_b, L1_ffn_ln1_w, L1_ffn_ln1_b, L1_ffn_lin1_w, L1_ffn_lin1_b, L1_ffn_lin2_w, L1_ffn_lin2_b, L1_ffn_ln2_w, L1_ffn_ln2_b, L1_ffn_gate_w, L1_ffn_gate_b):
    import jax
    import jax.numpy as jnp

    def _L0_attn_ref(x, qkv_w, qkv_b, out_w, out_b):
        import jax, jax.numpy as jnp
        import numpy as np
        EMBED_DIM = 128
        NUM_HEADS = 16
        HEAD_DIM = EMBED_DIM // NUM_HEADS
        FEATURE_EPS = 1e-06
        DEN_EPS = 1e-06
        b, l, e = x.shape
        qkv = (x @ qkv_w.T + qkv_b).reshape(b, l, 3, NUM_HEADS, HEAD_DIM)
        qkv = jnp.transpose(qkv, (2, 0, 3, 1, 4))
        q, k, v = (qkv[0], qkv[1], qkv[2])
        q = jax.nn.relu(q) + FEATURE_EPS
        k = jax.nn.relu(k) + FEATURE_EPS
        kv = jnp.cumsum(jnp.einsum('bhld,bhle->bhlde', k, v), axis=2)
        k_cum = jnp.cumsum(k, axis=2)
        num = jnp.einsum('bhld,bhlde->bhle', q, kv)
        den = jnp.maximum(jnp.einsum('bhld,bhld->bhl', q, k_cum)[..., None], DEN_EPS)
        out = num / den
        out = jnp.transpose(out, (0, 2, 1, 3)).reshape(b, l, e)
        return out @ out_w.T + out_b

    def _L0_xattn_ref(x, memory, memory_mask, Wq, bq, Wkv, bkv, Wout, bout):
        import jax, jax.numpy as jnp
        import numpy as np
        B, T1, T2, NFEAT, H = (8, 64, 1500, 128, 16)
        DK = NFEAT // H
        b, t1, _ = x.shape
        t2 = memory.shape[1]
        q = x @ Wq + bq
        kv = memory @ Wkv + bkv
        k, v = jnp.split(kv, 2, axis=-1)
        q_h = q.reshape(b, t1, H, DK).transpose(0, 2, 1, 3)
        k_h = k.reshape(b, t2, H, DK).transpose(0, 2, 1, 3)
        v_h = v.reshape(b, t2, H, DK).transpose(0, 2, 1, 3)
        q_h = q_h * DK ** (-0.5)
        scores = jnp.einsum('bhqd,bhkd->bhqk', q_h, k_h)
        mask0 = memory_mask[:, None, :, :] == 0
        scores = jnp.where(mask0, -jnp.inf, scores)
        attn = jax.nn.softmax(scores, axis=-1)
        attn = jnp.where(mask0, 0.0, attn)
        ctx = jnp.einsum('bhqk,bhkd->bhqd', attn, v_h)
        ctx = ctx.transpose(0, 2, 1, 3).reshape(b, t1, H * DK)
        return ctx @ Wout + bout

    def _L0_ffn_ref(x, gamma_x, gamma_slot, slot_embeds, w1, w2):
        import jax, jax.numpy as jnp
        import numpy as np
        EPS = 1e-12

        def rms_norm(t, gamma):
            n = jnp.maximum(jnp.linalg.norm(t, axis=-1, keepdims=True), EPS)
            scale = jnp.sqrt(jnp.asarray(t.shape[-1], t.dtype))
            return t / n * scale * gamma
        b, s, d = x.shape
        e, t, _ = slot_embeds.shape
        xn = rms_norm(x, gamma_x)
        se = rms_norm(slot_embeds, gamma_slot)
        logits = jnp.einsum('bsd,etd->bset', xn, se)
        dispatch = jax.nn.softmax(logits, axis=1)
        slots = jnp.einsum('bsd,bset->betd', xn, dispatch)
        h = jax.nn.gelu(slots @ w1, approximate=False)
        processed = h @ w2
        combine = jax.nn.softmax(logits.reshape(b, s, e * t), axis=-1)
        out = jnp.einsum('bnd,bsn->bsd', processed.reshape(b, e * t, d), combine)
        return out

    def _L1_attn_ref(x, Wq, bq, Wk, bk, Wv, bv, Wproj, bproj, wq_feat, wk_feat):
        import jax, jax.numpy as jnp
        import numpy as np
        B, N, DIM = (2, 512, 128)
        H, DH, F = (16, 64, 32)
        b, n, _ = x.shape
        q = (x @ Wq + bq).reshape(b, n, H, DH)
        k = (x @ Wk + bk).reshape(b, n, H, DH)
        v = (x @ Wv + bv).reshape(b, n, H, DH)
        q_prime = jnp.exp(jnp.einsum('bnhd,df->bnhf', q, wq_feat))
        k_prime = jnp.exp(jnp.einsum('bnhd,df->bnhf', k, wk_feat))
        k_sum = k_prime.sum(axis=1)
        D_inv = 1.0 / (jnp.einsum('bnhf,bhf->bnh', q_prime, k_sum) + 1e-06)
        context = jnp.einsum('bnhf,bnhd->bhfd', k_prime, v)
        out = jnp.einsum('bnhf,bhfd,bnh->bnhd', q_prime, context, D_inv)
        out = out.reshape(b, n, H * DH)
        return out @ Wproj + bproj

    def _L1_xattn_ref(query, key, value, mask, Wq, bq, Wk, bk, Wv, bv, Wo, bo):
        import jax, jax.numpy as jnp
        import numpy as np
        B, S, D, H = (2, 256, 128, 16)
        DK = D // H
        b = query.shape[0]
        Q = query @ Wq.T + bq
        K = key @ Wk.T + bk
        V = value @ Wv.T + bv
        Q = Q.reshape(b, -1, H, DK).transpose(0, 2, 1, 3)
        K = K.reshape(b, -1, H, DK).transpose(0, 2, 1, 3)
        V = V.reshape(b, -1, H, DK).transpose(0, 2, 1, 3)
        scores = jnp.einsum('bhqd,bhkd->bhqk', Q, K) / jnp.sqrt(jnp.float32(DK))
        scores = jnp.where(mask == 0, -jnp.inf, scores)
        weights = jax.nn.softmax(scores, axis=-1)
        attn = jnp.einsum('bhqk,bhkd->bhqd', weights, V)
        attn = attn.transpose(0, 2, 1, 3).reshape(b, -1, D)
        return attn @ Wo.T + bo

    def _L1_ffn_ref(x, in_proj_w, in_proj_b, out_proj_w, out_proj_b, ln1_w, ln1_b, lin1_w, lin1_b, lin2_w, lin2_b, ln2_w, ln2_b, gate_w, gate_b):
        import jax, jax.numpy as jnp
        import numpy as np
        B, S, D = (8, 64, 128)
        H = 16
        DFF = 512
        E = 4
        K = 2
        EPS = 1e-05

        def _layernorm(x, w, b):
            m = x.mean(-1, keepdims=True)
            v = ((x - m) ** 2).mean(-1, keepdims=True)
            return (x - m) / jnp.sqrt(v + EPS) * w + b

        def _encoder_layer(x, iw, ib, ow, ob, l1w, l1b, l2w, l2b, n1w, n1b, n2w, n2b):
            b, s, d = x.shape
            hd = d // H
            qkv = x @ iw.T + ib
            q, k, v = jnp.split(qkv, 3, axis=-1)
            rs = lambda t: t.reshape(b, s, H, hd).transpose(0, 2, 1, 3)
            q, k, v = (rs(q), rs(k), rs(v))
            scale = jnp.asarray(hd, x.dtype) ** 0.5
            scores = jnp.einsum('bhqd,bhkd->bhqk', q, k) / scale
            attn = jax.nn.softmax(scores, axis=-1)
            o = jnp.einsum('bhqk,bhkd->bhqd', attn, v).transpose(0, 2, 1, 3).reshape(b, s, d)
            o = o @ ow.T + ob
            x = _layernorm(x + o, n1w, n1b)
            ff = jax.nn.relu(x @ l1w.T + l1b) @ l2w.T + l2b
            return _layernorm(x + ff, n2w, n2b)
        gate_logits = x.mean(axis=1) @ gate_w.T + gate_b
        _, top_idx = jax.lax.top_k(gate_logits, K)
        gate_weights = jax.nn.softmax(gate_logits, axis=-1)
        mask = jnp.zeros_like(gate_weights).at[jnp.arange(x.shape[0])[:, None], top_idx].set(1.0)
        expert_outs = jax.vmap(_encoder_layer, in_axes=(None, 0, 0, 0, 0, 0, 0, 0, 0, 0, 0, 0, 0))(x, in_proj_w, in_proj_b, out_proj_w, out_proj_b, lin1_w, lin1_b, lin2_w, lin2_b, ln1_w, ln1_b, ln2_w, ln2_b)
        return jnp.einsum('be,ebsd->bsd', gate_weights * mask, expert_outs)
    x = _layernorm(x + _L0_attn_ref(x, L0_attn_qkv_w, L0_attn_qkv_b, L0_attn_out_w, L0_attn_out_b), axis=-1)
    x = _layernorm(x + _L0_xattn_ref(x, ctx_1024, mask_Bx1xS2_if1, L0_xattn_Wq, L0_xattn_bq, L0_xattn_Wkv, L0_xattn_bkv, L0_xattn_Wout, L0_xattn_bout), axis=-1)
    x = _layernorm(x + _L0_ffn_ref(x, L0_ffn_gamma_x, L0_ffn_gamma_slot, L0_ffn_slot_embeds, L0_ffn_w1, L0_ffn_w2), axis=-1)
    x = _layernorm(x + _L1_attn_ref(x, L1_attn_Wq, L1_attn_bq, L1_attn_Wk, L1_attn_bk, L1_attn_Wv, L1_attn_bv, L1_attn_Wproj, L1_attn_bproj, L1_attn_wq_feat, L1_attn_wk_feat), axis=-1)
    x = _layernorm(x + _L1_xattn_ref(x, ctx_1024, ctx_1024, mask_1x1xSxS2_ik0, L1_xattn_Wq, L1_xattn_bq, L1_xattn_Wk, L1_xattn_bk, L1_xattn_Wv, L1_xattn_bv, L1_xattn_Wo, L1_xattn_bo), axis=-1)
    x = _layernorm(x + _L1_ffn_ref(x, L1_ffn_in_proj_w, L1_ffn_in_proj_b, L1_ffn_out_proj_w, L1_ffn_out_proj_b, L1_ffn_ln1_w, L1_ffn_ln1_b, L1_ffn_lin1_w, L1_ffn_lin1_b, L1_ffn_lin2_w, L1_ffn_lin2_b, L1_ffn_ln2_w, L1_ffn_ln2_b, L1_ffn_gate_w, L1_ffn_gate_b), axis=-1)
    return x

_drawn_inputs = setup_inputs


def setup_inputs(seed=0):
    import zlib

    import numpy as np

    out = dict(_drawn_inputs(seed))
    spreads = {'L0_xattn_bq': (0.0, 2.0),
     'L0_xattn_bkv': (0.0, 0.1),
     'L0_xattn_bout': (0.0, 0.1),
     'L0_ffn_gamma_x': (1.0, 0.2),
     'L0_ffn_gamma_slot': (1.0, 0.2),
     'L1_ffn_ln1_w': (1.0, 0.2),
     'L1_ffn_ln1_b': (0.0, 0.3),
     'L1_ffn_ln2_w': (1.0, 0.2),
     'L1_ffn_ln2_b': (0.0, 0.291)}
    factors = {'L0_xattn_Wq': 64.0,
     'L1_attn_bq': 59.26,
     'L1_attn_bk': 51.249,
     'L1_attn_bproj': 4.066,
     'L1_xattn_bk': 64.0,
     'L1_ffn_in_proj_w': 5.342,
     'L1_ffn_in_proj_b': 8.0,
     'L1_ffn_out_proj_w': 4.673,
     'L1_ffn_out_proj_b': 8.0,
     'L1_ffn_lin1_w': 3.438,
     'L1_ffn_lin1_b': 33.016,
     'L1_ffn_lin2_b': 8.0,
     'L1_ffn_gate_b': 8.0}
    for name, (base, spread) in spreads.items():
        noise = np.random.default_rng([zlib.crc32(name.encode()), seed]).standard_normal(out[name].shape)
        drawn = base * np.exp(spread * noise) if base else spread * noise
        out[name] = jnp.asarray(drawn.astype(out[name].dtype))
    for name, factor in factors.items():
        out[name] = (out[name] * factor).astype(out[name].dtype)
    return out
```

```python
from contextlib import ExitStack

import concourse.bass as bass
from concourse import mybir

F32 = mybir.dt.float32
F16 = mybir.dt.float16
I32 = mybir.dt.int32
U32 = mybir.dt.uint32
ALU = mybir.AluOpType
ACT = mybir.ActivationFunctionType
AX = mybir.AxisListType

B, S, D = 4, 512, 128
H, DH = 16, 8
NG, GH = 4, 4
P = 128
NT = S // P
SK = 154
SKP = P + 32
ST = 3 * GH * DH
MR = ST + 2 * GH
MSCALE = 256.0
MCAP = 1.6e7
BIG = 60000.0
FH = 16
FD, FF = 64, 32
HID = 512
NSLOT = 512
NE, TOPK = 4, 2
EWC = 3 * D + D + HID + HID
EWN = EWC + 2 + HID // P
LN_EPS = 1e-5


def attention_signals(kind):
    units, pairs, msteps = shape_of(kind)
    both = {"projected": 3, "biased": 2, "split": 2, "selected": 2 * NG, "stacked": 2 * NG, "v_ready": 1, "k_ready": 1,
            "heads_turned": 1, "turned_out": 1, "y_ready": 1, "scored": NG * pairs, "weighted": NG * pairs,
            "pv_done": NG * units, "o_out": NG, "o_turned": NG, "normed": NG}
    own = {"diagonal": NG * pairs} if kind == "causal" else {
        "max_scored": NG * msteps, "reduced": NG * msteps, "m_parts": NG, "m_turned": NG, "m_rows": NG}
    return {**both, **own}


def shape_of(kind):
    return (NT, 2 * NT, NT * GH) if kind in ("causal", "self") else (2, 3, 2 * NT)


class Attention:

    def __init__(self, kind, sems, turn, nk, wait, wq, wk, wv, wo, bq, bk, bv, scale, kst, src):
        self.kind, self.turn, self.nk, self.wait = kind, turn, nk, wait
        self.self_keys = kind in ("causal", "self")
        self.has_max = kind != "causal"
        self.units, self.pairs, self.msteps = shape_of(kind)
        self.counts = attention_signals(kind)
        self.wq, self.wk, self.wv, self.wo = wq, wk, wv, wo
        self.bq, self.bk, self.bv, self.scale = bq, bk, bv, scale
        self.kst, self.src = kst, src
        self.projected, self.biased, self.split = sems["projected"], sems["biased"], sems["split"]
        self.selected, self.stacked = sems["selected"], sems["stacked"]
        self.v_ready, self.k_ready = sems["v_ready"], sems["k_ready"]
        self.heads_turned, self.turned_out, self.y_ready = sems["heads_turned"], sems["turned_out"], sems["y_ready"]
        self.scored, self.weighted, self.pv_done = sems["scored"], sems["weighted"], sems["pv_done"]
        self.o_out, self.o_turned, self.normed = sems["o_out"], sems["o_turned"], sems["normed"]
        if self.has_max:
            self.max_scored, self.reduced, self.m_parts = sems["max_scored"], sems["reduced"], sems["m_parts"]
            self.m_turned, self.m_rows = sems["m_turned"], sems["m_rows"]
        else:
            self.diagonal = sems["diagonal"]

    def past(self, what):
        return self.turn * self.counts[what]


def build(nc, t):
    with ExitStack() as ctx:
        def sb(name, shape, dt=F32):
            return ctx.enter_context(nc.sbuf_tensor(name, shape, dt))

        sems = []

        def sem(name):
            sems.append(ctx.enter_context(nc.semaphore(name)))
            return sems[-1]

        eye = sb("eye", [P, P])
        blockmask = sb("blockmask", [P, P])
        causal = sb("causal", [P, P])
        colmask = sb("colmask", [P, GH])
        eye16 = sb("eye16", [P, P], F16)
        bigeye = sb("bigeye", [P, P], F16)
        select = sb("select", [P, 2, NG, ST], F16)
        select_q = sb("select_q", [P, 2, NG, ST], F16)
        bigrow = sb("bigrow", [1, S], F16)
        ones = sb("ones", [P, P])
        half = sb("half", [P, NT])
        cols = sb("cols", [P, 6])
        cols_s = sb("cols_s", [P, 6])
        rows = sb("rows", [P, 9, D])
        w_a = sb("w_a", [P, 12, D])
        w1 = sb("w1", [P, HID])
        w2 = sb("w2", [P, NT, D])
        slot_raw = sb("slot_raw", [P, NT, D])
        slot_T = sb("slot_T", [P, NSLOT])
        feat = sb("feat", [FD, 2, FF])
        fbias = sb("fbias", [FD, 3, FH])
        bias_rep_v = sb("bias_rep_v", [FD, FH, FF])
        wqf = sb("wqf", [P, FH * FF])
        wkf = sb("wkf", [P, FH * FF])
        bqf = sb("bqf", [P, NG])
        bkf = sb("bkf", [P, FH * FF])
        wvp = sb("wvp", [P, FH, D])
        bvp = sb("bvp", [P, NG, D])
        headrep = sb("headrep", [FH, NG, P])
        gate_w = sb("gate_w", [P, NE])
        gate_b = sb("gate_b", [1, NE])
        mask_q = sb("mask_q", [P, NT, SKP], I32)
        bias_q = sb("bias_q", [P, NT, SKP], F16)

        x = sb("x", [P, NT, D + 1])
        x_T = sb("x_T", [P, S])
        xb = sb("xb", [P, 2, NT, D])
        r = sb("r", [P, NT, D])
        stats = sb("stats", [P, NT, 6])
        mv = sb("mv", [P, NT, 2])
        var = sb("var", [P, 11, NT])
        rstd = sb("rstd", [P, 11, NT])
        c_T = sb("c_T", [P, SKP + 96])
        mask_k = sb("mask_k", [1, SKP], I32)
        bias_k = sb("bias_k", [1, SKP], F16)
        q_full, k_full = sb("q_full", [P, S]), sb("k_full", [P, S])
        q_hi, q_lo = sb("q_hi", [P, S], F16), sb("q_lo", [P, S], F16)
        k_hi, k_lo = sb("k_hi", [P, S], F16), sb("k_lo", [P, S], F16)
        k_dense = sb("k_dense", [P, NG, S], F16)
        k_st = sb("k_st", [P, NG, GH, S], F16)
        k_stx = sb("k_stx", [P, NG, GH, SKP], F16)
        q_st = sb("q_st", [P, NG, S], F16)
        v = sb("v", [P, NT, H, 32])
        pt = sb("pt", [P, 2, GH, S])
        neg_max = sb("neg_max", [P, NG, NT, GH])
        m_full = sb("m_full", [P, NT, GH])
        m_parts = sb("m_parts", [P, NT, 2, GH], F16)
        o_sb = sb("o_sb", [P, 2, S])
        rden = sb("rden", [P, NT, GH])
        heads = sb("heads", [P, NT, D])
        heads_T = sb("heads_T", [P, S])
        hid = sb("hid", [P, NT, S])
        halves = [pt[:, 0, :, :], pt[:, 1, :, :]]
        wq_t, wk_t, wv_t = [a[0:FD].rearrange("p t (a d) -> p (t a) d", d=D) for a in (*halves, hid[:, :, :])]
        wp, bias_rep = [k_st[0:FD, i:i + 2, :, :].rearrange("p a b k -> p (a b k)").bitcast(F32)
                        .rearrange("p (h d) -> p h d", h=FH) for i in (0, 2)]
        xn = sb("xn", [P, NT, D + 1])
        xn_T = sb("xn_T", [P, S])
        squares = sb("squares", [P, D])
        nmax = sb("nmax", [P, 2, NT])
        nm_full = sb("nm_full", [P, 2, NT])
        nm_parts = sb("nm_parts", [P, 2, NT, 2], F16)
        nm_row = sb("nm_row", [2, 2, S], F16)
        scale_rows = sb("scale_rows", [2, P], F16)
        disp, comb = halves
        slots = sb("slots", [P, NT, D])
        slots_T = sb("slots_T", [P, NSLOT])
        rsum = sb("rsum", [P, 2, NT])
        proc = sb("proc", [P, NT, D + 1])
        qp, qn = halves
        kpre = sb("kpre", [P, 2, S])
        kp = hid
        kx = sb("kx", [P, NG, D])
        ks = sb("ks", [P, NG])
        ksc = sb("ksc", [P, NG, FH])
        headmask = sb("headmask", [P, NG, FH])
        kx_T = sb("kx_T", [P, FH * FF])
        den = sb("den", [FH, S])
        dinv = sb("dinv", [FH, S])
        z = sb("z", [P, NG, D])
        ew = [sb(f"ew{s}", [P, EWN]) for s in range(TOPK)]
        er = [sb(f"er{s}", [P, 7, D]) for s in range(TOPK)]
        ebq = sb("ebq", [P, TOPK])
        xsum = sb("xsum", [P, 1])
        logit8 = sb("logit8", [1, 8])
        top8 = sb("top8", [1, 8])
        idx8 = sb("idx8", [1, 8], U32)
        gexp = sb("gexp", [1, 8])
        gdiff = sb("gdiff", [1, 8])
        gsum = sb("gsum", [1, 2])
        gw1 = sb("gw1", [1, 2])
        gw = sb("gw", [P, 2])
        x1 = sb("x1", [P, NT, D])
        x1_T = sb("x1_T", [P, S])
        norm = sb("norm", [P, NT, D])
        acc = sb("acc", [P, NT, D])

        p_s = ctx.enter_context(nc.psum_tensor("p_s", [P, 2, 2 * S], F32))
        p_m = ctx.enter_context(nc.psum_tensor("p_m", [P, 2, S], F32))
        p_o = ctx.enter_context(nc.psum_tensor("p_o", [P, S], F32))
        p_t = ctx.enter_context(nc.psum_tensor("p_t", [P, S], F32))
        p_t16 = p_t[:, :].bitcast(F16)
        y = p_o[:, :].rearrange("p (t d) -> p t d", t=NT)
        bank = [p_s[:, 0, 0:S], p_s[:, 0, S:2 * S], p_s[:, 1, 0:S], p_s[:, 1, S:2 * S]]

        load_w, load_c, setup = sem("load_w"), sem("load_c"), sem("setup")
        s_pre, s_pre_ev = sem("pre_products"), sem("pre_evacuated")
        x_loaded, ctx_loaded = sem("x_loaded"), sem("ctx_loaded")
        dve_step, pool_step = sem("dve_step"), sem("pool_step")
        x_done, xt_turned, xt_done = sem("x_done"), sem("xt_turned"), sem("xt_done")
        xb_done, var_ready, rstd_ready = sem("xb_done"), sem("var_ready"), sem("rstd_ready")
        mask_ready = sem("mask_ready")
        stored = sem("stored")
        (m_xn, m_xnt, m_xnte, m_logit, m_red, m_rowt, m_row, m_again, m_exp, m_slot, m_slots, m_slt, m_slte, m_hid,
         m_gelu, m_proc, m_proce, m_out, m_outr) = [sem(f"mix_{n}") for n in (
             "normed", "turned", "turned_out", "logits", "reduced", "rows_turned", "rows", "rescored", "weights",
             "slots", "slots_out", "slots_turned", "slots_t", "hidden", "gelu", "processed", "processed_out",
             "combined", "read")]
        (f_q, f_qe, f_k, f_kb, f_ke, f_kx, f_kxe, f_kxt, f_kxte, f_den, f_dene, f_rep, f_qn, f_z, f_ze, f_y) = [
            sem(f"feat_{n}") for n in ("q", "q_exp", "k", "k_biased", "k_exp", "kx", "kx_out", "kx_turned",
                                       "kx_t", "den", "den_inv", "den_rep", "q_scaled", "z", "z_out", "y")]
        g_sum, g_logit, g_top, g_exp, g_w, g_rep, g_out = [sem(f"gate_{n}") for n in (
            "sum", "logits", "top", "exp", "weights", "spread", "ready")]
        e_bias, e_x1, e_x1t, e_x1te, e_hid, e_relu, e_y2, e_done = [sem(f"expert_{n}") for n in (
            "bias", "x1", "x1_turned", "x1_t", "hidden", "relu", "y2", "done")]
        e_load = [sem(f"expert_loaded{s}") for s in range(TOPK)]

        lin = {what: sem(f"linear_{what}") for what in attention_signals("causal")}
        cross = {what: sem(f"cross_{what}") for what in attention_signals("cross_key")}
        expert = {what: sem(f"expert_{what}") for what in attention_signals("self")}
        A0 = Attention("causal", lin, 0, S, lambda e: e.wait_ge(x_loaded, 32), wq=w_a[:, 0, :], wk=w_a[:, 1, :],
                       wv=w_a[:, 2, :], wo=w_a[:, 3, :], bq=cols[:, 0:1], bk=cols[:, 1:2], bv=rows[:, 0, :],
                       scale=1.0, kst=k_st, src=x_T)
        AX0 = Attention("cross_key", cross, 0, SKP, lambda e: e.wait_ge(xt_done, 1), wq=w_a[:, 4, :],
                        wk=w_a[:, 5, :], wv=w_a[:, 6, :], wo=w_a[:, 7, :], bq=cols_s[:, 2:3], bk=cols[:, 3:4],
                        bv=rows[:, 2, :], scale=DH ** -0.5, kst=k_stx, src=c_T)
        AX1 = Attention("cross_full", cross, 1, SKP, lambda e: e.wait_ge(xt_done, 3), wq=w_a[:, 8, :],
                        wk=w_a[:, 9, :], wv=w_a[:, 10, :], wo=w_a[:, 11, :], bq=cols_s[:, 4:5], bk=cols[:, 5:6],
                        bv=rows[:, 4, :], scale=DH ** -0.5, kst=k_stx, src=c_T)

        def expert_wait(s):
            def f(e):
                e.wait_ge(xt_done, 4)
                e.wait_ge(e_load[s], 32)
                e.wait_ge(e_bias, s + 1)
                if s:
                    e.wait_ge(e_done, s)
            return f

        AE = [Attention("self", expert, s, S, expert_wait(s), wq=ew[s][:, 0:D], wk=ew[s][:, D:2 * D],
                        wv=ew[s][:, 2 * D:3 * D], wo=ew[s][:, 3 * D:4 * D], bq=ebq[:, s:s + 1],
                        bk=ew[s][:, EWC + 1:EWC + 2], bv=er[s][:, 0, :], scale=DH ** -0.5, kst=k_st, src=x_T)
              for s in range(TOPK)]

        select_banks = [p_m[:, 0, :], p_m[:, 1, :], p_t[:, :], p_o[:, :]]

        with nc.Block() as block:
            @block.sync
            def _(sp):
                n = 0
                for dst, src in ((eye[:, :], t["c32"][:, 0:P]), (blockmask[:, :], t["c32"][:, P:2 * P]),
                                 (causal[:, :], t["c32"][:, 2 * P:3 * P]), (colmask[:, :], t["c32"][:, 3 * P:3 * P + GH]),
                                 (headmask[:, :, :], t["c32"][:, 3 * P + GH:3 * P + GH + NG * FH]),
                                 (headrep[:, :, :], t["headrep"]),
                                 (eye16[:, :], t["c16"][:, 0:P]), (bigeye[:, :], t["c16"][:, P:2 * P]),
                                 (select[:, :, :, :], t["c16"][:, 2 * P:2 * P + 2 * NG * ST]),
                                 (select_q[:, :, :, :], t["c16"][:, 2 * P + 2 * NG * ST:]),
                                 (k_st[ST:MR, :, :, :], t["krows"]), (k_stx[ST:MR, :, :, :], t["krows_x"]),
                                 (scale_rows[:, :], t["scale_rows"]), (bigrow[:, :], t["bigrow"])):
                    sp.dma_start(dst, src).then_inc(load_c, 16)
                    n += 1
                assert n == 14
                for dst, src in ((cols[:, :], t["cols"]), (rows[:, :, :], t["rows"].partition_broadcast(P)),
                                 (w_a[:, :, :], t["w_a"]), (w1[:, :], t["w1"]), (w2[:, :, :], t["w2"]),
                                 (slot_raw[:, :, :], t["slots"]), (wq_t[:, :, :], t["wq_t"]),
                                 (wk_t[:, :, :], t["wk_t"]), (wv_t[:, :, :], t["wv_t"]), (wp[:, :, :], t["wp"]),
                                 (feat[:, :, :], t["feat"]), (fbias[:, :, :], t["fbias"]),
                                 (gate_w[:, :], t["gate_w"]), (gate_b[:, :], t["gate_b"])):
                    sp.dma_start(dst, src).then_inc(load_w, 16)
                sp.wait_ge(setup, 1)
                sp.dma_start(mask_q[:, :, 0:SK], t["mask_q"]).then_inc(load_w, 16)

            @block.vector
            def _(dve):
                step = [0]

                def link(ins):
                    step[0] += 1
                    ins.then_inc(dve_step, 1)
                    dve.wait_ge(dve_step, step[0])

                nc.vector.memset(mask_q[:, :, :], 0).then_inc(setup, 1)
                nc.vector.memset(ones[:, :], 1.0)
                nc.vector.memset(half[:, :], -0.5)
                nc.vector.memset(c_T[:, :], 0.0)
                nc.vector.memset(mask_k[:, :], 0)
                nc.vector.memset(x[:, :, D:D + 1], 1.0)
                nc.vector.memset(xn[:, :, D:D + 1], 1.0)
                nc.vector.memset(proc[:, :, D:D + 1], 1.0)
                nc.vector.memset(logit8[:, :], -3.0e38)
                link(nc.vector.memset(v[:, :, :, :], 0.0))
                nc.vector.memset(v[:, :, :, DH:DH + 1], 1.0)
                dve.wait_ge(load_w, 16 * 15)
                nc.vector.tensor_scalar(cols_s[:, :], cols[:, :], DH ** -0.5, None, ALU.mult)
                nc.vector.tensor_scalar(rows[:, 7:9, :], rows[:, 7:9, :], float(D) ** 0.5, None, ALU.mult)
                nc.vector.tensor_scalar(bias_q[:, :, :], mask_q[:, :, :], 0, -BIG, ALU.is_equal, ALU.mult)
                nc.vector.tensor_copy(bias_rep[:, :, :], fbias[:, 1, :].unsqueeze(2).to_broadcast([FD, FH, P]))
                link(nc.vector.tensor_copy(bias_rep_v[:, :, :], fbias[:, 2, :].unsqueeze(2).to_broadcast([FD, FH, FF])))
                for j in range(NT):
                    link(nc.vector.tensor_tensor(squares[:, :], slot_raw[:, j, :], slot_raw[:, j, :], ALU.mult))
                    link(nc.vector.tensor_reduce(var[:, 0, j:j + 1], squares[:, :], AX.X, ALU.add))
                nc.vector.tensor_scalar(var[:, 0, :], var[:, 0, :], 1e-24, None, ALU.max).then_inc(var_ready, 1)
                dve.wait_ge(rstd_ready, 1)
                for j in range(NT):
                    last = nc.vector.scalar_tensor_tensor(out=slots[:, j, :], in0=slot_raw[:, j, :],
                                                          scalar=rstd[:, 0, j:j + 1], in1=rows[:, 8, :],
                                                          op0=ALU.mult, op1=ALU.mult)
                last.then_inc(setup, 1)
                dve.wait_ge(s_pre, 1)
                nc.vector.tensor_copy(wqf[:, :], bank[0])
                nc.vector.tensor_copy(wkf[:, :], bank[1])
                nc.vector.tensor_copy(bqf[:, :], p_m[:, 0, 0:NG])
                nc.vector.tensor_copy(bkf[:, :], bank[2])
                nc.vector.tensor_copy(bvp[:, :, :], bank[3].rearrange("p (g d) -> p g d", g=NG))
                nc.vector.tensor_copy(slot_T[:, :], p_t[:, :]).then_inc(s_pre_ev, 1)
                dve.wait_ge(s_pre, 2)
                for q in range(4):
                    last = nc.vector.tensor_copy(wvp[:, 4 * q:4 * q + 4, :],
                                                 bank[q].rearrange("p (g d) -> p g d", g=4))
                last.then_inc(s_pre_ev, 1)

            @block.gpsimd
            def _(pool):
                pool.wait_ge(var_ready, 1)
                nc.gpsimd.tensor_tensor(rstd[:, 0, :], var[:, 0, :], half[:, :], ALU.pow).then_inc(rstd_ready, 1)

            @block.tensor
            def _(pe):
                pe.wait_ge(load_w, 16 * 15)
                pe.wait_ge(load_c, 16 * 14)
                pe.wait_ge(setup, 2)
                for h in range(FH):
                    g, G = h % GH, h // GH
                    nc.tensor.matmul(bank[0][:, h * FF:(h + 1) * FF], wq_t[:, h, :], feat[:, 0, :], start=True, stop=True)
                    nc.tensor.matmul(bank[1][:, h * FF:(h + 1) * FF], wk_t[:, h, :], feat[:, 1, :], start=True, stop=True)
                    nc.tensor.matmul(bank[2][:, h * FF:(h + 1) * FF], bias_rep[:, h, :], feat[:, 1, :], start=True, stop=True)
                    nc.tensor.matmul(p_m[FF * g:FF * (g + 1), 0, G:G + 1], feat[:, 0, :], fbias[:, 0, h:h + 1],
                                     start=True, stop=True)
                    nc.tensor.matmul(bank[3][FF * g:FF * (g + 1), G * D:(G + 1) * D], bias_rep_v[:, h, :], wp[:, h, :],
                                     start=True, stop=True)
                for j in range(NT):
                    last = nc.tensor.transpose(p_t[:, j * P:(j + 1) * P], slots[:, j, :], eye[:, :])
                last.then_inc(s_pre, 1)
                pe.wait_ge(s_pre_ev, 1)
                for h in range(FH):
                    last = nc.tensor.matmul(bank[h // 4][:, (h % 4) * D:(h % 4 + 1) * D], wv_t[:, h, :], wp[:, h, :],
                                            start=True, stop=True)
                last.then_inc(s_pre, 1)

        nc.all_engine_barrier()
        nc.gpsimd.sem_clear(range(sems[0].num, sems[-1].num + 1))
        nc.all_engine_barrier()

        with nc.Fori(0, B) as b:
            with nc.Block() as block:

                @block.sync
                def _(sp):
                    one = lambda a: a[bass.ds(b, 1)].squeeze(0)
                    sp.dma_start(x_T[:, :], one(t["x_T"])).then_inc(x_loaded, 16)
                    sp.dma_start(x[:, :, 0:D], one(t["x"]).rearrange("(t p) d -> p t d", p=P)).then_inc(x_loaded, 16)
                    sp.dma_start(c_T[:, 0:SK], one(t["ctx_T"])).then_inc(ctx_loaded, 16)
                    for i in range(1, 4):
                        sp.dma_start(c_T[:, P + 32 * i:P + 32 * i + SK - P], one(t["ctx_T"])[:, P:SK]).then_inc(ctx_loaded, 16)
                    sp.dma_start(mask_k[:, 0:SK], one(t["mask_k"])).then_inc(ctx_loaded, 16)
                    sp.wait_ge(g_top, 1)
                    for s in range(TOPK):
                        e = sp.value_load(idx8[0:1, s:s + 1], min_val=0, max_val=NE - 1)
                        sp.dma_start(ew[s][:, :], t["ew"][bass.ds(e, 1)].squeeze(0)).then_inc(e_load[s], 16)
                        sp.dma_start(er[s][:, :, :], t["er"][bass.ds(e, 1)].squeeze(0).partition_broadcast(P)).then_inc(e_load[s], 16)
                    sp.wait_ge(x_done, 6)
                    sp.dma_start(one(t["out"]).rearrange("(t p) d -> p t d", p=P), x[:, :, 0:D]).then_inc(stored, 16)
                    sp.wait_ge(stored, 16)

                @block.gpsimd
                def _(pool):
                    npow, nxb = [0], [0]

                    def residual(bias, ready, count, src=x):
                        pool.wait_ge(ready, count)
                        nc.gpsimd.tensor_tensor(xb[:, nxb[0] % 2, :, :], src[:, :, 0:D],
                                                bias.unsqueeze(1).to_broadcast([P, NT, D]), ALU.add).then_inc(xb_done, 1)
                        nxb[0] += 1

                    def rsqrt():
                        k = npow[0]
                        pool.wait_ge(var_ready, k + 1)
                        nc.gpsimd.tensor_tensor(rstd[:, k, :], var[:, k, :], half[:, :], ALU.pow).then_inc(rstd_ready, 1)
                        npow[0] += 1

                    residual(rows[:, 1, :], x_loaded, 32)
                    rsqrt()
                    residual(rows[:, 3, :], x_done, 1)
                    rsqrt()
                    rsqrt()
                    rsqrt()
                    residual(rows[:, 6, :], x_done, 3)
                    rsqrt()
                    residual(rows[:, 5, :], x_done, 4)
                    rsqrt()
                    for s in range(TOPK):
                        pool.wait_ge(e_load[s], 32)
                        residual(er[s][:, 1, :], x_done, 5)
                        rsqrt()
                        residual(er[s][:, 4, :], e_x1, s + 1, x1)
                        rsqrt()
                    rsqrt()

                @block.tensor
                def _(pe):
                    mm, tr = nc.tensor.matmul, nc.tensor.transpose

                    def attention(a):
                        a.wait(pe)
                        if not a.self_keys:
                            pe.wait_ge(ctx_loaded, 16 * 5)
                        mm(bank[1][:, 0:a.nk], a.wk, a.src[:, 0:a.nk], start=True, stop=True).then_inc(a.projected, 1)
                        mm(bank[0], a.wq, x_T[:, :], start=True, stop=True).then_inc(a.projected, 1)
                        for kt in range(a.units):
                            last = mm(bank[2][:, kt * D:(kt + 1) * D], a.src[:, kt * P:(kt + 1) * P], a.wv,
                                      start=True, stop=True)
                        last.then_inc(a.projected, 1)
                        for i in range(2 * NG):
                            G, keys = i % NG, i < NG
                            if G == 0:
                                pe.wait_ge(a.split, a.past("split") + (1 if keys else 2))
                            if i >= NG:
                                pe.wait_ge(a.stacked, a.past("stacked") + i - NG + 1)
                            n, hi, lo, sel = (a.nk, k_hi, k_lo, select) if keys else (S, q_hi, q_lo, select_q)
                            mm(select_banks[G][0:ST, 0:n], sel[:, 0, G, :], hi[:, 0:n], start=True, stop=False)
                            mm(select_banks[G][0:ST, 0:n], sel[:, 1, G, :], lo[:, 0:n], start=False, stop=True)\
                                .then_inc(a.selected, 1)

                        def max_step(G, i):
                            n = G * a.msteps + i
                            if n == 0:
                                pe.wait_ge(a.k_ready, a.past("k_ready") + 1)
                                pe.wait_ge(a.stacked, a.past("stacked") + 2 * NG)
                            if n >= 2:
                                pe.wait_ge(a.reduced, a.past("reduced") + n - 1)
                            if a.self_keys:
                                qt, g = i // GH, i % GH
                                mm(p_m[:, n % 2, 0:a.nk], q_st[0:ST, G, qt * P:(qt + 1) * P], a.kst[0:ST, G, g, 0:a.nk],
                                   start=True, stop=True).then_inc(a.max_scored, 1)
                                return
                            qt = i // 2
                            for j in range(2):
                                g = 2 * (i % 2) + j
                                out = p_m[:, n % 2, j * SKP:(j + 1) * SKP]
                                mm(out, q_st[0:ST, G, qt * P:(qt + 1) * P], a.kst[0:ST, G, g, :], start=True, stop=False)
                                if a.kind == "cross_key":
                                    last = mm(out, bigrow[0:1, 0:P], bias_k[0:1, :], start=False, stop=True)
                                else:
                                    last = mm(out, bigeye[:, :], bias_q[:, qt, :], start=False, stop=True)
                            last.then_inc(a.max_scored, 1)

                        def turn_max(G):
                            pe.wait_ge(a.m_parts, a.past("m_parts") + G + 1)
                            if G >= 2:
                                pe.wait_ge(a.normed, a.past("normed") + G - 1)
                            for qt in range(NT):
                                last = tr(p_t16[ST:MR, qt * P:(qt + 1) * P], m_parts[:, qt, :, :], eye16[:, :])
                            last.then_inc(a.m_turned, 1)

                        def free_scores(n):
                            if n < 2:
                                return
                            pe.wait_ge(a.weighted, a.past("weighted") + n - 1)

                        def score(G, kt, pair):
                            n = G * a.pairs + 2 * kt + pair
                            free_scores(n)
                            if kt == 0 and pair == 0:
                                if a.has_max:
                                    pe.wait_ge(a.m_rows, a.past("m_rows") + G + 1)
                                if G == 0:
                                    pe.wait_ge(a.v_ready, a.past("v_ready") + 1)
                                    pe.wait_ge(a.k_ready, a.past("k_ready") + 1)
                                    pe.wait_ge(a.stacked, a.past("stacked") + 2 * NG)
                            K = MR if a.has_max else ST
                            if a.self_keys or kt == 0:
                                for j in range(2):
                                    g = 2 * pair + j
                                    lo = kt * P if a.kind == "causal" else 0
                                    out = p_s[:, n % 2, j * S:(j + 1) * S]
                                    last = mm(out[:, lo:S], a.kst[0:K, G, g, kt * P:(kt + 1) * P], q_st[0:K, G, lo:S],
                                              start=True, stop=a.self_keys)
                                    if a.kind == "cross_key":
                                        last = mm(out, bias_k[0:1, 0:P], bigrow[0:1, :], start=False, stop=True)
                                    if a.kind == "cross_full":
                                        for qt in range(NT):
                                            last = mm(out[:, qt * P:(qt + 1) * P], bias_q[:, qt, 0:P], bigeye[:, :],
                                                      start=False, stop=qt == NT - 1)
                            else:
                                for g in range(GH):
                                    out = p_s[32 * g:32 * g + 32, n % 2, 0:S]
                                    mm(out, a.kst[0:K, G, g, P:SKP], q_st[0:K, G, :], start=True, stop=False)
                                    if a.kind == "cross_key":
                                        last = mm(out, bias_k[0:1, P:SKP], bigrow[0:1, :], start=False, stop=True,
                                                  tile_position=(0, 32 * g))
                                    else:
                                        for qt in range(NT):
                                            last = mm(out[:, qt * P:(qt + 1) * P], bias_q[:, qt, P:SKP], bigeye[:, :],
                                                      start=False, stop=qt == NT - 1)
                            last.then_inc(a.scored, 1)

                        def weigh(u):
                            G, kt = divmod(u, a.units)
                            done = G * a.pairs + min(2 * kt + 2, a.pairs)
                            if a.has_max:
                                pe.wait_ge(a.weighted, a.past("weighted") + done)
                            else:
                                pe.wait_ge(a.diagonal, a.past("diagonal") + done)
                            if kt == 0 and G:
                                pe.wait_ge(a.o_out, a.past("o_out") + G)
                            rest = not a.self_keys and kt == 1
                            for g in range(GH):
                                k0, k1 = (32 * g, 32 * g + 32) if rest else (0, P)
                                lo = kt * P if a.kind == "causal" else 0
                                last = mm(p_o[32 * g:32 * g + 32, lo:S], v[k0:k1, kt, GH * G + g, :],
                                          pt[k0:k1, u % 2, 0 if rest else g, lo:S], start=kt == 0,
                                          stop=kt == a.units - 1 or a.kind == "causal", skip_group_check=True)
                            last.then_inc(a.pv_done, 1)

                        def turn_out(G):
                            pe.wait_ge(a.o_out, a.past("o_out") + G + 1)
                            if a.has_max:
                                pe.wait_ge(a.m_rows, a.past("m_rows") + min(G + 2, NG))
                            if G:
                                pe.wait_ge(a.normed, a.past("normed") + G)
                            for qt in range(NT):
                                last = tr(p_t[:, qt * P:(qt + 1) * P], o_sb[:, G % 2, qt * P:(qt + 1) * P], eye[:, :])
                            last.then_inc(a.o_turned, 1)

                        if a.has_max:
                            for i in range(a.msteps):
                                max_step(0, i)
                        per_unit = a.msteps // a.units
                        for u in range(NG * a.units):
                            G, kt = divmod(u, a.units)
                            ahead = range(kt * per_unit, (kt + 1) * per_unit) if a.has_max and G < NG - 1 else ()
                            for i in ahead[0:2]:
                                max_step(G + 1, i)
                            if kt == 0 and a.has_max:
                                turn_max(G)
                            score(G, kt, 0)
                            for i in ahead[2:]:
                                max_step(G + 1, i)
                            if a.self_keys or kt == 0:
                                score(G, kt, 1)
                            if u:
                                weigh(u - 1)
                            if kt == 1 and G:
                                turn_out(G - 1)
                        weigh(NG * a.units - 1)
                        turn_out(NG - 1)
                        pe.wait_ge(a.normed, a.past("normed") + NG)
                        for qt in range(NT):
                            last = tr(p_t[:, qt * P:(qt + 1) * P], heads[:, qt, :], eye[:, :])
                        last.then_inc(a.heads_turned, 1)
                        pe.wait_ge(a.turned_out, a.past("turned_out") + 1)
                        for qt in range(NT):
                            last = mm(y[:, qt, :], heads_T[:, qt * P:(qt + 1) * P], a.wo, start=True, stop=True)
                        last.then_inc(a.y_ready, 1)

                    def turn_x(n):
                        pe.wait_ge(x_done, n)
                        for i in range(NT):
                            last = tr(p_t[:, i * P:(i + 1) * P], x[:, i, 0:D], eye[:, :])
                        last.then_inc(xt_turned, 1)

                    attention(A0)
                    turn_x(1)
                    attention(AX0)

                    pe.wait_ge(m_xn, 1)
                    for i in range(NT):
                        last = tr(p_t[:, i * P:(i + 1) * P], xn[:, i, 0:D], eye[:, :])
                    last.then_inc(m_xnt, 1)
                    pe.wait_ge(m_xnte, 1)
                    for i in range(NT):
                        mm(bank[i], xn_T[:, i * P:(i + 1) * P], slot_T[:, :], start=True, stop=True).then_inc(m_logit, 1)
                    for j in range(NT):
                        if j >= 2:
                            pe.wait_ge(m_red, NT + j - 1)
                        mm(p_m[:, j % 2, :], slot_T[:, j * P:(j + 1) * P], xn_T[:, :], start=True, stop=True)\
                            .then_inc(m_logit, 1)
                    pe.wait_ge(m_red, 2 * NT + 1)
                    for which in range(2):
                        for i in range(NT):
                            last = tr(p_t16[0:2, which * S + i * P:which * S + (i + 1) * P], nm_parts[:, which, i, :],
                                      eye16[:, :])
                    last.then_inc(m_rowt, 1)
                    pe.wait_ge(m_row, 1)
                    for k in range(2 * NT):
                        i, which = k % NT, k // NT
                        if k >= NT:
                            pe.wait_ge(m_exp, k - NT + 1)
                        st, mv_ = (xn_T[:, i * P:(i + 1) * P], slot_T) if which == 0 else \
                            (slot_T[:, i * P:(i + 1) * P], xn_T)
                        mm(bank[i], st, mv_[:, :], start=True, stop=False)
                        mm(bank[i], scale_rows[:, :], nm_row[:, 1 - which, :], start=False, stop=True).then_inc(m_again, 1)
                    for j in range(NT):
                        for i in range(NT):
                            if j == 0:
                                pe.wait_ge(m_exp, i + 1)
                            last = mm(p_m[:, j // 2, (j % 2) * (D + 1):(j % 2 + 1) * (D + 1)],
                                      disp[:, i, j * P:(j + 1) * P], xn[:, i, :], start=i == 0, stop=i == NT - 1)
                    last.then_inc(m_slot, 1)
                    pe.wait_ge(m_slots, 1)
                    for j in range(NT):
                        last = tr(p_t[:, j * P:(j + 1) * P], slots[:, j, :], eye[:, :])
                    last.then_inc(m_slt, 1)
                    pe.wait_ge(m_slte, 1)
                    pe.wait_ge(m_exp, 2 * NT)
                    for k in range(NT):
                        mm(bank[k], w1[:, k * P:(k + 1) * P], slots_T[:, :], start=True, stop=True).then_inc(m_hid, 1)
                    pe.wait_ge(m_gelu, NT)
                    for j in range(NT):
                        for k in range(NT):
                            last = mm(y[:, j, :], hid[:, k, j * P:(j + 1) * P], w2[:, k, :], start=k == 0, stop=k == NT - 1)
                    last.then_inc(m_proc, 1)
                    pe.wait_ge(m_proce, 1)
                    for i in range(NT):
                        for j in range(NT):
                            last = mm(p_m[:, i // 2, (i % 2) * (D + 1):(i % 2 + 1) * (D + 1)],
                                      comb[:, j, i * P:(i + 1) * P], proc[:, j, :], start=j == 0, stop=j == NT - 1)
                    last.then_inc(m_out, 1)
                    turn_x(3)

                    pe.wait_ge(xt_done, 3 - 1)
                    for G in range(NG):
                        mm(bank[G], wqf[:, G * P:(G + 1) * P], x_T[:, :], start=True, stop=True).then_inc(f_q, 1)
                    for i in range(NT):
                        if i >= 2:
                            pe.wait_ge(f_kb, i - 1)
                        mm(p_m[:, i % 2, :], x_T[:, i * P:(i + 1) * P], wkf[:, :], start=True, stop=True).then_inc(f_k, 1)
                    pe.wait_ge(f_kb, NT)
                    pe.wait_ge(f_ke, NT)
                    for G in range(NG):
                        for i in range(NT):
                            last = mm(p_m[:, G // 2, (G % 2) * (D + 1):(G % 2 + 1) * (D + 1)], kp[:, i, G * P:(G + 1) * P],
                                      x[:, i, :], start=i == 0, stop=i == NT - 1)
                    last.then_inc(f_kx, 1)
                    pe.wait_ge(f_kxe, 1)
                    pe.wait_ge(f_qe, NG)
                    for G in range(NG):
                        last = mm(p_o[0:FH, :], ksc[:, G, :], qp[:, G, :], start=G == 0, stop=G == NG - 1)
                    last.then_inc(f_den, 1)
                    for G in range(NG):
                        last = tr(p_t[:, G * P:(G + 1) * P], kx[:, G, :], eye[:, :])
                    last.then_inc(f_kxt, 1)
                    pe.wait_ge(f_kxte, 1)
                    for h in range(FH):
                        G, g = divmod(h, GH)
                        last = mm(p_m[FF * g:FF * (g + 1), 0, G * D:(G + 1) * D], kx_T[:, h * FF:(h + 1) * FF],
                                  wvp[:, h, :], start=True, stop=True)
                    last.then_inc(f_z, 1)
                    pe.wait_ge(f_dene, 1)
                    for G in range(NG):
                        mm(bank[G], headrep[:, G, :], dinv[:, :], start=True, stop=True).then_inc(f_rep, 1)
                    pe.wait_ge(f_ze, 1)
                    pe.wait_ge(f_qn, NG)
                    for i in range(NT):
                        for G in range(NG):
                            last = mm(y[:, i, :], qn[:, G, i * P:(i + 1) * P], z[:, G, :], start=G == 0, stop=G == NG - 1)
                    last.then_inc(f_y, 1)
                    turn_x(4)
                    attention(AX1)
                    turn_x(5)

                    pe.wait_ge(g_sum, 1)
                    mm(p_o[0:1, 0:NE], xsum[:, :], gate_w[:, :], start=True, stop=True).then_inc(g_logit, 1)
                    pe.wait_ge(g_w, 1)
                    mm(p_o[:, 8:10], ones[0:1, :], gw1[:, :], start=True, stop=True).then_inc(g_rep, 1)
                    pe.wait_ge(g_out, 1)

                    for s in range(TOPK):
                        attention(AE[s])
                        pe.wait_ge(e_x1, s + 1)
                        for i in range(NT):
                            last = tr(p_t[:, i * P:(i + 1) * P], x1[:, i, :], eye[:, :])
                        last.then_inc(e_x1t, 1)
                        pe.wait_ge(e_x1te, s + 1)
                        for k in range(NT):
                            mm(bank[k], ew[s][:, 4 * D + k * P:4 * D + (k + 1) * P], x1_T[:, :], start=True, stop=True)\
                                .then_inc(e_hid, 1)
                        pe.wait_ge(e_relu, NT * (s + 1))
                        for i in range(NT):
                            for k in range(NT):
                                last = mm(y[:, i, :], hid[:, k, i * P:(i + 1) * P],
                                          ew[s][:, 4 * D + HID + k * D:4 * D + HID + (k + 1) * D],
                                          start=k == 0, stop=k == NT - 1)
                        last.then_inc(e_y2, 1)

                @block.scalar
                def _(act):
                    actv = nc.scalar.activation

                    def attention(a):
                        act.wait_ge(a.projected, a.past("projected") + 1)
                        actv(k_full[:, 0:a.nk], bank[1][:, 0:a.nk], ACT.Identity, bias=a.bk).then_inc(a.biased, 1)
                        act.wait_ge(a.projected, a.past("projected") + 2)
                        actv(q_full[:, :], bank[0], ACT.Identity, bias=a.bq, scale=a.scale).then_inc(a.biased, 1)
                        for i in range(2 * NG):
                            G, keys = i % NG, i < NG
                            act.wait_ge(a.selected, a.past("selected") + i + 1)
                            dst, n = (k_dense, a.nk) if keys else (q_st, S)
                            nc.scalar.copy(dst[0:ST, G, 0:n], select_banks[G][0:ST, 0:n]).then_inc(a.stacked, 1)

                        def weights(u, pair):
                            G, kt = divmod(u, a.units)
                            n = G * a.pairs + 2 * kt + pair
                            act.wait_ge(a.scored, a.past("scored") + n + 1)
                            if u >= 2:
                                act.wait_ge(a.pv_done, a.past("pv_done") + u - 1)
                            src = p_s[:, n % 2, :].rearrange("p (j q) -> p j q", j=2)
                            dst = pt[:, u % 2, 2 * pair:2 * pair + 2, :]
                            if a.kind == "causal":
                                nc.scalar.copy(dst[:, :, kt * P:S], src[:, :, kt * P:S]).then_inc(a.weighted, 1)
                            elif a.self_keys or kt == 0:
                                actv(dst, src, ACT.Exp).then_inc(a.weighted, 1)
                            else:
                                actv(pt[:, u % 2, 0, :], p_s[:, n % 2, 0:S], ACT.Exp).then_inc(a.weighted, 1)

                        def outputs(G):
                            act.wait_ge(a.pv_done, a.past("pv_done") + (G + 1) * a.units)
                            if G >= 2:
                                act.wait_ge(a.o_turned, a.past("o_turned") + G - 1)
                            nc.scalar.copy(o_sb[:, G % 2, :], p_o[:, :]).then_inc(a.o_out, 1)

                        for u in range(NG * a.units):
                            G, kt = divmod(u, a.units)
                            weights(u, 0)
                            if a.self_keys or kt == 0:
                                weights(u, 1)
                            if kt == 0 and G:
                                outputs(G - 1)
                        outputs(NG - 1)
                        act.wait_ge(a.heads_turned, a.past("heads_turned") + 1)
                        nc.scalar.copy(heads_T[:, :], p_t[:, :]).then_inc(a.turned_out, 1)

                    def x_turned(n):
                        act.wait_ge(xt_turned, n)
                        nc.scalar.copy(x_T[:, :], p_t[:, :]).then_inc(xt_done, 1)

                    attention(A0)
                    x_turned(1)
                    attention(AX0)

                    act.wait_ge(m_xnt, 1)
                    nc.scalar.copy(xn_T[:, :], p_t[:, :]).then_inc(m_xnte, 1)
                    act.wait_ge(m_rowt, 1)
                    nc.scalar.copy(nm_row[:, :, :], p_t16[0:2, :].rearrange("p (w s) -> p w s", w=2)).then_inc(m_row, 1)
                    for k in range(2 * NT):
                        i, which = k % NT, k // NT
                        act.wait_ge(m_again, k + 1)
                        actv((disp if which == 0 else comb)[:, i, :], bank[i], ACT.Exp).then_inc(m_exp, 1)
                    act.wait_ge(m_slt, 1)
                    nc.scalar.copy(slots_T[:, :], p_t[:, :]).then_inc(m_slte, 1)
                    for k in range(NT):
                        act.wait_ge(m_hid, k + 1)
                        actv(hid[:, k, :], bank[k], ACT.Gelu).then_inc(m_gelu, 1)
                    act.wait_ge(m_proc, 1)
                    nc.scalar.copy(proc[:, :, 0:D], y).then_inc(m_proce, 1)
                    x_turned(2)

                    for G in range(NG):
                        act.wait_ge(f_q, G + 1)
                        actv(qp[:, G, :], bank[G], ACT.Exp, bias=bqf[:, G:G + 1]).then_inc(f_qe, 1)
                    for i in range(NT):
                        act.wait_ge(f_kb, i + 1)
                        actv(kp[:, i, :], kpre[:, i % 2, :], ACT.Exp).then_inc(f_ke, 1)
                    act.wait_ge(f_kxt, 1)
                    nc.scalar.copy(kx_T[:, :], p_t[:, :]).then_inc(f_kxte, 1)
                    x_turned(3)
                    attention(AX1)
                    x_turned(4)

                    act.wait_ge(g_top, 1)
                    actv(gexp[0:1, 0:NE], gdiff[0:1, 0:NE], ACT.Exp, accum_out=gsum[0:1, 0:1])
                    actv(gexp[0:1, 4:6], gdiff[0:1, 4:6], ACT.Exp).then_inc(g_exp, 1)

                    for s in range(TOPK):
                        attention(AE[s])
                        act.wait_ge(e_x1t, s + 1)
                        nc.scalar.copy(x1_T[:, :], p_t[:, :]).then_inc(e_x1te, 1)
                        for k in range(NT):
                            act.wait_ge(e_hid, NT * s + k + 1)
                            actv(hid[:, k, :], bank[k], ACT.Relu, bias=ew[s][:, EWC + 2 + k:EWC + 3 + k]).then_inc(e_relu, 1)

                @block.vector
                def _(dve):
                    V = nc.vector
                    step, npow, nxb = [0], [0], [0]

                    def link(ins):
                        step[0] += 1
                        ins.then_inc(dve_step, 1)
                        dve.wait_ge(dve_step, step[0])

                    def attention(a):
                        for i, (full, hi, lo, n) in enumerate(((k_full, k_hi, k_lo, a.nk), (q_full, q_hi, q_lo, S))):
                            dve.wait_ge(a.biased, a.past("biased") + i + 1)
                            if a.kind == "causal":
                                link(V.tensor_scalar(full[:, 0:n], full[:, 0:n], 0.0, 1e-6, ALU.max, ALU.add))
                            link(V.tensor_copy(hi[:, 0:n], full[:, 0:n]))
                            V.tensor_tensor(lo[:, 0:n], full[:, 0:n], hi[:, 0:n], ALU.subtract).then_inc(a.split, 1)
                        dve.wait_ge(a.projected, a.past("projected") + 3)
                        V.tensor_tensor(v[:, 0:a.units, :, 0:DH],
                                        bank[2][:, 0:a.units * D].rearrange("p (k h d) -> p k h d", k=a.units, h=H),
                                        a.bv.rearrange("p (h d) -> p h d", h=H).unsqueeze(1)
                                        .to_broadcast([P, a.units, H, DH]), ALU.add).then_inc(a.v_ready, 1)
                        dve.wait_ge(a.stacked, a.past("stacked") + NG)
                        for g in range(GH):
                            last = V.tensor_scalar(a.kst[0:ST, :, g, 0:a.nk], k_dense[0:ST, :, 0:a.nk],
                                                   colmask[0:ST, g:g + 1], None, ALU.mult)
                        last.then_inc(a.k_ready, 1)

                        def reduce(G, i):
                            n = G * a.msteps + i
                            dve.wait_ge(a.max_scored, a.past("max_scored") + n + 1)
                            if a.self_keys:
                                qt, g = i // GH, i % GH
                                V.tensor_reduce(neg_max[:, G, qt, g:g + 1], p_m[:, n % 2, 0:a.nk], AX.X, ALU.max,
                                                negate=True).then_inc(a.reduced, 1)
                            else:
                                qt, g = i // 2, 2 * (i % 2)
                                V.tensor_reduce(neg_max[:, G, qt, g:g + 2],
                                                p_m[:, n % 2, 0:2 * SKP].rearrange("p (j k) -> p j k", j=2), AX.X,
                                                ALU.max, negate=True).then_inc(a.reduced, 1)

                        def parts(G):
                            dve.wait_ge(a.reduced, a.past("reduced") + (G + 1) * a.msteps)
                            link(V.tensor_scalar(m_full[:, :, :], neg_max[:, G, :, :], MCAP, 1.0 / MSCALE, ALU.min, ALU.mult))
                            if G:
                                dve.wait_ge(a.m_turned, a.past("m_turned") + G)
                            link(V.tensor_copy(m_parts[:, :, 0, :], m_full[:, :, :]))
                            V.tensor_tensor(m_parts[:, :, 1, :], m_full[:, :, :], m_parts[:, :, 0, :], ALU.subtract)\
                                .then_inc(a.m_parts, 1)

                        def m_rows(G):
                            dve.wait_ge(a.m_turned, a.past("m_turned") + G + 1)
                            V.tensor_copy(q_st[ST:MR, G, :], p_t16[ST:MR, 0:S]).then_inc(a.m_rows, 1)

                        def diagonal(u, pair):
                            G, kt = divmod(u, a.units)
                            n = G * a.pairs + 2 * kt + pair
                            dve.wait_ge(a.weighted, a.past("weighted") + n + 1)
                            block_ = pt[:, u % 2, 2 * pair:2 * pair + 2, kt * P:(kt + 1) * P]
                            V.tensor_tensor(block_, block_, causal[:, :].unsqueeze(1).to_broadcast([P, 2, P]), ALU.mult)\
                                .then_inc(a.diagonal, 1)

                        def normalise(G):
                            dve.wait_ge(a.o_turned, a.past("o_turned") + G + 1)
                            o = p_t[:, :].rearrange("p (t g c) -> p t g c", t=NT, g=GH)
                            if a.kind in ("causal", "cross_key"):
                                link(V.tensor_scalar(rden[:, :, :], o[:, :, :, DH], 1e-6 if a.kind == "causal" else 1e-30,
                                                     None, ALU.max))
                                link(V.reciprocal(rden[:, :, :], rden[:, :, :]))
                            else:
                                link(V.reciprocal(rden[:, :, :], o[:, :, :, DH]))
                            V.tensor_tensor(heads[:, :, 4 * DH * G:4 * DH * (G + 1)].rearrange("p t (g d) -> p t g d", g=GH),
                                            o[:, :, :, 0:DH], rden[:, :, :].unsqueeze(3).to_broadcast([P, NT, GH, DH]),
                                            ALU.mult).then_inc(a.normed, 1)

                        if a.has_max:
                            for i in range(a.msteps):
                                reduce(0, i)
                            parts(0)
                        per_unit = a.msteps // a.units
                        for u in range(NG * a.units):
                            G, kt = divmod(u, a.units)
                            ahead = range(kt * per_unit, (kt + 1) * per_unit) if a.has_max and G < NG - 1 else ()
                            for i in ahead[0:2]:
                                reduce(G + 1, i)
                            if kt == 0 and a.has_max:
                                m_rows(G)
                            for i in ahead[2:]:
                                reduce(G + 1, i)
                            if a.kind == "causal":
                                diagonal(u, 0)
                                diagonal(u, 1)
                            if kt == 1 and G:
                                normalise(G - 1)
                            if kt == a.units - 1 and a.has_max and G < NG - 1:
                                parts(G + 1)
                        normalise(NG - 1)

                    def rsqrt(src, eps, op=ALU.add):
                        k = npow[0]
                        V.tensor_scalar(var[:, k, :], src, eps, None, op).then_inc(var_ready, 1)
                        dve.wait_ge(rstd_ready, k + 1)
                        npow[0] += 1
                        return k

                    def layernorm(dst):
                        for i in range(NT):
                            last = V.bn_stats(stats[:, i, :], r[:, i, :])
                        link(last)
                        for i in range(NT):
                            last = V.bn_aggr(mv[:, i, :], stats[:, i, :])
                        link(last)
                        k = rsqrt(mv[:, :, 1], LN_EPS)
                        for i in range(NT):
                            last = V.tensor_scalar(dst(i), r[:, i, :], mv[:, i, 0:1], rstd[:, k, i:i + 1],
                                                   ALU.subtract, ALU.mult)
                        return last

                    def add_residual(ready, count):
                        dve.wait_ge(ready, count)
                        dve.wait_ge(xb_done, nxb[0] + 1)
                        link(V.tensor_tensor(r[:, :, :], y, xb[:, nxb[0] % 2, :, :], ALU.add))
                        nxb[0] += 1

                    def new_x():
                        layernorm(lambda i: x[:, i, 0:D]).then_inc(x_done, 1)

                    dve.wait_ge(ctx_loaded, 16 * 5)
                    V.tensor_scalar(bias_k[:, :], mask_k[:, :], 0, -BIG, ALU.is_equal, ALU.mult).then_inc(mask_ready, 1)

                    attention(A0)
                    add_residual(A0.y_ready, 1)
                    new_x()
                    attention(AX0)
                    add_residual(AX0.y_ready, 1)
                    new_x()

                    dve.wait_ge(x_done, 2)
                    for i in range(NT):
                        link(V.tensor_tensor(squares[:, :], x[:, i, 0:D], x[:, i, 0:D], ALU.mult))
                        link(V.tensor_reduce(nmax[:, 0, i:i + 1], squares[:, :], AX.X, ALU.add))
                    k = rsqrt(nmax[:, 0, :], 1e-24, ALU.max)
                    for i in range(NT):
                        last = V.scalar_tensor_tensor(out=xn[:, i, 0:D], in0=x[:, i, 0:D], scalar=rstd[:, k, i:i + 1],
                                                      in1=rows[:, 7, :], op0=ALU.mult, op1=ALU.mult)
                    last.then_inc(m_xn, 1)
                    for i in range(NT):
                        dve.wait_ge(m_logit, i + 1)
                        V.tensor_reduce(nmax[:, 0, i:i + 1], bank[i], AX.X, ALU.max, negate=True).then_inc(m_red, 1)
                    for j in range(NT):
                        dve.wait_ge(m_logit, NT + j + 1)
                        V.tensor_reduce(nmax[:, 1, j:j + 1], p_m[:, j % 2, :], AX.X, ALU.max, negate=True).then_inc(m_red, 1)
                    dve.wait_ge(m_red, 2 * NT)
                    link(V.tensor_scalar(nm_full[:, :, :], nmax[:, :, :], 1.0 / MSCALE, None, ALU.mult))
                    link(V.tensor_copy(nm_parts[:, :, :, 0], nm_full[:, :, :]))
                    V.tensor_tensor(nm_parts[:, :, :, 1], nm_full[:, :, :], nm_parts[:, :, :, 0], ALU.subtract)\
                        .then_inc(m_red, 1)
                    dve.wait_ge(m_slot, 1)
                    s4 = p_m[:, :, 0:2 * (D + 1)].rearrange("p a (b d) -> p a b d", b=2)
                    link(V.reciprocal(rsum[:, 0, :].rearrange("p (a b) -> p a b", a=2), s4[:, :, :, D]))
                    for j in range(NT):
                        last = V.tensor_scalar(slots[:, j, :], s4[:, j // 2, j % 2, 0:D], rsum[:, 0, j:j + 1], None, ALU.mult)
                    last.then_inc(m_slots, 1)
                    dve.wait_ge(m_out, 1)
                    link(V.reciprocal(rsum[:, 1, :].rearrange("p (a b) -> p a b", a=2), s4[:, :, :, D]))
                    for j in range(NT):
                        last = V.scalar_tensor_tensor(out=r[:, j, :], in0=s4[:, j // 2, j % 2, 0:D],
                                                      scalar=rsum[:, 1, j:j + 1], in1=x[:, j, 0:D],
                                                      op0=ALU.mult, op1=ALU.add)
                    link(last)
                    new_x()

                    for i in range(NT):
                        dve.wait_ge(f_k, i + 1)
                        if i >= 2:
                            dve.wait_ge(f_ke, i - 1)
                        V.tensor_tensor(kpre[:, i % 2, :], p_m[:, i % 2, :], bkf[:, :], ALU.add).then_inc(f_kb, 1)
                    dve.wait_ge(f_kx, 1)
                    link(V.tensor_copy(ks[:, :].rearrange("p (a b) -> p a b", a=2), s4[:, :, :, D]))
                    for G in range(NG):
                        V.tensor_scalar(ksc[:, G, :], headmask[:, G, :], ks[:, G:G + 1], None, ALU.mult)
                    V.tensor_copy(kx[:, :, :].rearrange("p (a b) d -> p a b d", a=2), s4[:, :, :, 0:D]).then_inc(f_kxe, 1)
                    dve.wait_ge(f_den, 1)
                    link(V.tensor_scalar(den[:, :], p_o[0:FH, :], 1e-6, None, ALU.add))
                    V.reciprocal(dinv[:, :], den[:, :]).then_inc(f_dene, 1)
                    dve.wait_ge(f_z, 1)
                    for G in range(NG):
                        last = V.scalar_tensor_tensor(out=z[:, G, :], in0=bvp[:, G, :], scalar=ks[:, G:G + 1],
                                                      in1=p_m[:, 0, G * D:(G + 1) * D], op0=ALU.mult, op1=ALU.add)
                    last.then_inc(f_ze, 1)
                    for G in range(NG):
                        dve.wait_ge(f_rep, G + 1)
                        V.tensor_tensor(qn[:, G, :], bank[G], qp[:, G, :], ALU.mult).then_inc(f_qn, 1)
                    add_residual(f_y, 1)
                    new_x()
                    attention(AX1)
                    add_residual(AX1.y_ready, 2)
                    new_x()

                    dve.wait_ge(xt_done, 4)
                    V.tensor_reduce(xsum[:, :], x_T[:, :], AX.X, ALU.add).then_inc(g_sum, 1)
                    dve.wait_ge(g_logit, 1)
                    link(V.scalar_tensor_tensor(out=logit8[0:1, 0:NE], in0=p_o[0:1, 0:NE], scalar=1.0 / S,
                                                in1=gate_b[:, :], op0=ALU.mult, op1=ALU.add))
                    link(V.max(top8[:, :], logit8[:, :]))
                    V.max_index(idx8[:, :], top8[:, :], logit8[:, :])
                    V.tensor_scalar(gdiff[0:1, 0:NE], logit8[0:1, 0:NE], top8[0:1, 0:1], None, ALU.subtract)
                    V.tensor_scalar(gdiff[0:1, 4:6], top8[0:1, 0:2], top8[0:1, 0:1], None, ALU.subtract).then_inc(g_top, 1)
                    dve.wait_ge(g_exp, 1)
                    link(V.reciprocal(gsum[0:1, 1:2], gsum[0:1, 0:1]))
                    V.tensor_scalar(gw1[:, :], gexp[0:1, 4:6], gsum[0:1, 1:2], None, ALU.mult).then_inc(g_w, 1)
                    dve.wait_ge(g_rep, 1)
                    V.tensor_copy(gw[:, :], p_o[:, 8:10]).then_inc(g_out, 1)

                    for s in range(TOPK):
                        dve.wait_ge(e_load[s], 32)
                        V.tensor_scalar(ebq[:, s:s + 1], ew[s][:, EWC:EWC + 1], DH ** -0.5, None, ALU.mult)\
                            .then_inc(e_bias, 1)
                        attention(AE[s])
                        add_residual(AE[s].y_ready, s + 1)
                        link(layernorm(lambda i: norm[:, i, :]))
                        wide = lambda k: er[s][:, k, :].unsqueeze(1).to_broadcast([P, NT, D])
                        link(V.tensor_tensor(norm[:, :, :], norm[:, :, :], wide(2), ALU.mult))
                        V.tensor_tensor(x1[:, :, :], norm[:, :, :], wide(3), ALU.add).then_inc(e_x1, 1)
                        add_residual(e_y2, s + 1)
                        link(layernorm(lambda i: norm[:, i, :]))
                        link(V.tensor_tensor(norm[:, :, :], norm[:, :, :], wide(5), ALU.mult))
                        link(V.tensor_tensor(norm[:, :, :], norm[:, :, :], wide(6), ALU.add))
                        out = acc if s == 0 else r
                        prev = x[:, :, 0:D] if s == 0 else acc[:, :, :]
                        ins = V.scalar_tensor_tensor(out=out[:, :, :], in0=norm[:, :, :], scalar=gw[:, s:s + 1], in1=prev,
                                                     op0=ALU.mult, op1=ALU.add)
                        if s == 0:
                            ins.then_inc(e_done, 1)
                            dve.wait_ge(e_done, 1)
                        else:
                            link(ins)
                    new_x()

            nc.all_engine_barrier()
            nc.gpsimd.sem_clear(range(sems[0].num, sems[-1].num + 1))
            nc.all_engine_barrier()


def constants():
    import numpy as np
    c32 = np.zeros((P, 3 * P + GH + NG * FH), np.float32)
    p = np.arange(P)
    c32[:, 0:P] = np.eye(P)
    c32[:, P:2 * P] = p[:, None] // FF == p[None, :] // FF
    c32[:, 2 * P:3 * P] = p[:, None] <= p[None, :]
    for g in range(GH):
        c32[:, 3 * P + g] = (p % 32) // DH == g
    for G in range(NG):
        for g in range(GH):
            c32[32 * g:32 * g + 32, 3 * P + GH + G * FH + GH * G + g] = 1
    headrep = np.zeros((FH, NG, P), np.float32)
    for h in range(FH):
        headrep[h, h // GH, (h % GH) * FF:(h % GH + 1) * FF] = 1
    sel = np.zeros((2, P, 2, NG, ST), np.float16)
    for G in range(NG):
        for part in range(3):
            for c in range(32):
                sel[0, 32 * G + c, int(part == 1), G, 32 * part + c] = 1
                sel[1, 32 * G + c, int(part == 2), G, 32 * part + c] = 1
    c16 = np.concatenate([np.eye(P), BIG * np.eye(P), sel[0].reshape(P, -1), sel[1].reshape(P, -1)], 1).astype(np.float16)
    krow = np.zeros((2, GH, NG, GH), np.float16)
    for g in range(GH):
        krow[:, g, :, g] = MSCALE
    krow = krow.reshape(2 * GH, NG, GH, 1)
    return {
        "c32": c32, "c16": c16, "headrep": headrep,
        "krows": np.ascontiguousarray(np.broadcast_to(krow, (2 * GH, NG, GH, S))),
        "krows_x": np.ascontiguousarray(np.broadcast_to(krow, (2 * GH, NG, GH, SKP))),
        "scale_rows": np.full((2, P), MSCALE, np.float16),
        "bigrow": np.full((1, S), BIG, np.float16),
    }


def layout(i):
    import numpy as np
    i = {k: np.asarray(a) for k, a in i.items()}
    cut = lambda w: w.reshape(-1, P, w.shape[1]).transpose(1, 0, 2)
    per_head = lambda w: w.reshape(FH, FD, D).transpose(1, 0, 2)
    qkv = i["L0_attn_qkv_w"].T
    kv, bkv = i["L0_xattn_Wkv"], i["L0_xattn_bkv"]
    mats = [qkv[:, 0:D], qkv[:, D:2 * D], qkv[:, 2 * D:], i["L0_attn_out_w"].T, i["L0_xattn_Wq"], kv[:, 0:D], kv[:, D:],
            i["L0_xattn_Wout"], i["L1_xattn_Wq"].T, i["L1_xattn_Wk"].T, i["L1_xattn_Wv"].T, i["L1_xattn_Wo"].T]
    qb = i["L0_attn_qkv_b"]
    ew = np.concatenate([
        i["L1_ffn_in_proj_w"].transpose(0, 2, 1), i["L1_ffn_out_proj_w"].transpose(0, 2, 1),
        i["L1_ffn_lin1_w"].transpose(0, 2, 1),
        i["L1_ffn_lin2_w"].transpose(0, 2, 1).reshape(NE, HID // P, P, D).transpose(0, 2, 1, 3).reshape(NE, P, HID),
        i["L1_ffn_in_proj_b"][:, 0:2 * D].reshape(NE, 2, D).transpose(0, 2, 1),
        i["L1_ffn_lin1_b"].reshape(NE, HID // P, P).transpose(0, 2, 1)], 2)
    er = np.stack([i["L1_ffn_in_proj_b"][:, 2 * D:], i["L1_ffn_out_proj_b"], i["L1_ffn_ln1_w"], i["L1_ffn_ln1_b"],
                   i["L1_ffn_lin2_b"], i["L1_ffn_ln2_w"], i["L1_ffn_ln2_b"]], 1)
    return {
        "x": i["x"], "x_T": i["x"].transpose(0, 2, 1), "ctx_T": i["ctx_1024"].transpose(0, 2, 1),
        "mask_k": i["mask_Bx1xS2_if1"],
        "mask_q": i["mask_1x1xSxS2_ik0"].reshape(NT, P, SK).transpose(1, 0, 2),
        "w_a": np.stack(mats, 1),
        "cols": np.stack([qb[0:D], qb[D:2 * D], i["L0_xattn_bq"], bkv[0:D], i["L1_xattn_bq"], i["L1_xattn_bk"]], 1),
        "rows": np.stack([qb[2 * D:], i["L0_attn_out_b"], bkv[D:], i["L0_xattn_bout"], i["L1_xattn_bv"],
                          i["L1_xattn_bo"], i["L1_attn_bproj"], i["L0_ffn_gamma_x"], i["L0_ffn_gamma_slot"]], 0),
        "w1": i["L0_ffn_w1"], "w2": cut(i["L0_ffn_w2"]), "slots": cut(i["L0_ffn_slot_embeds"].reshape(NSLOT, D)),
        "wq_t": per_head(i["L1_attn_Wq"].T), "wk_t": per_head(i["L1_attn_Wk"].T), "wv_t": per_head(i["L1_attn_Wv"].T),
        "wp": per_head(i["L1_attn_Wproj"]), "feat": np.stack([i["L1_attn_wq_feat"], i["L1_attn_wk_feat"]], 1),
        "fbias": np.stack([i[f"L1_attn_b{n}"].reshape(FH, FD).T for n in "qkv"], 1),
        "gate_w": i["L1_ffn_gate_w"].T, "gate_b": i["L1_ffn_gate_b"].reshape(1, NE), "ew": ew, "er": er,
    }


def kernel(**inputs):
    import numpy as _np
    import concourse.bacc as _bacc
    from concourse import mybir as _mybir
    from concourse.bass_utils import run_bass_kernel_spmd as _run

    nc = _bacc.Bacc("TRN2", target_bir_lowering=False, num_devices=1)
    arrays, aps = {}, {}
    for name, a in {**layout(inputs), **constants()}.items():
        arrays[f"in_{name}"] = _np.ascontiguousarray(a)
        aps[name] = nc.dram_tensor(f"in_{name}", a.shape, _mybir.dt.from_np(a.dtype), kind="ExternalInput").ap()
    aps["out"] = nc.dram_tensor("out_0", (B, S, D), _mybir.dt.float32, kind="ExternalOutput").ap()
    build(nc, aps)
    r = _run(nc, [arrays], core_ids=[0])
    return r.results[0]["out_0"]
```

```python
from contextlib import ExitStack

import concourse.bass as bass
from concourse import mybir

F32 = mybir.dt.float32
F16 = mybir.dt.float16
I32 = mybir.dt.int32
U32 = mybir.dt.uint32
ALU = mybir.AluOpType
ACT = mybir.ActivationFunctionType
AX = mybir.AxisListType

B, S, D = 4, 512, 128
H, DH = 16, 8
NG, GH = 4, 4
P = 128
NT = S // P
SK = 154
SKP = P + 32
ST = 3 * GH * DH
MR = ST + 2 * GH
MK = MR + 1
MSCALE = 256.0
MCAP = 1.6e7
BIG = 60000.0
FH = 16
FD, FF = 64, 32
HID = 512
NSLOT = 512
NE, TOPK = 4, 2
EIN = 3 * D + 2
EO, E1, E2, EB = EIN, EIN + D, EIN + D + HID, EIN + D + 2 * HID
EWN = EB + HID // P
LN_EPS = 1e-5


TURNS = ("heads lin", "x 1", "heads cross 0", "xn", "slots", "x 3", "kx", "x 4", "heads cross 1", "x 5", "heads expert 0",
         "x1 0", "heads expert 1", "x1 1")


def turn_no(name):
    return TURNS.index(name) + 1


def ring_of(kind):
    if kind in ("causal", "self"):
        ring = ["max"] + list(range(2 * GH)) + ["out"] + list(range(2 * GH, NT * GH))
    else:
        ring = ["max", 0, 1, 2, 3, "out", GH, None]
    return [None if w == "max" and kind == "causal" else w for w in ring]


class Attention:

    def __init__(self, name, kind, before, nk, wq, wk, wv, wo, bq, bk, bv, scale):
        self.name, self.kind, self.nk, self.before = name, kind, nk, before
        self.self_keys = kind in ("causal", "self")
        self.has_max = kind != "causal"
        self.expert = None
        self.units = NT if self.self_keys else 2
        self.tiles = NT * GH if self.self_keys else GH + 1
        self.msteps = (NT * GH if self.self_keys else 2 * NT) if self.has_max else 0
        self.ring = ring_of(kind)
        self.wq, self.wk, self.wv, self.wo = wq, wk, wv, wo
        self.bq, self.bk, self.bv, self.scale = bq, bk, bv, scale
        m = NG if self.has_max else 0
        self.counts = {"projected": 3, "biased": 2, "split": 2, "selected": 2 * NG, "stacked": 2 * NG, "v_ready": 1,
                       "k_ready": 1, "y_ready": 1, "scored": NG * self.tiles, "weighted": NG * self.tiles,
                       "pv_done": NG * self.units, "o_out": NG, "o_turned": NG, "normed": NG,
                       "max_scored": NG * self.msteps, "reduced": NG * self.msteps, "m_parts": m, "m_turned": m,
                       "m_rows": m, "diagonal": 0 if self.has_max else NG * self.tiles}

    def past(self, what):
        return sum(a.counts[what] for a in self.before)

    def rows(self, with_max):
        if self.kind == "cross_key":
            return MK
        return MR if self.has_max and with_max else ST

    def bank_before(self, G, p):
        q = G * len(self.ring) + p - 2
        while q >= 0:
            Gq, w = q // len(self.ring), self.ring[q % len(self.ring)]
            if w == "max":
                return "m_rows", Gq + 1
            if w == "out" and Gq:
                return "normed", Gq
            if w is not None and w != "out":
                return "weighted", Gq * self.tiles + w + 1
            q -= 2
        return None


def both(first, second):
    for _ in first:
        next(second)
    for _ in second:
        raise AssertionError("the streams differ")


class Stream:

    def __init__(self, n, sb, psum, sem):
        name = lambda what: f"{what}_{n}"
        self.x = sb(name("x"), [P, NT, D + 1])
        self.x_T = sb(name("x_T"), [P, S])
        self.xb = sb(name("xb"), [P, NT, D])
        self.r = sb(name("r"), [P, NT, D])
        self.stats = sb(name("stats"), [P, NT, 6])
        self.mv = sb(name("mv"), [P, NT, 2])
        self.var = sb(name("var"), [P, 11, NT])
        self.rstd = sb(name("rstd"), [P, 11, NT])
        self.c_T = sb(name("c_T"), [P, SKP + 96])
        self.mask_k = sb(name("mask_k"), [1, SKP], I32)
        self.bias_k = sb(name("bias_k"), [1, SKP], F16)
        self.k_st = sb(name("k_st"), [P, NG, GH, S], F16)
        self.q_st = sb(name("q_st"), [P, NG, S], F16)
        self.v = sb(name("v"), [P, NT, H * (DH + 1) + 32 - DH - 1])
        self.pt = sb(name("pt"), [P, 2, GH, S])
        self.o_sb = sb(name("o_sb"), [P, 2, S])
        self.hid = sb(name("hid"), [P, NT, S])
        self.neg_max = sb(name("neg_max"), [P, NG, NT, GH])
        self.m_full = sb(name("m_full"), [P, NT, GH])
        self.m_parts = sb(name("m_parts"), [P, NT, 2, GH], F16)
        self.rden = sb(name("rden"), [P, NT, GH])
        self.heads_1 = sb(name("heads"), [P, NT, D + 1])
        self.heads = self.heads_1[:, :, 0:D]
        self.heads_T = sb(name("heads_T"), [P, S])
        self.xn = sb(name("xn"), [P, NT, D + 1])
        self.xn_T = sb(name("xn_T"), [P, S])
        self.nmax = sb(name("nmax"), [P, 2, NT])
        self.nm_full = sb(name("nm_full"), [P, 2, NT])
        self.nm_parts = sb(name("nm_parts"), [P, 2, NT, 2], F16)
        self.rsum = sb(name("rsum"), [P, 2, NT])
        self.ks = sb(name("ks"), [P, NG])
        self.ksc = sb(name("ksc"), [P, NG, FH])
        self.ew = sb(name("ew"), [P, EWN])
        self.er = sb(name("er"), [P, 7, D])
        self.ebq = sb(name("ebq"), [P, TOPK])
        self.xsum = sb(name("xsum"), [P, 1])
        self.logit8 = sb(name("logit8"), [1, 8])
        self.top8 = sb(name("top8"), [1, 8])
        self.idx8 = sb(name("idx8"), [1, 8], U32)
        self.gdiff = sb(name("gdiff"), [1, 8])
        self.gexp = sb(name("gexp"), [1, 8])
        self.gsum = sb(name("gsum"), [1, 2])
        self.gw1 = sb(name("gw1"), [1, 2])
        self.gw = sb(name("gw"), [P, 2])

        self.q_full, self.k_full = self.hid[:, 0, :], self.hid[:, 1, :]
        self.q_hi, self.q_lo = [self.hid[:, 2, :].bitcast(F16)[:, i * S:(i + 1) * S] for i in range(2)]
        self.k_hi, self.k_lo = [self.hid[:, 3, :].bitcast(F16)[:, i * S:(i + 1) * S] for i in range(2)]
        self.kp = self.hid
        self.k_dense = self.pt[:, 1, 0:2, :].rearrange("p a b -> p (a b)").bitcast(F16)\
            .rearrange("p (g k) -> p g k", g=NG)
        self.disp, self.comb = self.pt[:, 0, :, :], self.pt[:, 1, :, :]
        self.qp, self.qn = self.disp, self.comb
        self.kpre = self.o_sb
        self.den, self.dinv = self.o_sb[0:FH, 0, :], self.o_sb[0:FH, 1, :]
        self.slots, self.slots_T = self.heads, self.heads_T
        self.kx, self.kx_T = self.heads, self.heads_T
        self.proc, self.z, self.x1 = self.heads_1, self.heads, self.heads
        self.nm_row = self.hid[0:2, 0, :].bitcast(F16).rearrange("p (w s) -> p w s", w=2)
        self.x1_T = self.heads_T
        self.norm = self.xn[:, :, 0:D]
        self.acc = self.xn_T[:, :].rearrange("p (t d) -> p t d", t=NT)

        self.p = psum(name("psum"), [P, 4, S])
        self.bank = [self.p[:, k, :] for k in range(4)]
        self.bank16 = [self.p[:, k, :].bitcast(F16) for k in range(4)]
        self.y = self.p[:, 3, :].rearrange("p (t d) -> p t d", t=NT)
        self.four = self.p[:, 0:2, 0:2 * (D + 1)].rearrange("p a (b d) -> p a b d", b=2)

        sig = lambda what: sem(name(what))
        self.x_loaded, self.ctx_loaded, self.stored = sig("x_loaded"), sig("ctx_loaded"), sig("stored")
        self.mask_loaded, self.bias_ready, self.bias_placed = sig("mask_loaded"), sig("bias_ready"), sig("bias_placed")
        self.x_done, self.xb_done = sig("x_done"), sig("xb_done")
        self.var_ready, self.rstd_ready = sig("var_ready"), sig("rstd_ready")
        self.turned, self.turned_out = sig("turned"), sig("turned_out")
        self.projected, self.biased, self.split = sig("projected"), sig("biased"), sig("split")
        self.selected, self.stacked = sig("selected"), sig("stacked")
        self.v_ready, self.k_ready, self.y_ready = sig("v_ready"), sig("k_ready"), sig("y_ready")
        self.scored, self.weighted, self.diagonal = sig("scored"), sig("weighted"), sig("diagonal")
        self.pv_done, self.o_out, self.o_turned = sig("pv_done"), sig("o_out"), sig("o_turned")
        self.normed = sig("normed")
        self.max_scored, self.reduced, self.m_parts_ready = sig("max_scored"), sig("reduced"), sig("m_parts_ready")
        self.m_turned, self.m_rows = sig("m_turned"), sig("m_rows")
        self.mix_normed, self.logits, self.logits_max = sig("mix_normed"), sig("logits"), sig("logits_max")
        self.rows_turned, self.rows_out = sig("rows_turned"), sig("rows_out")
        self.rescored, self.mix_weights = sig("rescored"), sig("mix_weights")
        self.slots_summed, self.slots_out = sig("slots_summed"), sig("slots_out")
        self.hidden, self.hidden_out = sig("hidden"), sig("hidden_out")
        self.processed, self.processed_out, self.combined = sig("processed"), sig("processed_out"), sig("combined")
        self.f_q, self.f_q_exp, self.f_k = sig("f_q"), sig("f_q_exp"), sig("f_k")
        self.f_k_biased, self.f_k_exp = sig("f_k_biased"), sig("f_k_exp")
        self.f_kx, self.f_kx_out = sig("f_kx"), sig("f_kx_out")
        self.f_den, self.f_den_inv, self.f_spread = sig("f_den"), sig("f_den_inv"), sig("f_spread")
        self.f_scaled, self.f_z, self.f_z_out, self.f_y = sig("f_scaled"), sig("f_z"), sig("f_z_out"), sig("f_y")
        self.g_sum, self.g_logit, self.g_top, self.g_exp = sig("g_sum"), sig("g_logit"), sig("g_top"), sig("g_exp")
        self.g_weights, self.g_spread, self.g_ready = sig("g_weights"), sig("g_spread"), sig("g_ready")
        self.e_in, self.e_rest = sig("e_in"), sig("e_rest")
        self.e_bias, self.e_x1, self.e_y2, self.e_done = sig("e_bias"), sig("e_x1"), sig("e_y2"), sig("e_done")


def build(nc, t):
    with ExitStack() as ctx:
        def sb(name, shape, dt=F32):
            return ctx.enter_context(nc.sbuf_tensor(name, shape, dt))

        def psum(name, shape):
            return ctx.enter_context(nc.psum_tensor(name, shape, F32))

        sems = []

        def sem(name):
            sems.append(ctx.enter_context(nc.semaphore(name)))
            return sems[-1]

        eye = sb("eye", [P, P])
        causal = sb("causal", [P, P])
        colmask = sb("colmask", [P, GH])
        headmask = sb("headmask", [P, NG, FH])
        eye16 = sb("eye16", [P, P], F16)
        bigeye = sb("bigeye", [P, P], F16)
        select = sb("select", [P, 2, NG, ST], F16)
        select_q = sb("select_q", [P, 2, NG, ST], F16)
        scale_rows = sb("scale_rows", [2, P], F16)
        headrep = sb("headrep", [FH, NG, P])
        ones = sb("ones", [1, P])
        half = sb("half", [P, NT])
        cols = sb("cols", [P, 6])
        cols_s = sb("cols_s", [P, 6])
        rows = sb("rows", [P, 9, D])
        w_a = sb("w_a", [P, 12, D])
        w1 = sb("w1", [P, HID])
        w2 = sb("w2", [P, NT, D])
        slot_T = sb("slot_T", [P, NSLOT])
        feat = sb("feat", [FD, 2, FF])
        fbias = sb("fbias", [FD, 3, FH])
        wqf = sb("wqf", [P, FH * FF])
        wkf = sb("wkf", [P, FH * FF])
        bqf = sb("bqf", [P, NG])
        bkf = sb("bkf", [P, FH * FF])
        wvp = sb("wvp", [P, FH, D])
        bvp = sb("bvp", [P, NG, D])
        gate_w = sb("gate_w", [P, NE])
        gate_b = sb("gate_b", [1, NE])
        bias_q = sb("bias_q", [P, NT, SKP], F16)
        bias_kq = sb("bias_kq", [P, 2, S], F16)
        squares = sb("squares", [P, D])

        load_w, load_c, setup = sem("load_w"), sem("load_c"), sem("setup")
        composed, composed_out = sem("composed"), sem("composed_out")
        dve_step = sem("dve_step")
        streams = [Stream(n, sb, psum, sem) for n in range(2)]
        s0, s1 = streams

        wq_t, wk_t, wv_t = [a[0:FD].rearrange("p t (a d) -> p (t a) d", d=D)
                            for a in (s0.pt[:, 0, :, :], s0.pt[:, 1, :, :], s0.hid[:, :, :])]
        wp, bias_rep = [s0.k_st[0:FD, i:i + 2, :, :].rearrange("p a b k -> p (a b k)").bitcast(F32)
                        .rearrange("p (h d) -> p h d", h=FH) for i in (0, 2)]
        bias_rep_v = s1.hid[0:FD, 0, :].rearrange("p (h f) -> p h f", h=FH)
        slot_raw = s1.pt[:, 0, 0, :].rearrange("p (t d) -> p t d", t=NT)
        mask_q = s1.pt[:, 1, 0:2, :].rearrange("p a b -> p (a b)").bitcast(I32)[:, 0:NT * SKP]\
            .rearrange("p (t k) -> p t k", t=NT)
        mask_kq = s1.pt[:, 1, 2:4, :].bitcast(I32)

        def attentions(w):
            out = []
            head_scale = DH ** -0.5
            out.append(Attention("lin", "causal", [], S, w_a[:, 0, :], w_a[:, 1, :], w_a[:, 2, :], w_a[:, 3, :],
                                 cols[:, 0:1], cols[:, 1:2], rows[:, 0, :], 1.0))
            out.append(Attention("cross 0", "cross_key", out[:], SKP, w_a[:, 4, :], w_a[:, 5, :], w_a[:, 6, :], w_a[:, 7, :],
                                 cols_s[:, 2:3], cols[:, 3:4], rows[:, 2, :], head_scale))
            out.append(Attention("cross 1", "cross_full", out[:], SKP, w_a[:, 8, :], w_a[:, 9, :], w_a[:, 10, :],
                                 w_a[:, 11, :], cols_s[:, 4:5], cols[:, 5:6], rows[:, 4, :], head_scale))
            for s in range(TOPK):
                out.append(Attention(f"expert {s}", "self", out[:], S, w.ew[:, 0:D], w.ew[:, D:2 * D],
                                     w.ew[:, 2 * D:3 * D], w.ew[:, EO:EO + D], w.ebq[:, s:s + 1],
                                     w.ew[:, EIN - 1:EIN], w.er[:, 0, :], head_scale))
                out[-1].expert = s
            return out

        with nc.Block() as block:
            @block.sync
            def _(sp):
                for dst, src in ((eye[:, :], t["c32"][:, 0:P]),
                                 (causal[:, :], t["c32"][:, P:2 * P]), (colmask[:, :], t["c32"][:, 2 * P:2 * P + GH]),
                                 (headmask[:, :, :], t["c32"][:, 2 * P + GH:2 * P + GH + NG * FH]),
                                 (headrep[:, :, :], t["headrep"]),
                                 (eye16[:, :], t["c16"][:, 0:P]), (bigeye[:, :], t["c16"][:, P:2 * P]),
                                 (select[:, :, :, :], t["c16"][:, 2 * P:2 * P + 2 * NG * ST]),
                                 (select_q[:, :, :, :], t["c16"][:, 2 * P + 2 * NG * ST:]),
                                 (s0.k_st[ST:MR, :, :, :], t["krows"]), (s1.k_st[ST:MR, :, :, :], t["krows"]),
                                 (s0.q_st[MR:MK, :, :], t["bigrow"]), (s1.q_st[MR:MK, :, :], t["bigrow"]),
                                 (scale_rows[:, :], t["scale_rows"])):
                    sp.dma_start(dst, src).then_inc(load_c, 16)
                for dst, src in ((cols[:, :], t["cols"]), (rows[:, :, :], t["rows"].partition_broadcast(P)),
                                 (w_a[:, :, :], t["w_a"]), (w1[:, :], t["w1"]), (w2[:, :, :], t["w2"]),
                                 (slot_raw[:, :, :], t["slots"]), (wq_t[:, :, :], t["wq_t"]),
                                 (wk_t[:, :, :], t["wk_t"]), (wv_t[:, :, :], t["wv_t"]), (wp[:, :, :], t["wp"]),
                                 (feat[:, :, :], t["feat"]), (fbias[:, :, :], t["fbias"]),
                                 (gate_w[:, :], t["gate_w"]), (gate_b[:, :], t["gate_b"])):
                    sp.dma_start(dst, src).then_inc(load_w, 16)
                sp.wait_ge(setup, 1)
                sp.dma_start(mask_q[:, :, 0:SK], t["mask_q"]).then_inc(load_w, 16)
                sp.dma_start(mask_kq[:, 0, :], t["mask_kq"][0:P]).then_inc(load_w, 16)
                sp.dma_start(mask_kq[0:SK - P, 1, :], t["mask_kq"][P:SK]).then_inc(load_w, 16)

            @block.vector
            def _(dve):
                step = [0]

                def link(ins):
                    step[0] += 1
                    ins.then_inc(dve_step, 1)
                    dve.wait_ge(dve_step, step[0])

                nc.vector.memset(mask_kq[:, 1, :], 0)
                nc.vector.memset(mask_q[:, :, :], 0).then_inc(setup, 1)
                nc.vector.memset(ones[:, :], 1.0)
                nc.vector.memset(half[:, :], -0.5)
                for w in streams:
                    nc.vector.memset(w.c_T[:, :], 0.0)
                    nc.vector.memset(w.mask_k[:, :], 0)
                    nc.vector.memset(w.x[:, :, D:D + 1], 1.0)
                    nc.vector.memset(w.xn[:, :, D:D + 1], 1.0)
                    nc.vector.memset(w.proc[:, :, D:D + 1], 1.0)
                    nc.vector.memset(w.logit8[:, :], -3.0e38)
                    nc.vector.memset(w.v[:, :, :], 1.0)
                dve.wait_ge(load_w, 16 * 17)
                nc.vector.tensor_scalar(cols_s[:, :], cols[:, :], DH ** -0.5, None, ALU.mult)
                nc.vector.tensor_scalar(rows[:, 7:9, :], rows[:, 7:9, :], float(D) ** 0.5, None, ALU.mult)
                nc.vector.tensor_scalar(bias_q[:, :, :], mask_q[:, :, :], 0, -BIG, ALU.is_equal, ALU.mult)
                nc.vector.tensor_scalar(bias_kq[:, :, :], mask_kq, 0, -BIG, ALU.is_equal, ALU.mult)
                nc.vector.tensor_copy(bias_rep[:, :, :], fbias[:, 1, :].unsqueeze(2).to_broadcast([FD, FH, P]))
                link(nc.vector.tensor_copy(bias_rep_v[:, :, :], fbias[:, 2, :].unsqueeze(2).to_broadcast([FD, FH, FF])))
                for j in range(NT):
                    link(nc.vector.tensor_tensor(squares[:, :], slot_raw[:, j, :], slot_raw[:, j, :], ALU.mult))
                    link(nc.vector.tensor_reduce(s0.var[:, 0, j:j + 1], squares[:, :], AX.X, ALU.add))
                nc.vector.tensor_scalar(s0.var[:, 0, :], s0.var[:, 0, :], 1e-24, None, ALU.max).then_inc(s0.var_ready, 1)
                dve.wait_ge(s0.rstd_ready, 1)
                for j in range(NT):
                    last = nc.vector.scalar_tensor_tensor(out=s0.slots[:, j, :], in0=slot_raw[:, j, :],
                                                          scalar=s0.rstd[:, 0, j:j + 1], in1=rows[:, 8, :],
                                                          op0=ALU.mult, op1=ALU.mult)
                last.then_inc(setup, 1)
                dve.wait_ge(composed, 1)
                nc.vector.tensor_copy(wqf[:, :], s0.bank[0])
                nc.vector.tensor_copy(wkf[:, :], s0.bank[1])
                nc.vector.tensor_copy(bqf[:, :], s1.bank[0][:, 0:NG])
                nc.vector.tensor_copy(bkf[:, :], s0.bank[2])
                nc.vector.tensor_copy(bvp[:, :, :], s0.bank[3].rearrange("p (g d) -> p g d", g=NG))
                nc.vector.tensor_copy(slot_T[:, :], s1.bank[1]).then_inc(composed_out, 1)
                dve.wait_ge(composed, 2)
                for q in range(4):
                    last = nc.vector.tensor_copy(wvp[:, 4 * q:4 * q + 4, :],
                                                 s0.bank[q].rearrange("p (g d) -> p g d", g=4))
                last.then_inc(composed_out, 1)

            @block.gpsimd
            def _(pool):
                pool.wait_ge(s0.var_ready, 1)
                nc.gpsimd.tensor_tensor(s0.rstd[:, 0, :], s0.var[:, 0, :], half[:, :], ALU.pow).then_inc(s0.rstd_ready, 1)

            @block.tensor
            def _(pe):
                mm = nc.tensor.matmul
                pe.wait_ge(load_w, 16 * 17)
                pe.wait_ge(load_c, 16 * 14)
                pe.wait_ge(setup, 2)
                for h in range(FH):
                    G, g = divmod(h, GH)
                    out = slice(h * FF, (h + 1) * FF)
                    mm(s0.bank[0][:, out], wq_t[:, h, :], feat[:, 0, :], start=True, stop=True)
                    mm(s0.bank[1][:, out], wk_t[:, h, :], feat[:, 1, :], start=True, stop=True)
                    mm(s0.bank[2][:, out], bias_rep[:, h, :], feat[:, 1, :], start=True, stop=True)
                    mm(s1.bank[0][FF * g:FF * (g + 1), G:G + 1], feat[:, 0, :], fbias[:, 0, h:h + 1], start=True, stop=True)
                    mm(s0.bank[3][FF * g:FF * (g + 1), G * D:(G + 1) * D], bias_rep_v[:, h, :], wp[:, h, :],
                       start=True, stop=True)
                for j in range(NT):
                    last = nc.tensor.transpose(s1.bank[1][:, j * P:(j + 1) * P], s0.slots[:, j, :], eye[:, :])
                last.then_inc(composed, 1)
                pe.wait_ge(composed_out, 1)
                for h in range(FH):
                    last = mm(s0.bank[h // 4][:, (h % 4) * D:(h % 4 + 1) * D], wv_t[:, h, :], wp[:, h, :],
                              start=True, stop=True)
                last.then_inc(composed, 1)

        nc.all_engine_barrier()
        nc.gpsimd.sem_clear(range(sems[0].num, sems[-1].num + 1))
        nc.all_engine_barrier()

        with nc.Fori(0, B // 2) as b:
            with nc.Block() as block:

                def of_batch(a, n):
                    return a.rearrange("(b n) r c -> n b r c", n=2)[n][bass.ds(b, 1)].squeeze(0)

                @block.sync
                def _(sp):
                    for n, w in enumerate(streams):
                        one = lambda a: of_batch(a, n)
                        sp.dma_start(w.x_T[:, :], one(t["x_T"])).then_inc(w.x_loaded, 16)
                        sp.dma_start(w.x[:, :, 0:D], one(t["x"]).rearrange("(t p) d -> p t d", p=P)).then_inc(w.x_loaded, 16)
                        sp.dma_start(w.mask_k[:, 0:SK], one(t["mask_k"])).then_inc(w.mask_loaded, 16)
                    for n, w in enumerate(streams):
                        one = lambda a: of_batch(a, n)
                        sp.dma_start(w.c_T[:, 0:SK], one(t["ctx_T"])).then_inc(w.ctx_loaded, 16)
                        for i in range(1, 4):
                            sp.dma_start(w.c_T[:, P + 32 * i:P + 32 * i + SK - P], one(t["ctx_T"])[:, P:SK])\
                                .then_inc(w.ctx_loaded, 16)
                    for n, w in enumerate(streams):
                        sp.wait_ge(w.bias_ready, 1)
                        sp.dma_start(w.k_st[MR:MK, :, :, 0:SKP].rearrange("p a b k -> p (a b) k"),
                                     w.bias_k[:, :].unsqueeze(1).to_broadcast([1, H, SKP])).then_inc(w.bias_placed, 16)
                    for s in range(TOPK):
                        chosen = []
                        for w in streams:
                            expert = attentions(w)[3]
                            if s == 0:
                                sp.wait_ge(w.g_top, 1)
                            else:
                                sp.wait_ge(w.projected, expert.past("projected") + 3)
                                sp.wait_ge(w.biased, expert.past("biased") + 2)
                            chosen.append(sp.value_load(w.idx8[0:1, s:s + 1], min_val=0, max_val=NE - 1))
                            sp.dma_start(w.ew[:, 0:EIN], t["ew"][bass.ds(chosen[-1], 1)].squeeze(0)[:, 0:EIN])\
                                .then_inc(w.e_in, 16)
                        for w, e in zip(streams, chosen):
                            if s:
                                sp.wait_ge(w.e_y2, s)
                            sp.dma_start(w.ew[:, EIN:EWN], t["ew"][bass.ds(e, 1)].squeeze(0)[:, EIN:EWN])\
                                .then_inc(w.e_rest, 16)
                        for w, e in zip(streams, chosen):
                            if s:
                                sp.wait_ge(w.e_done, s)
                            sp.dma_start(w.er[:, :, :], t["er"][bass.ds(e, 1)].squeeze(0).partition_broadcast(P))\
                                .then_inc(w.e_rest, 16)
                    for n, w in enumerate(streams):
                        sp.wait_ge(w.x_done, 6)
                        sp.dma_start(of_batch(t["out"], n).rearrange("(t p) d -> p t d", p=P),
                                     w.x[:, :, 0:D]).then_inc(w.stored, 16)
                    for w in streams:
                        sp.wait_ge(w.stored, 16)

                @block.gpsimd
                def _(pool):
                    def stream(w):
                        npow = [0]

                        def residual(bias, ready, count, src):
                            pool.wait_ge(ready, count)
                            nc.gpsimd.tensor_tensor(w.xb[:, :, :], src, bias.unsqueeze(1).to_broadcast([P, NT, D]),
                                                    ALU.add).then_inc(w.xb_done, 1)

                        def rsqrt():
                            k = npow[0]
                            pool.wait_ge(w.var_ready, k + 1)
                            nc.gpsimd.tensor_tensor(w.rstd[:, k, :], w.var[:, k, :], half[:, :], ALU.pow)\
                                .then_inc(w.rstd_ready, 1)
                            npow[0] += 1

                        x = w.x[:, :, 0:D]
                        residual(rows[:, 1, :], w.x_loaded, 32, x)
                        yield
                        rsqrt()
                        yield
                        residual(rows[:, 3, :], w.x_done, 1, x)
                        yield
                        for _ in range(3):
                            rsqrt()
                            yield
                        residual(rows[:, 6, :], w.x_done, 3, x)
                        yield
                        rsqrt()
                        yield
                        residual(rows[:, 5, :], w.x_done, 4, x)
                        yield
                        rsqrt()
                        yield
                        for s in range(TOPK):
                            pool.wait_ge(w.e_rest, 32 * (s + 1))
                            if s:
                                pool.wait_ge(w.e_done, s)
                            residual(w.er[:, 1, :], w.x_done, 5, x)
                            yield
                            rsqrt()
                            yield
                            residual(w.er[:, 4, :], w.e_x1, s + 1, w.x1)
                            yield
                            rsqrt()
                            yield
                        rsqrt()
                        yield

                    both(stream(s0), stream(s1))

                @block.tensor
                def _(pe):
                    mm, tr = nc.tensor.matmul, nc.tensor.transpose

                    def turn(w, bank, src, name):
                        for i in range(NT):
                            last = tr(bank[:, i * P:(i + 1) * P], src[:, i, 0:D], eye[:, :])
                        last.then_inc(w.turned, 1)

                    def attention(w, a):
                        bank = w.bank
                        src = w.x_T if a.self_keys else w.c_T
                        mm(bank[1][:, 0:a.nk], a.wk, src[:, 0:a.nk], start=True, stop=True).then_inc(w.projected, 1)
                        mm(bank[0], a.wq, w.x_T[:, :], start=True, stop=True).then_inc(w.projected, 1)
                        for kt in range(a.units):
                            last = mm(bank[2][:, kt * D:(kt + 1) * D], src[:, kt * P:(kt + 1) * P], a.wv,
                                      start=True, stop=True)
                        last.then_inc(w.projected, 1)
                        yield
                        for i in range(2 * NG):
                            G, keys = i % NG, i < NG
                            if G == 0:
                                pe.wait_ge(w.split, a.past("split") + (1 if keys else 2))
                            if i >= 2:
                                pe.wait_ge(w.stacked, a.past("stacked") + i - 1)
                            n, hi, lo, sel = (a.nk, w.k_hi, w.k_lo, select) if keys else (S, w.q_hi, w.q_lo, select_q)
                            out = bank[(3, 1)[i % 2]][0:ST, 0:n]
                            mm(out, sel[:, 0, G, :], hi[:, 0:n], start=True, stop=False)
                            mm(out, sel[:, 1, G, :], lo[:, 0:n], start=False, stop=True).then_inc(w.selected, 1)
                            if i % 2:
                                yield

                        def max_step(G, i):
                            n = G * a.msteps + i
                            if n == 0:
                                pe.wait_ge(w.v_ready, a.past("v_ready") + 1)
                                pe.wait_ge(w.k_ready, a.past("k_ready") + 1)
                                pe.wait_ge(w.stacked, a.past("stacked") + 2 * NG)
                            else:
                                pe.wait_ge(w.reduced, a.past("reduced") + n)
                            if a.self_keys:
                                qt, g = i // GH, i % GH
                                mm(bank[2][:, 0:a.nk], w.q_st[0:ST, G, qt * P:(qt + 1) * P], w.k_st[0:ST, G, g, 0:a.nk],
                                   start=True, stop=True).then_inc(w.max_scored, 1)
                                return
                            qt, g = i // 2, 2 * (i % 2)
                            out, K = bank[2][:, 0:2 * SKP].rearrange("p (j k) -> p j k", j=2), a.rows(False)
                            last = mm(out, w.q_st[0:K, G, qt * P:(qt + 1) * P], w.k_st[0:K, G, g:g + 2, 0:SKP],
                                      start=True, stop=a.kind == "cross_key")
                            if a.kind == "cross_full":
                                last = mm(out, bigeye[:, :], bias_q[:, qt, :].unsqueeze(1).to_broadcast([P, 2, SKP]),
                                          start=False, stop=True)
                            last.then_inc(w.max_scored, 1)

                        def place(G, what):
                            p = a.ring.index(what)
                            before = a.bank_before(G, p)
                            if before is not None:
                                name, count = before
                                held = {"weighted": w.weighted, "m_rows": w.m_rows, "normed": w.normed}[name]
                                pe.wait_ge(held, a.past(name) + count)
                            return p % 2

                        def turn_max(G):
                            k = place(G, "max")
                            pe.wait_ge(w.m_parts_ready, a.past("m_parts") + G + 1)
                            for qt in range(NT):
                                last = tr(w.bank16[k][ST:MR, qt * P:(qt + 1) * P], w.m_parts[:, qt, :, :], eye16[:, :])
                            last.then_inc(w.m_turned, 1)

                        def score(G, tile):
                            k = place(G, tile)
                            if tile == 0:
                                if a.has_max:
                                    pe.wait_ge(w.m_rows, a.past("m_rows") + G + 1)
                                if G == 0:
                                    pe.wait_ge(w.k_ready, a.past("k_ready") + 1)
                                    pe.wait_ge(w.stacked, a.past("stacked") + 2 * NG)
                            K = a.rows(True)
                            if a.self_keys or tile < GH:
                                kt, g = divmod(tile, GH)
                                lo = kt * P if a.kind == "causal" else 0
                                out = bank[k]
                                last = mm(out[:, lo:S], w.k_st[0:K, G, g, kt * P:(kt + 1) * P], w.q_st[0:K, G, lo:S],
                                          start=True, stop=a.kind != "cross_full")
                                if a.kind == "cross_full":
                                    last = mm(out, bigeye[:, :], bias_kq[:, 0, :], start=False, stop=True)
                            else:
                                for g in range(GH):
                                    out = w.p[32 * g:32 * g + 32, k, :]
                                    last = mm(out, w.k_st[0:K, G, g, P:SKP], w.q_st[0:K, G, :], start=True,
                                              stop=a.kind != "cross_full")
                                    if a.kind == "cross_full":
                                        last = mm(out, bigeye[0:32, 0:32], bias_kq[0:32, 1, :], start=False, stop=True,
                                                  tile_position=(0, 32 * g))
                            last.then_inc(w.scored, 1)

                        def weigh(u):
                            G, kt = divmod(u, a.units)
                            done = G * a.tiles + min(GH * (kt + 1), a.tiles)
                            if a.has_max:
                                pe.wait_ge(w.weighted, a.past("weighted") + done)
                            else:
                                pe.wait_ge(w.diagonal, a.past("diagonal") + done)
                            if kt == 0 and G:
                                pe.wait_ge(w.o_out, a.past("o_out") + G)
                            if u == 0:
                                pe.wait_ge(w.v_ready, a.past("v_ready") + 1)
                            rest = not a.self_keys and kt == 1
                            for g in range(GH):
                                k0, k1 = (32 * g, 32 * g + 32) if rest else (0, P)
                                lo = kt * P if a.kind == "causal" else 0
                                c = (GH * G + g) * (DH + 1)
                                last = mm(w.p[32 * g:32 * g + 32, 3, lo:S], w.v[k0:k1, kt, c:c + 32],
                                          w.pt[k0:k1, u % 2, 0 if rest else g, lo:S], start=kt == 0,
                                          stop=kt == a.units - 1 or a.kind == "causal", skip_group_check=True)
                            last.then_inc(w.pv_done, 1)

                        def turn_outputs(G, k):
                            pe.wait_ge(w.o_out, a.past("o_out") + G + 1)
                            for qt in range(NT):
                                last = tr(bank[k][:, qt * P:(qt + 1) * P], w.o_sb[:, G % 2, qt * P:(qt + 1) * P], eye[:, :])
                            last.then_inc(w.o_turned, 1)

                        for i in range(a.msteps):
                            max_step(0, i)
                            yield
                        out_at = a.ring.index("out") - 1
                        for G in range(NG):
                            ahead = a.msteps // GH // (a.units if a.self_keys else 1) if G < NG - 1 else 0
                            for tile in range(a.tiles):
                                for i in range(ahead if tile < NT * GH and (a.self_keys or tile < GH) else 0):
                                    max_step(G + 1, tile * ahead + i)
                                    if i:
                                        yield
                                if tile == 0 and a.has_max:
                                    turn_max(G)
                                score(G, tile)
                                if tile % GH == GH - 1 or tile == a.tiles - 1:
                                    u = G * a.units + tile // GH
                                    if u:
                                        weigh(u - 1)
                                if a.ring[out_at] == tile and G:
                                    turn_outputs(G - 1, place(G, "out"))
                                yield
                        weigh(NG * a.units - 1)
                        yield
                        pe.wait_ge(w.weighted, a.past("weighted") + NG * a.tiles)
                        turn_outputs(NG - 1, 0)
                        yield
                        pe.wait_ge(w.normed, a.past("normed") + NG)
                        turn(w, bank[1], w.heads, f"heads {a.name}")
                        yield
                        pe.wait_ge(w.turned_out, turn_no(f"heads {a.name}"))
                        if a.expert is not None:
                            pe.wait_ge(w.e_rest, 32 * (a.expert + 1))
                        for qt in range(NT):
                            last = mm(w.y[:, qt, :], w.heads_T[:, qt * P:(qt + 1) * P], a.wo, start=True, stop=True)
                        last.then_inc(w.y_ready, 1)
                        yield

                    def turn_x(w, n):
                        pe.wait_ge(w.x_done, n)
                        turn(w, w.bank[0], w.x, f"x {n}")
                        yield

                    def stream(w):
                        lin, cross0, cross1, *experts = attentions(w)
                        bank = w.bank
                        pe.wait_ge(w.x_loaded, 32)
                        yield from attention(w, lin)
                        yield from turn_x(w, 1)
                        pe.wait_ge(w.ctx_loaded, 16 * 4)
                        pe.wait_ge(w.bias_placed, 16)
                        pe.wait_ge(w.turned_out, turn_no("x 1"))
                        yield from attention(w, cross0)

                        yield
                        pe.wait_ge(w.mix_normed, 1)
                        turn(w, bank[0], w.xn, "xn")
                        yield
                        pe.wait_ge(w.turned_out, turn_no("xn"))
                        for i in range(2 * NT):
                            if i >= NT:
                                pe.wait_ge(w.logits_max, i - NT + 1)
                            j = i % NT
                            st, mov = (w.xn_T[:, j * P:(j + 1) * P], slot_T) if i < NT else \
                                (slot_T[:, j * P:(j + 1) * P], w.xn_T)
                            mm(bank[j], st, mov[:, :], start=True, stop=True).then_inc(w.logits, 1)
                            yield
                        pe.wait_ge(w.logits_max, 2 * NT + 1)
                        for which in range(2):
                            for i in range(NT):
                                last = tr(w.bank16[0][0:2, which * S + i * P:which * S + (i + 1) * P],
                                          w.nm_parts[:, which, i, :], eye16[:, :])
                        last.then_inc(w.rows_turned, 1)
                        yield
                        pe.wait_ge(w.rows_out, 1)
                        for k in range(2 * NT):
                            j, which = k % NT, k // NT
                            if k >= NT:
                                pe.wait_ge(w.mix_weights, k - NT + 1)
                            st, mov = (w.xn_T[:, j * P:(j + 1) * P], slot_T) if which == 0 else \
                                (slot_T[:, j * P:(j + 1) * P], w.xn_T)
                            mm(bank[j], st, mov[:, :], start=True, stop=False)
                            mm(bank[j], scale_rows[:, :], w.nm_row[:, 1 - which, :], start=False, stop=True)\
                                .then_inc(w.rescored, 1)
                            yield
                        pe.wait_ge(w.mix_weights, NT + 2)
                        for j in range(NT):
                            for i in range(NT):
                                last = mm(w.four[:, j // 2, j % 2, :], w.disp[:, i, j * P:(j + 1) * P], w.xn[:, i, :],
                                          start=i == 0, stop=i == NT - 1)
                            if j == NT - 1:
                                last.then_inc(w.slots_summed, 1)
                            yield
                        pe.wait_ge(w.slots_out, 1)
                        pe.wait_ge(w.mix_weights, 2 * NT)
                        turn(w, bank[2], w.slots, "slots")
                        yield
                        pe.wait_ge(w.turned_out, turn_no("slots"))
                        for k in range(NT):
                            mm(bank[k], w1[:, k * P:(k + 1) * P], w.slots_T[:, :], start=True, stop=True).then_inc(w.hidden, 1)
                            yield
                        pe.wait_ge(w.hidden_out, NT)
                        for j in range(NT):
                            for k in range(NT):
                                last = mm(w.y[:, j, :], w.hid[:, k, j * P:(j + 1) * P], w2[:, k, :],
                                          start=k == 0, stop=k == NT - 1)
                            if j == NT - 1:
                                last.then_inc(w.processed, 1)
                            yield
                        pe.wait_ge(w.processed_out, 1)
                        for i in range(NT):
                            for j in range(NT):
                                last = mm(w.four[:, i // 2, i % 2, :], w.comb[:, j, i * P:(i + 1) * P], w.proc[:, j, :],
                                          start=j == 0, stop=j == NT - 1)
                            if i == NT - 1:
                                last.then_inc(w.combined, 1)
                            yield
                        yield from turn_x(w, 3)

                        pe.wait_ge(w.turned_out, turn_no("x 3"))
                        for G in range(NG):
                            mm(bank[G], wqf[:, G * P:(G + 1) * P], w.x_T[:, :], start=True, stop=True).then_inc(w.f_q, 1)
                            yield
                        for i in range(NT):
                            pe.wait_ge(w.f_q_exp, i + 1)
                            mm(bank[i], w.x_T[:, i * P:(i + 1) * P], wkf[:, :], start=True, stop=True).then_inc(w.f_k, 1)
                            yield
                        pe.wait_ge(w.f_k_exp, NT)
                        for G in range(NG):
                            for i in range(NT):
                                last = mm(w.four[:, G // 2, G % 2, :], w.kp[:, i, G * P:(G + 1) * P], w.x[:, i, :],
                                          start=i == 0, stop=i == NT - 1)
                            if G == NG - 1:
                                last.then_inc(w.f_kx, 1)
                            yield
                        pe.wait_ge(w.f_kx_out, 1)
                        for G in range(NG):
                            last = mm(bank[3][0:FH, :], w.ksc[:, G, :], w.qp[:, G, :], start=G == 0, stop=G == NG - 1)
                        last.then_inc(w.f_den, 1)
                        turn(w, bank[2], w.kx, "kx")
                        yield
                        pe.wait_ge(w.turned_out, turn_no("kx"))
                        for h in range(FH):
                            G, g = divmod(h, GH)
                            last = mm(w.p[FF * g:FF * (g + 1), 0, G * D:(G + 1) * D], w.kx_T[:, h * FF:(h + 1) * FF],
                                      wvp[:, h, :], start=True, stop=True)
                        last.then_inc(w.f_z, 1)
                        yield
                        pe.wait_ge(w.f_den_inv, 1)
                        for G in range(NG):
                            if G == NG - 1:
                                pe.wait_ge(w.f_z_out, 1)
                            mm(bank[(G + 1) % 4], headrep[:, G, :], w.dinv, start=True, stop=True).then_inc(w.f_spread, 1)
                            yield
                        pe.wait_ge(w.f_scaled, NG)
                        for i in range(NT):
                            for G in range(NG):
                                last = mm(w.y[:, i, :], w.qn[:, G, i * P:(i + 1) * P], w.z[:, G, :],
                                          start=G == 0, stop=G == NG - 1)
                            if i == NT - 1:
                                last.then_inc(w.f_y, 1)
                            yield
                        yield from turn_x(w, 4)
                        pe.wait_ge(w.turned_out, turn_no("x 4"))
                        yield from attention(w, cross1)
                        yield from turn_x(w, 5)

                        pe.wait_ge(w.g_sum, 1)
                        mm(bank[3][0:1, 0:NE], w.xsum[:, :], gate_w[:, :], start=True, stop=True).then_inc(w.g_logit, 1)
                        yield
                        pe.wait_ge(w.g_weights, 1)
                        mm(bank[3][:, 8:10], ones[0:1, :], w.gw1[:, :], start=True, stop=True).then_inc(w.g_spread, 1)
                        yield
                        pe.wait_ge(w.g_ready, 1)

                        for s in range(TOPK):
                            pe.wait_ge(w.e_in, 16 * (s + 1))
                            if s:
                                pe.wait_ge(w.e_done, s)
                            yield from attention(w, experts[s])
                            pe.wait_ge(w.e_x1, s + 1)
                            turn(w, bank[0], w.x1, f"x1 {s}")
                            yield
                            pe.wait_ge(w.turned_out, turn_no(f"x1 {s}"))
                            for k in range(NT):
                                mm(bank[k], w.ew[:, E1 + k * P:E1 + (k + 1) * P], w.x1_T[:, :],
                                   start=True, stop=True).then_inc(w.hidden, 1)
                                yield
                            pe.wait_ge(w.hidden_out, NT * (s + 2))
                            for i in range(NT):
                                for k in range(NT):
                                    c = E2 + k * D
                                    last = mm(w.y[:, i, :], w.hid[:, k, i * P:(i + 1) * P], w.ew[:, c:c + D],
                                              start=k == 0, stop=k == NT - 1)
                                if i == NT - 1:
                                    last.then_inc(w.e_y2, 1)
                                yield

                    both(stream(s0), stream(s1))

                @block.scalar
                def _(act):
                    actv, copy = nc.scalar.activation, nc.scalar.copy

                    def take(w, dst, bank, name):
                        act.wait_ge(w.turned, turn_no(name))
                        copy(dst, bank).then_inc(w.turned_out, 1)

                    def attention(w, a):
                        act.wait_ge(w.projected, a.past("projected") + 1)
                        actv(w.k_full[:, 0:a.nk], w.bank[1][:, 0:a.nk], ACT.Identity, bias=a.bk).then_inc(w.biased, 1)
                        act.wait_ge(w.projected, a.past("projected") + 2)
                        if a.expert is not None:
                            act.wait_ge(w.e_bias, a.expert + 1)
                        actv(w.q_full, w.bank[0], ACT.Identity, bias=a.bq, scale=a.scale).then_inc(w.biased, 1)
                        yield
                        for i in range(2 * NG):
                            G, keys = i % NG, i < NG
                            act.wait_ge(w.selected, a.past("selected") + i + 1)
                            dst, n = (w.k_dense, a.nk) if keys else (w.q_st, S)
                            copy(dst[0:ST, G, 0:n], w.bank[(3, 1)[i % 2]][0:ST, 0:n]).then_inc(w.stacked, 1)
                            if i % 2:
                                yield

                        def weights(G, tile):
                            u, g = G * a.units + tile // GH, tile % GH
                            act.wait_ge(w.scored, a.past("scored") + G * a.tiles + tile + 1)
                            if u >= 2 and g == 0:
                                act.wait_ge(w.pv_done, a.past("pv_done") + u - 1)
                            bank = w.bank[a.ring.index(tile) % 2]
                            if a.kind == "causal":
                                lo = tile // GH * P
                                copy(w.pt[:, u % 2, g, lo:S], bank[:, lo:S]).then_inc(w.weighted, 1)
                            else:
                                actv(w.pt[:, u % 2, g, :], bank, ACT.Exp).then_inc(w.weighted, 1)

                        def outputs(G):
                            act.wait_ge(w.pv_done, a.past("pv_done") + (G + 1) * a.units)
                            if G >= 2:
                                act.wait_ge(w.o_turned, a.past("o_turned") + G - 1)
                            copy(w.o_sb[:, G % 2, :], w.bank[3]).then_inc(w.o_out, 1)

                        for G in range(NG):
                            for tile in range(a.tiles):
                                weights(G, tile)
                                if tile == GH - 1 and G:
                                    outputs(G - 1)
                                yield
                        outputs(NG - 1)
                        yield
                        take(w, w.heads_T[:, :], w.bank[1], f"heads {a.name}")
                        yield

                    def stream(w):
                        lin, cross0, cross1, *experts = attentions(w)
                        yield from attention(w, lin)
                        take(w, w.x_T[:, :], w.bank[0], "x 1")
                        yield
                        yield from attention(w, cross0)

                        take(w, w.xn_T[:, :], w.bank[0], "xn")
                        yield
                        act.wait_ge(w.rows_turned, 1)
                        copy(w.nm_row[:, :, :], w.bank16[0][0:2, :].rearrange("p (w s) -> p w s", w=2)).then_inc(w.rows_out, 1)
                        yield
                        for k in range(2 * NT):
                            j, which = k % NT, k // NT
                            act.wait_ge(w.rescored, k + 1)
                            actv((w.disp if which == 0 else w.comb)[:, j, :], w.bank[j], ACT.Exp).then_inc(w.mix_weights, 1)
                            yield
                        take(w, w.slots_T[:, :], w.bank[2], "slots")
                        yield
                        for k in range(NT):
                            act.wait_ge(w.hidden, k + 1)
                            actv(w.hid[:, k, :], w.bank[k], ACT.Gelu).then_inc(w.hidden_out, 1)
                            yield
                        act.wait_ge(w.processed, 1)
                        copy(w.proc[:, :, 0:D], w.y).then_inc(w.processed_out, 1)
                        yield
                        take(w, w.x_T[:, :], w.bank[0], "x 3")
                        yield

                        for G in range(NG):
                            act.wait_ge(w.f_q, G + 1)
                            actv(w.qp[:, G, :], w.bank[G], ACT.Exp, bias=bqf[:, G:G + 1]).then_inc(w.f_q_exp, 1)
                            yield
                        for i in range(NT):
                            act.wait_ge(w.f_k_biased, i + 1)
                            actv(w.kp[:, i, :], w.kpre[:, i % 2, :], ACT.Exp).then_inc(w.f_k_exp, 1)
                            yield
                        take(w, w.kx_T[:, :], w.bank[2], "kx")
                        yield
                        take(w, w.x_T[:, :], w.bank[0], "x 4")
                        yield
                        yield from attention(w, cross1)
                        take(w, w.x_T[:, :], w.bank[0], "x 5")
                        yield

                        act.wait_ge(w.g_top, 1)
                        actv(w.gexp[0:1, 0:NE], w.gdiff[0:1, 0:NE], ACT.Exp, accum_out=w.gsum[0:1, 0:1])
                        actv(w.gexp[0:1, 4:6], w.gdiff[0:1, 4:6], ACT.Exp).then_inc(w.g_exp, 1)
                        yield

                        for s in range(TOPK):
                            yield from attention(w, experts[s])
                            take(w, w.x1_T[:, :], w.bank[0], f"x1 {s}")
                            yield
                            for k in range(NT):
                                act.wait_ge(w.hidden, NT * (s + 1) + k + 1)
                                actv(w.hid[:, k, :], w.bank[k], ACT.Relu, bias=w.ew[:, EB + k:EB + k + 1])\
                                    .then_inc(w.hidden_out, 1)
                                yield

                    both(stream(s0), stream(s1))

                @block.vector
                def _(dve):
                    V = nc.vector
                    step = [0]

                    def link(ins):
                        step[0] += 1
                        ins.then_inc(dve_step, 1)
                        dve.wait_ge(dve_step, step[0])

                    def attention(w, a):
                        for i, (full, hi, lo, n) in enumerate(((w.k_full, w.k_hi, w.k_lo, a.nk),
                                                               (w.q_full, w.q_hi, w.q_lo, S))):
                            dve.wait_ge(w.biased, a.past("biased") + i + 1)
                            if a.kind == "causal":
                                link(V.tensor_scalar(full[:, 0:n], full[:, 0:n], 0.0, 1e-6, ALU.max, ALU.add))
                            link(V.tensor_copy(hi[:, 0:n], full[:, 0:n]))
                            V.tensor_tensor(lo[:, 0:n], full[:, 0:n], hi[:, 0:n], ALU.subtract).then_inc(w.split, 1)
                            yield
                        dve.wait_ge(w.projected, a.past("projected") + 3)
                        if a.expert is not None:
                            dve.wait_ge(w.e_rest, 32 * (a.expert + 1))
                        V.tensor_tensor(w.v[:, 0:a.units, 0:H * (DH + 1)].rearrange("p k (h c) -> p k h c", h=H)[:, :, :, 0:DH],
                                        w.bank[2][:, 0:a.units * D].rearrange("p (k h d) -> p k h d", k=a.units, h=H),
                                        a.bv.rearrange("p (h d) -> p h d", h=H).unsqueeze(1)
                                        .to_broadcast([P, a.units, H, DH]), ALU.add).then_inc(w.v_ready, 1)
                        yield
                        dve.wait_ge(w.stacked, a.past("stacked") + NG)
                        for g in range(GH):
                            last = V.tensor_scalar(w.k_st[0:ST, :, g, 0:a.nk], w.k_dense[0:ST, :, 0:a.nk],
                                                   colmask[0:ST, g:g + 1], None, ALU.mult)
                        last.then_inc(w.k_ready, 1)
                        yield

                        def reduce(G, i):
                            n = G * a.msteps + i
                            dve.wait_ge(w.max_scored, a.past("max_scored") + n + 1)
                            if a.self_keys:
                                qt, g = i // GH, i % GH
                                V.tensor_reduce(w.neg_max[:, G, qt, g:g + 1], w.bank[2][:, 0:a.nk], AX.X, ALU.max,
                                                negate=True).then_inc(w.reduced, 1)
                            else:
                                qt, g = i // 2, 2 * (i % 2)
                                V.tensor_reduce(w.neg_max[:, G, qt, g:g + 2],
                                                w.bank[2][:, 0:2 * SKP].rearrange("p (j k) -> p j k", j=2), AX.X,
                                                ALU.max, negate=True).then_inc(w.reduced, 1)

                        def parts(G):
                            dve.wait_ge(w.reduced, a.past("reduced") + (G + 1) * a.msteps)
                            link(V.tensor_scalar(w.m_full[:, :, :], w.neg_max[:, G, :, :], MCAP, 1.0 / MSCALE,
                                                 ALU.min, ALU.mult))
                            if G:
                                dve.wait_ge(w.m_turned, a.past("m_turned") + G)
                            link(V.tensor_copy(w.m_parts[:, :, 0, :], w.m_full[:, :, :]))
                            V.tensor_tensor(w.m_parts[:, :, 1, :], w.m_full[:, :, :], w.m_parts[:, :, 0, :], ALU.subtract)\
                                .then_inc(w.m_parts_ready, 1)

                        def m_rows(G):
                            dve.wait_ge(w.m_turned, a.past("m_turned") + G + 1)
                            V.tensor_copy(w.q_st[ST:MR, G, :], w.bank16[a.ring.index("max") % 2][ST:MR, 0:S])\
                                .then_inc(w.m_rows, 1)

                        def diagonal(G, tile):
                            u, (kt, g) = G * a.units + tile // GH, divmod(tile, GH)
                            dve.wait_ge(w.weighted, a.past("weighted") + G * a.tiles + tile + 1)
                            block_ = w.pt[:, u % 2, g, kt * P:(kt + 1) * P]
                            V.tensor_tensor(block_, block_, causal[:, :], ALU.mult).then_inc(w.diagonal, 1)

                        def normalise(G, k):
                            dve.wait_ge(w.o_turned, a.past("o_turned") + G + 1)
                            o = w.bank[k].rearrange("p (t g c) -> p t g c", t=NT, g=GH)
                            if a.kind in ("causal", "cross_key"):
                                link(V.tensor_scalar(w.rden[:, :, :], o[:, :, :, DH], 1e-6 if a.kind == "causal" else 1e-30,
                                                     None, ALU.max))
                                link(V.reciprocal(w.rden[:, :, :], w.rden[:, :, :]))
                            else:
                                link(V.reciprocal(w.rden[:, :, :], o[:, :, :, DH]))
                            c = GH * DH * G
                            V.tensor_tensor(w.heads[:, :, c:c + GH * DH].rearrange("p t (g d) -> p t g d", g=GH),
                                            o[:, :, :, 0:DH], w.rden[:, :, :].unsqueeze(3).to_broadcast([P, NT, GH, DH]),
                                            ALU.mult).then_inc(w.normed, 1)

                        for i in range(a.msteps):
                            reduce(0, i)
                            yield
                        if a.has_max:
                            parts(0)
                        out_at = a.ring.index("out") - 1
                        for G in range(NG):
                            ahead = a.msteps // GH // (a.units if a.self_keys else 1) if G < NG - 1 else 0
                            for tile in range(a.tiles):
                                for i in range(ahead if a.self_keys or tile < GH else 0):
                                    reduce(G + 1, tile * ahead + i)
                                    if i:
                                        yield
                                if tile == 0 and a.has_max:
                                    m_rows(G)
                                if a.kind == "causal":
                                    diagonal(G, tile)
                                if a.ring[out_at] == tile and G:
                                    normalise(G - 1, a.ring.index("out") % 2)
                                if tile == a.tiles - 1 and a.has_max and G < NG - 1:
                                    parts(G + 1)
                                yield
                        normalise(NG - 1, 0)
                        yield

                    def rsqrt(w, npow, src, eps, op=ALU.add):
                        k = npow[0]
                        V.tensor_scalar(w.var[:, k, :], src, eps, None, op).then_inc(w.var_ready, 1)
                        yield
                        dve.wait_ge(w.rstd_ready, k + 1)
                        npow[0] += 1

                    def layernorm(w, npow, dst):
                        for i in range(NT):
                            last = V.bn_stats(w.stats[:, i, :], w.r[:, i, :])
                        link(last)
                        for i in range(NT):
                            last = V.bn_aggr(w.mv[:, i, :], w.stats[:, i, :])
                        link(last)
                        yield from rsqrt(w, npow, w.mv[:, :, 1], LN_EPS)
                        for i in range(NT):
                            last = V.tensor_scalar(dst[:, i, 0:D], w.r[:, i, :], w.mv[:, i, 0:1],
                                                   w.rstd[:, npow[0] - 1, i:i + 1], ALU.subtract, ALU.mult)
                        return last

                    def stream(w):
                        lin, cross0, cross1, *experts = attentions(w)
                        npow, nxb = [0], [0]

                        def add_residual(ready, count):
                            dve.wait_ge(ready, count)
                            nxb[0] += 1
                            dve.wait_ge(w.xb_done, nxb[0])
                            link(V.tensor_tensor(w.r[:, :, :], w.y, w.xb[:, :, :], ALU.add))

                        def new_x():
                            last = yield from layernorm(w, npow, w.x)
                            last.then_inc(w.x_done, 1)
                            yield

                        dve.wait_ge(w.mask_loaded, 16)
                        V.tensor_scalar(w.bias_k[:, :], w.mask_k[:, :], 0, -BIG, ALU.is_equal, ALU.mult)
                        V.memset(w.q_st[ST:MR, :, :], 0.0).then_inc(w.bias_ready, 1)
                        yield from attention(w, lin)
                        add_residual(w.y_ready, 1)
                        yield from new_x()
                        yield from attention(w, cross0)
                        add_residual(w.y_ready, 2)
                        yield from new_x()

                        dve.wait_ge(w.x_done, 2)
                        for i in range(NT):
                            link(V.tensor_tensor(squares[:, :], w.x[:, i, 0:D], w.x[:, i, 0:D], ALU.mult))
                            link(V.tensor_reduce(w.nmax[:, 0, i:i + 1], squares[:, :], AX.X, ALU.add))
                        yield from rsqrt(w, npow, w.nmax[:, 0, :], 1e-24, ALU.max)
                        for i in range(NT):
                            last = V.scalar_tensor_tensor(out=w.xn[:, i, 0:D], in0=w.x[:, i, 0:D],
                                                          scalar=w.rstd[:, npow[0] - 1, i:i + 1],
                                                          in1=rows[:, 7, :], op0=ALU.mult, op1=ALU.mult)
                        last.then_inc(w.mix_normed, 1)
                        yield
                        for i in range(2 * NT):
                            dve.wait_ge(w.logits, i + 1)
                            V.tensor_reduce(w.nmax[:, i // NT, i % NT:i % NT + 1], w.bank[i % NT], AX.X, ALU.max,
                                            negate=True).then_inc(w.logits_max, 1)
                            yield
                        dve.wait_ge(w.logits_max, 2 * NT)
                        link(V.tensor_scalar(w.nm_full[:, :, :], w.nmax[:, :, :], 1.0 / MSCALE, None, ALU.mult))
                        link(V.tensor_copy(w.nm_parts[:, :, :, 0], w.nm_full[:, :, :]))
                        V.tensor_tensor(w.nm_parts[:, :, :, 1], w.nm_full[:, :, :], w.nm_parts[:, :, :, 0], ALU.subtract)\
                            .then_inc(w.logits_max, 1)
                        yield
                        dve.wait_ge(w.slots_summed, 1)
                        pairs = lambda a: a.rearrange("p (a b) -> p a b", a=2)
                        link(V.reciprocal(pairs(w.rsum[:, 0, :]), w.four[:, :, :, D]))
                        for j in range(NT):
                            last = V.tensor_scalar(w.slots[:, j, :], w.four[:, j // 2, j % 2, 0:D], w.rsum[:, 0, j:j + 1],
                                                   None, ALU.mult)
                        last.then_inc(w.slots_out, 1)
                        yield
                        dve.wait_ge(w.combined, 1)
                        link(V.reciprocal(pairs(w.rsum[:, 1, :]), w.four[:, :, :, D]))
                        for j in range(NT):
                            last = V.scalar_tensor_tensor(out=w.r[:, j, :], in0=w.four[:, j // 2, j % 2, 0:D],
                                                          scalar=w.rsum[:, 1, j:j + 1], in1=w.x[:, j, 0:D],
                                                          op0=ALU.mult, op1=ALU.add)
                        link(last)
                        yield from new_x()

                        for i in range(NT):
                            dve.wait_ge(w.f_k, i + 1)
                            if i >= 2:
                                dve.wait_ge(w.f_k_exp, i - 1)
                            V.tensor_tensor(w.kpre[:, i % 2, :], w.bank[i], bkf[:, :], ALU.add).then_inc(w.f_k_biased, 1)
                            yield
                        dve.wait_ge(w.f_kx, 1)
                        link(V.tensor_copy(pairs(w.ks[:, :]), w.four[:, :, :, D]))
                        for G in range(NG):
                            V.tensor_scalar(w.ksc[:, G, :], headmask[:, G, :], w.ks[:, G:G + 1], None, ALU.mult)
                        V.tensor_copy(w.kx[:, :, :].rearrange("p (a b) d -> p a b d", a=2), w.four[:, :, :, 0:D])\
                            .then_inc(w.f_kx_out, 1)
                        yield
                        dve.wait_ge(w.f_den, 1)
                        link(V.tensor_scalar(w.den, w.bank[3][0:FH, :], 1e-6, None, ALU.add))
                        V.reciprocal(w.dinv, w.den).then_inc(w.f_den_inv, 1)
                        yield
                        dve.wait_ge(w.f_z, 1)
                        for G in range(NG):
                            last = V.scalar_tensor_tensor(out=w.z[:, G, :], in0=bvp[:, G, :], scalar=w.ks[:, G:G + 1],
                                                          in1=w.bank[0][:, G * D:(G + 1) * D], op0=ALU.mult, op1=ALU.add)
                        last.then_inc(w.f_z_out, 1)
                        yield
                        for G in range(NG):
                            dve.wait_ge(w.f_spread, G + 1)
                            V.tensor_tensor(w.qn[:, G, :], w.bank[(G + 1) % 4], w.qp[:, G, :], ALU.mult)\
                                .then_inc(w.f_scaled, 1)
                            yield
                        add_residual(w.f_y, 1)
                        yield from new_x()
                        yield from attention(w, cross1)
                        add_residual(w.y_ready, 3)
                        yield from new_x()

                        dve.wait_ge(w.turned_out, turn_no("x 5"))
                        V.tensor_reduce(w.xsum[:, :], w.x_T[:, :], AX.X, ALU.add).then_inc(w.g_sum, 1)
                        yield
                        dve.wait_ge(w.g_logit, 1)
                        link(V.scalar_tensor_tensor(out=w.logit8[0:1, 0:NE], in0=w.bank[3][0:1, 0:NE], scalar=1.0 / S,
                                                    in1=gate_b[:, :], op0=ALU.mult, op1=ALU.add))
                        link(V.max(w.top8[:, :], w.logit8[:, :]))
                        V.max_index(w.idx8[:, :], w.top8[:, :], w.logit8[:, :])
                        V.tensor_scalar(w.gdiff[0:1, 0:NE], w.logit8[0:1, 0:NE], w.top8[0:1, 0:1], None, ALU.subtract)
                        V.tensor_scalar(w.gdiff[0:1, 4:6], w.top8[0:1, 0:2], w.top8[0:1, 0:1], None, ALU.subtract)\
                            .then_inc(w.g_top, 1)
                        yield
                        dve.wait_ge(w.g_exp, 1)
                        link(V.reciprocal(w.gsum[0:1, 1:2], w.gsum[0:1, 0:1]))
                        V.tensor_scalar(w.gw1[:, :], w.gexp[0:1, 4:6], w.gsum[0:1, 1:2], None, ALU.mult)\
                            .then_inc(w.g_weights, 1)
                        yield
                        dve.wait_ge(w.g_spread, 1)
                        V.tensor_copy(w.gw[:, :], w.bank[3][:, 8:10]).then_inc(w.g_ready, 1)
                        yield

                        for s in range(TOPK):
                            dve.wait_ge(w.e_in, 16 * (s + 1))
                            V.tensor_scalar(w.ebq[:, s:s + 1], w.ew[:, EIN - 2:EIN - 1], DH ** -0.5, None, ALU.mult)\
                                .then_inc(w.e_bias, 1)
                            yield from attention(w, experts[s])
                            add_residual(w.y_ready, s + 4)
                            last = yield from layernorm(w, npow, w.norm)
                            link(last)
                            wide = lambda k: w.er[:, k, :].unsqueeze(1).to_broadcast([P, NT, D])
                            link(V.tensor_tensor(w.norm, w.norm, wide(2), ALU.mult))
                            V.tensor_tensor(w.x1, w.norm, wide(3), ALU.add).then_inc(w.e_x1, 1)
                            yield
                            add_residual(w.e_y2, s + 1)
                            last = yield from layernorm(w, npow, w.norm)
                            link(last)
                            link(V.tensor_tensor(w.norm, w.norm, wide(5), ALU.mult))
                            link(V.tensor_tensor(w.norm, w.norm, wide(6), ALU.add))
                            out, prev = (w.acc, w.x[:, :, 0:D]) if s == 0 else (w.r[:, :, :], w.acc)
                            ins = V.scalar_tensor_tensor(out=out, in0=w.norm, scalar=w.gw[:, s:s + 1], in1=prev,
                                                         op0=ALU.mult, op1=ALU.add)
                            if s == 0:
                                ins.then_inc(w.e_done, 1)
                            else:
                                link(ins)
                            yield
                        yield from new_x()

                    both(stream(s0), stream(s1))

            nc.all_engine_barrier()
            nc.gpsimd.sem_clear(range(sems[0].num, sems[-1].num + 1))
            nc.all_engine_barrier()


def constants():
    import numpy as np
    c32 = np.zeros((P, 2 * P + GH + NG * FH), np.float32)
    p = np.arange(P)
    c32[:, 0:P] = np.eye(P)
    c32[:, P:2 * P] = p[:, None] <= p[None, :]
    for g in range(GH):
        c32[:, 2 * P + g] = (p % 32) // DH == g
    for G in range(NG):
        for g in range(GH):
            c32[32 * g:32 * g + 32, 2 * P + GH + G * FH + GH * G + g] = 1
    headrep = np.zeros((FH, NG, P), np.float32)
    for h in range(FH):
        headrep[h, h // GH, (h % GH) * FF:(h % GH + 1) * FF] = 1
    sel = np.zeros((2, P, 2, NG, ST), np.float16)
    for G in range(NG):
        for part in range(3):
            for c in range(32):
                sel[0, 32 * G + c, int(part == 1), G, 32 * part + c] = 1
                sel[1, 32 * G + c, int(part == 2), G, 32 * part + c] = 1
    c16 = np.concatenate([np.eye(P), BIG * np.eye(P), sel[0].reshape(P, -1), sel[1].reshape(P, -1)], 1).astype(np.float16)
    krow = np.zeros((2, GH, NG, GH), np.float16)
    for g in range(GH):
        krow[:, g, :, g] = MSCALE
    krow = krow.reshape(2 * GH, NG, GH, 1)
    return {
        "c32": c32, "c16": c16, "headrep": headrep,
        "krows": np.ascontiguousarray(np.broadcast_to(krow, (2 * GH, NG, GH, S))),
        "scale_rows": np.full((2, P), MSCALE, np.float16),
        "bigrow": np.full((1, NG, S), BIG, np.float16),
    }


def layout(i):
    import numpy as np
    i = {k: np.asarray(a) for k, a in i.items()}
    cut = lambda w: w.reshape(-1, P, w.shape[1]).transpose(1, 0, 2)
    per_head = lambda w: w.reshape(FH, FD, D).transpose(1, 0, 2)
    qkv = i["L0_attn_qkv_w"].T
    kv, bkv = i["L0_xattn_Wkv"], i["L0_xattn_bkv"]
    mats = [qkv[:, 0:D], qkv[:, D:2 * D], qkv[:, 2 * D:], i["L0_attn_out_w"].T, i["L0_xattn_Wq"], kv[:, 0:D], kv[:, D:],
            i["L0_xattn_Wout"], i["L1_xattn_Wq"].T, i["L1_xattn_Wk"].T, i["L1_xattn_Wv"].T, i["L1_xattn_Wo"].T]
    qb = i["L0_attn_qkv_b"]
    ew = np.concatenate([
        i["L1_ffn_in_proj_w"].transpose(0, 2, 1),
        i["L1_ffn_in_proj_b"][:, 0:2 * D].reshape(NE, 2, D).transpose(0, 2, 1), i["L1_ffn_out_proj_w"].transpose(0, 2, 1),
        i["L1_ffn_lin1_w"].transpose(0, 2, 1),
        i["L1_ffn_lin2_w"].transpose(0, 2, 1).reshape(NE, HID // P, P, D).transpose(0, 2, 1, 3).reshape(NE, P, HID),
        i["L1_ffn_lin1_b"].reshape(NE, HID // P, P).transpose(0, 2, 1)], 2)
    er = np.stack([i["L1_ffn_in_proj_b"][:, 2 * D:], i["L1_ffn_out_proj_b"], i["L1_ffn_ln1_w"], i["L1_ffn_ln1_b"],
                   i["L1_ffn_lin2_b"], i["L1_ffn_ln2_w"], i["L1_ffn_ln2_b"]], 1)
    return {
        "x": i["x"], "x_T": i["x"].transpose(0, 2, 1), "ctx_T": i["ctx_1024"].transpose(0, 2, 1),
        "mask_k": i["mask_Bx1xS2_if1"],
        "mask_q": i["mask_1x1xSxS2_ik0"].reshape(NT, P, SK).transpose(1, 0, 2),
        "mask_kq": i["mask_1x1xSxS2_ik0"].reshape(S, SK).T,
        "w_a": np.stack(mats, 1),
        "cols": np.stack([qb[0:D], qb[D:2 * D], i["L0_xattn_bq"], bkv[0:D], i["L1_xattn_bq"], i["L1_xattn_bk"]], 1),
        "rows": np.stack([qb[2 * D:], i["L0_attn_out_b"], bkv[D:], i["L0_xattn_bout"], i["L1_xattn_bv"],
                          i["L1_xattn_bo"], i["L1_attn_bproj"], i["L0_ffn_gamma_x"], i["L0_ffn_gamma_slot"]], 0),
        "w1": i["L0_ffn_w1"], "w2": cut(i["L0_ffn_w2"]), "slots": cut(i["L0_ffn_slot_embeds"].reshape(NSLOT, D)),
        "wq_t": per_head(i["L1_attn_Wq"].T), "wk_t": per_head(i["L1_attn_Wk"].T), "wv_t": per_head(i["L1_attn_Wv"].T),
        "wp": per_head(i["L1_attn_Wproj"]), "feat": np.stack([i["L1_attn_wq_feat"], i["L1_attn_wk_feat"]], 1),
        "fbias": np.stack([i[f"L1_attn_b{n}"].reshape(FH, FD).T for n in "qkv"], 1),
        "gate_w": i["L1_ffn_gate_w"].T, "gate_b": i["L1_ffn_gate_b"].reshape(1, NE), "ew": ew, "er": er,
    }


def kernel(**inputs):
    import numpy as _np
    import concourse.bacc as _bacc
    from concourse import mybir as _mybir
    from concourse.bass_utils import run_bass_kernel_spmd as _run

    nc = _bacc.Bacc("TRN2", target_bir_lowering=False, num_devices=1)
    arrays, aps = {}, {}
    for name, a in {**layout(inputs), **constants()}.items():
        arrays[f"in_{name}"] = _np.ascontiguousarray(a)
        aps[name] = nc.dram_tensor(f"in_{name}", a.shape, _mybir.dt.from_np(a.dtype), kind="ExternalInput").ap()
    aps["out"] = nc.dram_tensor("out_0", (B, S, D), _mybir.dt.float32, kind="ExternalOutput").ap()
    build(nc, aps)
    r = _run(nc, [arrays], core_ids=[0])
    return r.results[0]["out_0"]
```

```python
from contextlib import ExitStack

import concourse.bass as bass
from concourse import mybir

F32 = mybir.dt.float32
F16 = mybir.dt.float16
I32 = mybir.dt.int32
U32 = mybir.dt.uint32
ALU = mybir.AluOpType
ACT = mybir.ActivationFunctionType
AX = mybir.AxisListType

B, S, D = 4, 512, 128
H, DH = 16, 8
NG, GH = 4, 4
P = 128
NT = S // P
SK = 154
SKP = P + 32
ST = 3 * GH * DH
MR = ST + 2 * GH
MK = MR + 1
LSCALE = 1024.0
MSCALE = 256.0
MCAP = 1.6e7
BIG = 60000.0
FH = 16
FD, FF = 64, 32
HID = 512
NSLOT = 512
NE, TOPK = 4, 2
EIN = 3 * D + 2
EO, E1, E2, EB = EIN, EIN + D, EIN + D + HID, EIN + D + 2 * HID
EWN = EB + HID // P
LN_EPS = 1e-5


TURNS = ("heads lin", "x 1", "heads cross 0", "xn", "slots", "x 3", "kx", "x 4", "heads cross 1", "x 5", "heads expert 0",
         "x1 0", "heads expert 1", "x1 1")


def turn_no(name):
    return TURNS.index(name) + 1


class Attention:

    def __init__(self, name, kind, before, nk, wq, wk, wv, wo, bq, bk, bv, scale):
        self.name, self.kind, self.nk, self.before = name, kind, nk, before
        self.self_keys = kind in ("causal", "self")
        self.has_max = kind != "causal"
        self.expert = None
        self.units = NT if self.self_keys else 2
        self.tiles = NT * GH if self.self_keys else GH + 1
        self.msteps = (NT * GH if self.self_keys else 2 * NT) if self.has_max else 0
        self.wq, self.wk, self.wv, self.wo = wq, wk, wv, wo
        self.bq, self.bk, self.bv, self.scale, self.k_scale = bq, bk, bv, scale, 1.0
        self.beside, self.over, self.ahead = {"causal": (0, 0, 0), "self": (1, NT * GH, 2)}.get(kind, (2, GH, 6))
        self.out_after, self.turn_after = {"causal": (7, None), "self": (7, 14)}.get(kind, (3, 1))
        m = NG if self.has_max else 0
        self.counts = {"projected": 3, "biased": 2, "split": 2, "selected": 2 * NG, "stacked": 2 * NG, "v_ready": 1,
                       "y_ready": 1, "scored": NG * self.tiles, "weighted": NG * self.tiles,
                       "pv_done": NG * self.units, "o_out": NG, "o_turned": NG, "normed": NG,
                       "max_scored": NG * self.msteps, "reduced": NG * self.msteps, "m_parts": m, "m_turned": m,
                       "m_rows": m, "diagonal": 0 if self.has_max else NG * self.tiles}

        self.late = {2 * G + i: (G - 2, 7 + 2 * i) for G in (2, 3) for i in range(2)} if kind == "self" else {}
        self.order = self.holders()

    def steps_beside(self, G, tile):
        first = (G + 1) * self.msteps + self.ahead + tile * self.beside
        return [n for n in range(first, first + self.beside) if tile < self.over and n < NG * self.msteps]

    def steps_first(self):
        return range(self.msteps + self.ahead)

    def place_max(self, n):
        return at(f"{self.name} max", n / len(self.steps_first()))

    def place_select(self, i):
        if not self.has_max:
            return at(f"{self.name} select", 0.2 + 0.1 * i)
        return at(f"{self.name} select", 0.4 + 0.3 * i) if i < 2 else at(f"{self.name} max", 0.1 * i - 0.15)

    def select_beside(self, G, tile):
        return [i for i, beside in self.late.items() if beside == (G, tile)]

    def follows(self, what, G, tile):
        return tile == (self.out_after if what == "out" else self.turn_after) and (G > 0 if what == "out" else G < NG - 1)

    def start(self):
        steps = [(self.place_select(i), "select", i) for i in range(2 * NG) if i not in self.late]
        steps += [(self.place_max(n), "max", n) for n in self.steps_first()]
        return sorted(steps, key=lambda step: step[0])

    def holders(self):
        out = []
        for _, what, n in self.start():
            if (what, n) == ("max", self.msteps + 1):
                out.append(("turn", 0))
            out.append((what, n))
        for G in range(NG):
            for tile in range(self.tiles):
                steps = [("max", n) for n in self.steps_beside(G, tile)]
                out += steps[0:1] + [("select", i) for i in self.select_beside(G, tile)]
                out += [("score", G * self.tiles + tile)] + steps[1:]
                out += [("out", G - 1)] if self.follows("out", G, tile) else []
                out += [("turn", G + 1)] if self.has_max and self.follows("turn", G, tile) else []
        return out + [("out", NG - 1)]

    def bank_of(self, what, n):
        return self.order.index((what, n)) % 3

    def bank_before(self, what, n):
        p = self.order.index((what, n))
        return self.order[p - 3] if p >= 3 else None

    def past(self, what):
        return sum(a.counts[what] for a in self.before)

    def rows(self, with_max):
        if self.kind == "cross_key":
            return MK
        return MR if self.has_max and with_max else ST


def timeline():
    plan = []

    def attention(name, select, first, group):
        plan.extend([(f"{name} select", select), (f"{name} max", first)])
        plan.extend([(f"{name} group {G}", group) for G in range(NG)])
        plan.append((f"{name} tail", 5))

    attention("lin", 9, 1, 16)
    plan.append(("norm 1", 6.2))
    attention("cross 0", 6, 12, 12)
    plan.extend([("norm 2", 6.2), ("unit norm", 4.25), ("logits", 16.1), ("weights", 14), ("slots", 6),
                 ("hidden", 6.9), ("processed", 4), ("combine", 5), ("norm 3", 6.2), ("queries", 6), ("keys", 8),
                 ("sums", 4.65), ("scale", 8), ("spread", 6), ("features", 5), ("norm 4", 6.2)])
    attention("cross 1", 6, 12, 12)
    plan.extend([("norm 5", 6.2), ("gate", 6)])
    for s in range(TOPK):
        attention(f"expert {s}", 6, 24.2, 24)
        plan.extend([(f"norm x1 {s}", 7.4), (f"mlp {s}", 9), (f"norm y {s}", 9.6)])
    plan.extend([("norm 6", 6.2), ("store", 1)])
    starts = [sum(length for _, length in plan[:i]) for i in range(len(plan))]
    return {name: (start, length) for (name, length), start in zip(plan, starts)}


TIMELINE = timeline()
LAG = 9


def at(phase, part=0.0):
    start, length = TIMELINE[phase]
    return start + length * part


def by_plan(*streams):
    streams = [(n * LAG, stream) for n, stream in enumerate(streams)]
    due = [(lag + next(stream), n) for n, (lag, stream) in enumerate(streams)]
    while due:
        now, n = min(due)
        due.remove((now, n))
        lag, stream = streams[n]
        then = next(stream, None)
        if then is not None:
            assert then + lag >= now
            due.append((then + lag, n))


class Stream:

    def __init__(self, n, sb, psum, sem):
        name = lambda what: f"{what}_{n}"
        self.x = sb(name("x"), [P, NT, D + 1])
        self.x_T = sb(name("x_T"), [P, S])
        self.xb = sb(name("xb"), [P, NT, D])
        self.r = sb(name("r"), [P, NT, D])
        self.stats = sb(name("stats"), [P, NT, 6])
        self.mv = sb(name("mv"), [P, NT, 2])
        self.var = sb(name("var"), [P, 11, NT])
        self.rstd = sb(name("rstd"), [P, 11, NT])
        self.c_T = sb(name("c_T"), [P, SKP + 96])
        self.mask_k = sb(name("mask_k"), [1, SKP], I32)
        self.bias_k = sb(name("bias_k"), [1, SKP], F16)
        self.k_st = sb(name("k_st"), [P, NG, GH, S], F16)
        self.q_st = sb(name("q_st"), [P, NG, S], F16)
        self.v = sb(name("v"), [P, NT, H * (DH + 1) + 32 - DH - 1])
        self.pt = sb(name("pt"), [P, 2, GH, S])
        self.o_sb = sb(name("o_sb"), [P, 2, S])
        self.hid = sb(name("hid"), [P, NT, S])
        self.neg_max = sb(name("neg_max"), [P, NG, NT, GH])
        self.m_full = sb(name("m_full"), [P, NT, GH])
        self.m_parts = sb(name("m_parts"), [P, NT, 2, GH], F16)
        self.rden = sb(name("rden"), [P, 2, NT, GH])
        self.heads_1 = sb(name("heads"), [P, NT, D + 1])
        self.heads = self.heads_1[:, :, 0:D]
        self.heads_T = sb(name("heads_T"), [P, S])
        self.xn = sb(name("xn"), [P, NT, D + 1])
        self.xn_T = sb(name("xn_T"), [P, S])
        self.nmax = sb(name("nmax"), [P, 2, NT])
        self.nm_full = sb(name("nm_full"), [P, 2, NT])
        self.nm_parts = sb(name("nm_parts"), [P, 2, NT, 2], F16)
        self.rsum = sb(name("rsum"), [P, 2, NT])
        self.ks = sb(name("ks"), [P, NG])
        self.ksc = sb(name("ksc"), [P, NG, FH])
        self.ew = sb(name("ew"), [P, EWN])
        self.er = sb(name("er"), [P, 7, D])
        self.ebq = sb(name("ebq"), [P, TOPK])
        self.xsum = sb(name("xsum"), [P, 1])
        self.logit8 = sb(name("logit8"), [1, 8])
        self.top8 = sb(name("top8"), [1, 8])
        self.idx8 = sb(name("idx8"), [1, 8], U32)
        self.gdiff = sb(name("gdiff"), [1, 8])
        self.gexp = sb(name("gexp"), [1, 8])
        self.gsum = sb(name("gsum"), [1, 2])
        self.gw1 = sb(name("gw1"), [1, 2])
        self.gw = sb(name("gw"), [P, 2])

        self.q_full, self.k_full = self.hid[:, 0, :], self.hid[:, 1, :]
        self.q_hi, self.q_lo = [self.hid[:, 2, :].bitcast(F16)[:, i * S:(i + 1) * S] for i in range(2)]
        self.k_hi, self.k_lo = [self.hid[:, 3, :].bitcast(F16)[:, i * S:(i + 1) * S] for i in range(2)]
        self.kp = self.hid
        self.k_dense = self.pt[:, 1, 0:2, :].rearrange("p a b -> p (a b)").bitcast(F16)\
            .rearrange("p (g k) -> p g k", g=NG)
        self.disp, self.comb = self.pt[:, 0, :, :], self.pt[:, 1, :, :]
        self.qp, self.qn = self.disp, self.comb
        self.kpre = self.o_sb
        self.den, self.dinv = self.o_sb[0:FH, 0, :], self.o_sb[0:FH, 1, :]
        self.slots, self.slots_T = self.heads, self.heads_T
        self.kx, self.kx_T = self.heads, self.heads_T
        self.proc, self.z, self.x1 = self.heads_1, self.heads, self.heads
        self.nm_row = self.hid[0:2, 0, :].bitcast(F16).rearrange("p (w s) -> p w s", w=2)
        self.x1_T = self.heads_T
        self.norm = self.xn[:, :, 0:D]
        self.acc = self.xn_T[:, :].rearrange("p (t d) -> p t d", t=NT)

        self.p = psum(name("psum"), [P, 4, S])
        self.bank = [self.p[:, k, :] for k in range(4)]
        self.bank16 = [self.p[:, k, :].bitcast(F16) for k in range(4)]
        self.y = self.p[:, 3, :].rearrange("p (t d) -> p t d", t=NT)
        self.four = self.p[:, 0:2, 0:2 * (D + 1)].rearrange("p a (b d) -> p a b d", b=2)

        sig = lambda what: sem(name(what))
        self.x_loaded, self.ctx_loaded, self.stored = sig("x_loaded"), sig("ctx_loaded"), sig("stored")
        self.mask_loaded, self.bias_ready, self.bias_placed = sig("mask_loaded"), sig("bias_ready"), sig("bias_placed")
        self.x_done, self.xb_done = sig("x_done"), sig("xb_done")
        self.var_ready, self.rstd_ready = sig("var_ready"), sig("rstd_ready")
        self.turned, self.turned_out = sig("turned"), sig("turned_out")
        self.projected, self.biased, self.split = sig("projected"), sig("biased"), sig("split")
        self.selected, self.stacked, self.k_masked = sig("selected"), sig("stacked"), sig("k_masked")
        self.v_ready, self.y_ready = sig("v_ready"), sig("y_ready")
        self.scored, self.weighted, self.diagonal = sig("scored"), sig("weighted"), sig("diagonal")
        self.pv_done, self.o_out, self.o_turned = sig("pv_done"), sig("o_out"), sig("o_turned")
        self.normed = sig("normed")
        self.max_scored, self.reduced, self.m_parts_ready = sig("max_scored"), sig("reduced"), sig("m_parts_ready")
        self.m_turned, self.m_rows = sig("m_turned"), sig("m_rows")
        self.mix_normed, self.logits, self.logits_max = sig("mix_normed"), sig("logits"), sig("logits_max")
        self.rows_turned, self.rows_out = sig("rows_turned"), sig("rows_out")
        self.rescored, self.mix_weights = sig("rescored"), sig("mix_weights")
        self.slots_summed, self.slots_out = sig("slots_summed"), sig("slots_out")
        self.hidden, self.hidden_out = sig("hidden"), sig("hidden_out")
        self.processed, self.processed_out, self.combined = sig("processed"), sig("processed_out"), sig("combined")
        self.f_q, self.f_q_exp, self.f_k = sig("f_q"), sig("f_q_exp"), sig("f_k")
        self.f_k_biased, self.f_k_exp = sig("f_k_biased"), sig("f_k_exp")
        self.f_kx, self.f_kx_out = sig("f_kx"), sig("f_kx_out")
        self.f_den, self.f_den_inv, self.f_spread = sig("f_den"), sig("f_den_inv"), sig("f_spread")
        self.f_scaled, self.f_z, self.f_z_out, self.f_y = sig("f_scaled"), sig("f_z"), sig("f_z_out"), sig("f_y")
        self.g_sum, self.g_logit, self.g_top, self.g_exp = sig("g_sum"), sig("g_logit"), sig("g_top"), sig("g_exp")
        self.g_weights, self.g_spread, self.g_ready = sig("g_weights"), sig("g_spread"), sig("g_ready")
        self.e_in, self.e_rest = sig("e_in"), sig("e_rest")
        self.e_bias, self.e_x1, self.e_y2, self.e_done = sig("e_bias"), sig("e_x1"), sig("e_y2"), sig("e_done")


def build(nc, t):
    with ExitStack() as ctx:
        def sb(name, shape, dt=F32):
            return ctx.enter_context(nc.sbuf_tensor(name, shape, dt))

        def psum(name, shape):
            return ctx.enter_context(nc.psum_tensor(name, shape, F32))

        sems = []

        def sem(name):
            sems.append(ctx.enter_context(nc.semaphore(name)))
            return sems[-1]

        eye = sb("eye", [P, P])
        causal = sb("causal", [P, P])
        colmask = sb("colmask", [P, GH])
        headmask = sb("headmask", [P, NG, FH])
        eye16 = sb("eye16", [P, P], F16)
        bigeye = sb("bigeye", [P, P], F16)
        select = sb("select", [P, 2, NG, ST], F16)
        select_q = sb("select_q", [P, 2, NG, ST], F16)
        scale_rows = sb("scale_rows", [2, P], F16)
        headrep = sb("headrep", [FH, NG, P])
        ones = sb("ones", [1, P])
        half = sb("half", [P, NT])
        cols = sb("cols", [P, 6])
        cols_s = sb("cols_s", [P, 6])
        rows = sb("rows", [P, 9, D])
        w_a = sb("w_a", [P, 12, D])
        w1 = sb("w1", [P, HID])
        w2 = sb("w2", [P, NT, D])
        slot_T = sb("slot_T", [P, NSLOT])
        feat = sb("feat", [FD, 2, FF])
        fbias = sb("fbias", [FD, 3, FH])
        wqf = sb("wqf", [P, FH * FF])
        wkf = sb("wkf", [P, FH * FF])
        bqf = sb("bqf", [P, NG])
        bkf = sb("bkf", [P, FH * FF])
        wvp = sb("wvp", [P, FH, D])
        bvp = sb("bvp", [P, NG, D])
        gate_w = sb("gate_w", [P, NE])
        gate_b = sb("gate_b", [1, NE])
        bias_q = sb("bias_q", [P, NT, SKP], F16)
        bias_kq = sb("bias_kq", [P, 2, S], F16)
        squares = sb("squares", [P, D])

        load_f, load_w, load_c, setup = sem("load_f"), sem("load_w"), sem("load_c"), sem("setup")
        composed, composed_out = sem("composed"), sem("composed_out")
        dve_step = sem("dve_step")
        streams = [Stream(n, sb, psum, sem) for n in range(2)]
        s0, s1 = streams

        wq_t, wk_t, wv_t = [a[0:FD].rearrange("p t (a d) -> p (t a) d", d=D)
                            for a in (s0.pt[:, 0, :, :], s0.pt[:, 1, :, :], s0.hid[:, :, :])]
        wp, bias_rep = [s0.k_st[0:FD, i:i + 2, :, :].rearrange("p a b k -> p (a b k)").bitcast(F32)
                        .rearrange("p (h d) -> p h d", h=FH) for i in (0, 2)]
        bias_rep_v = s1.hid[0:FD, 0, :].rearrange("p (h f) -> p h f", h=FH)
        slot_raw = s1.pt[:, 0, 0, :].rearrange("p (t d) -> p t d", t=NT)
        mask_q = s1.pt[:, 1, 0:2, :].rearrange("p a b -> p (a b)").bitcast(I32)[:, 0:NT * SKP]\
            .rearrange("p (t k) -> p t k", t=NT)
        mask_kq = s1.pt[:, 1, 2:4, :].bitcast(I32)

        def attentions(w):
            out = []
            head_scale = DH ** -0.5
            out.append(Attention("lin", "causal", [], S, w_a[:, 0, :], w_a[:, 1, :], w_a[:, 2, :], w_a[:, 3, :],
                                 cols_s[:, 0:1], cols_s[:, 1:2], rows[:, 0, :], LSCALE))
            out[-1].k_scale = LSCALE
            out.append(Attention("cross 0", "cross_key", out[:], SKP, w_a[:, 4, :], w_a[:, 5, :], w_a[:, 6, :], w_a[:, 7, :],
                                 cols_s[:, 2:3], cols[:, 3:4], rows[:, 2, :], head_scale))
            out.append(Attention("cross 1", "cross_full", out[:], SKP, w_a[:, 8, :], w_a[:, 9, :], w_a[:, 10, :],
                                 w_a[:, 11, :], cols_s[:, 4:5], cols[:, 5:6], rows[:, 4, :], head_scale))
            for s in range(TOPK):
                out.append(Attention(f"expert {s}", "self", out[:], S, w.ew[:, 0:D], w.ew[:, D:2 * D],
                                     w.ew[:, 2 * D:3 * D], w.ew[:, EO:EO + D], w.ebq[:, s:s + 1],
                                     w.ew[:, EIN - 1:EIN], w.er[:, 0, :], head_scale))
                out[-1].expert = s
            return out

        with nc.Block() as block:
            @block.sync
            def _(sp):
                for dst, src in ((feat[:, :, :], t["feat"]), (fbias[:, :, :], t["fbias"]), (wq_t[:, :, :], t["wq_t"]),
                                 (wk_t[:, :, :], t["wk_t"]), (wp[:, :, :], t["wp"]), (wv_t[:, :, :], t["wv_t"])):
                    sp.dma_start(dst, src).then_inc(load_f, 16)
                for dst, src in ((eye[:, :], t["c32"][:, 0:P]),
                                 (causal[:, :], t["c32"][:, P:2 * P]), (colmask[:, :], t["c32"][:, 2 * P:2 * P + GH]),
                                 (headmask[:, :, :], t["c32"][:, 2 * P + GH:2 * P + GH + NG * FH]),
                                 (headrep[:, :, :], t["headrep"]),
                                 (eye16[:, :], t["c16"][:, 0:P]), (bigeye[:, :], t["c16"][:, P:2 * P]),
                                 (select[:, :, :, :], t["c16"][:, 2 * P:2 * P + 2 * NG * ST]),
                                 (select_q[:, :, :, :], t["c16"][:, 2 * P + 2 * NG * ST:]),
                                 (s0.k_st[ST:MR, :, :, :], t["krows"]), (s1.k_st[ST:MR, :, :, :], t["krows"]),
                                 (s0.q_st[MR:MK, :, :], t["bigrow"]), (s1.q_st[MR:MK, :, :], t["bigrow"]),
                                 (scale_rows[:, :], t["scale_rows"])):
                    sp.dma_start(dst, src).then_inc(load_c, 16)
                for dst, src in ((cols[:, :], t["cols"]), (rows[:, :, :], t["rows"].partition_broadcast(P)),
                                 (w_a[:, :, :], t["w_a"]), (w1[:, :], t["w1"]), (w2[:, :, :], t["w2"]),
                                 (slot_raw[:, :, :], t["slots"]),
                                 (gate_w[:, :], t["gate_w"]), (gate_b[:, :], t["gate_b"])):
                    sp.dma_start(dst, src).then_inc(load_w, 16)
                sp.wait_ge(setup, 1)
                sp.dma_start(mask_q[:, :, 0:SK], t["mask_q"]).then_inc(load_w, 16)
                sp.dma_start(mask_kq[:, 0, :], t["mask_kq"][0:P]).then_inc(load_w, 16)
                sp.dma_start(mask_kq[0:SK - P, 1, :], t["mask_kq"][P:SK]).then_inc(load_w, 16)

            @block.vector
            def _(dve):
                step = [0]

                def link(ins):
                    step[0] += 1
                    ins.then_inc(dve_step, 1)
                    dve.wait_ge(dve_step, step[0])

                nc.vector.memset(mask_kq[:, 1, :], 0)
                nc.vector.memset(mask_q[:, :, :], 0).then_inc(setup, 1)
                nc.vector.memset(ones[:, :], 1.0)
                nc.vector.memset(half[:, :], -0.5)
                for w in streams:
                    nc.vector.memset(w.c_T[:, :], 0.0)
                    nc.vector.memset(w.mask_k[:, :], 0)
                    nc.vector.memset(w.x[:, :, D:D + 1], 1.0)
                    nc.vector.memset(w.xn[:, :, D:D + 1], 1.0)
                    nc.vector.memset(w.proc[:, :, D:D + 1], 1.0)
                    nc.vector.memset(w.logit8[:, :], -3.0e38)
                    nc.vector.memset(w.v[:, :, :], 1.0)
                dve.wait_ge(load_f, 16 * 6)
                nc.vector.tensor_copy(bias_rep[:, :, :], fbias[:, 1, :].unsqueeze(2).to_broadcast([FD, FH, P]))
                nc.vector.tensor_copy(bias_rep_v[:, :, :], fbias[:, 2, :].unsqueeze(2).to_broadcast([FD, FH, FF]))\
                    .then_inc(setup, 1)
                dve.wait_ge(load_w, 16 * 11)
                nc.vector.tensor_scalar(cols_s[:, 0:2], cols[:, 0:2], LSCALE, None, ALU.mult)
                nc.vector.tensor_scalar(cols_s[:, 2:6], cols[:, 2:6], DH ** -0.5, None, ALU.mult)
                nc.vector.tensor_scalar(rows[:, 7:9, :], rows[:, 7:9, :], float(D) ** 0.5, None, ALU.mult)
                nc.vector.tensor_scalar(bias_q[:, :, :], mask_q[:, :, :], 0, -BIG, ALU.is_equal, ALU.mult)
                link(nc.vector.tensor_scalar(bias_kq[:, :, :], mask_kq, 0, -BIG, ALU.is_equal, ALU.mult))
                for j in range(NT):
                    link(nc.vector.tensor_tensor(squares[:, :], slot_raw[:, j, :], slot_raw[:, j, :], ALU.mult))
                    link(nc.vector.tensor_reduce(s0.var[:, 0, j:j + 1], squares[:, :], AX.X, ALU.add))
                nc.vector.tensor_scalar(s0.var[:, 0, :], s0.var[:, 0, :], 1e-24, None, ALU.max).then_inc(s0.var_ready, 1)
                dve.wait_ge(s0.rstd_ready, 1)
                for j in range(NT):
                    last = nc.vector.scalar_tensor_tensor(out=s0.slots[:, j, :], in0=slot_raw[:, j, :],
                                                          scalar=s0.rstd[:, 0, j:j + 1], in1=rows[:, 8, :],
                                                          op0=ALU.mult, op1=ALU.mult)
                last.then_inc(setup, 1)
                dve.wait_ge(composed, 1)
                nc.vector.tensor_copy(wqf[:, :], s0.bank[0])
                nc.vector.tensor_copy(wkf[:, :], s0.bank[1])
                nc.vector.tensor_copy(bqf[:, :], s1.bank[0][:, 0:NG])
                nc.vector.tensor_copy(bkf[:, :], s0.bank[2])
                nc.vector.tensor_copy(bvp[:, :, :], s0.bank[3].rearrange("p (g d) -> p g d", g=NG))
                nc.vector.tensor_copy(slot_T[:, :], s1.bank[1]).then_inc(composed_out, 1)
                dve.wait_ge(composed, 2)
                for q in range(4):
                    last = nc.vector.tensor_copy(wvp[:, 4 * q:4 * q + 4, :],
                                                 s0.bank[q].rearrange("p (g d) -> p g d", g=4))
                last.then_inc(composed_out, 1)

            @block.gpsimd
            def _(pool):
                pool.wait_ge(s0.var_ready, 1)
                nc.gpsimd.tensor_tensor(s0.rstd[:, 0, :], s0.var[:, 0, :], half[:, :], ALU.pow).then_inc(s0.rstd_ready, 1)

            @block.tensor
            def _(pe):
                mm = nc.tensor.matmul
                pe.wait_ge(load_f, 16 * 6)
                pe.wait_ge(setup, 2)
                for h in range(FH):
                    G, g = divmod(h, GH)
                    out = slice(h * FF, (h + 1) * FF)
                    mm(s0.bank[0][:, out], wq_t[:, h, :], feat[:, 0, :], start=True, stop=True)
                    mm(s0.bank[1][:, out], wk_t[:, h, :], feat[:, 1, :], start=True, stop=True)
                    mm(s0.bank[2][:, out], bias_rep[:, h, :], feat[:, 1, :], start=True, stop=True)
                    mm(s1.bank[0][FF * g:FF * (g + 1), G:G + 1], feat[:, 0, :], fbias[:, 0, h:h + 1], start=True, stop=True)
                    mm(s0.bank[3][FF * g:FF * (g + 1), G * D:(G + 1) * D], bias_rep_v[:, h, :], wp[:, h, :],
                       start=True, stop=True)
                pe.wait_ge(load_c, 16 * 14)
                pe.wait_ge(setup, 3)
                for j in range(NT):
                    last = nc.tensor.transpose(s1.bank[1][:, j * P:(j + 1) * P], s0.slots[:, j, :], eye[:, :])
                last.then_inc(composed, 1)
                pe.wait_ge(composed_out, 1)
                for h in range(FH):
                    last = mm(s0.bank[h // 4][:, (h % 4) * D:(h % 4 + 1) * D], wv_t[:, h, :], wp[:, h, :],
                              start=True, stop=True)
                last.then_inc(composed, 1)

        nc.all_engine_barrier()
        nc.gpsimd.sem_clear(range(sems[0].num, sems[-1].num + 1))
        nc.all_engine_barrier()

        with nc.Fori(0, B // 2) as b:
            with nc.Block() as block:

                def of_batch(a, n):
                    return a.rearrange("(b n) r c -> n b r c", n=2)[n][bass.ds(b, 1)].squeeze(0)

                @block.sync
                def _(sp):
                    def stream(n, w):
                        one = lambda a: of_batch(a, n)
                        yield -LAG * n
                        sp.dma_start(w.x_T[:, :], one(t["x_T"])).then_inc(w.x_loaded, 16)
                        sp.dma_start(w.x[:, :, 0:D], one(t["x"]).rearrange("(t p) d -> p t d", p=P)).then_inc(w.x_loaded, 16)
                        sp.dma_start(w.mask_k[:, 0:SK], one(t["mask_k"])).then_inc(w.mask_loaded, 16)
                        sp.dma_start(w.c_T[:, 0:SK], one(t["ctx_T"])).then_inc(w.ctx_loaded, 16)
                        for i in range(1, 4):
                            sp.dma_start(w.c_T[:, P + 32 * i:P + 32 * i + SK - P], one(t["ctx_T"])[:, P:SK])\
                                .then_inc(w.ctx_loaded, 16)
                        yield at("lin select", 0.1)
                        sp.wait_ge(w.bias_ready, 1)
                        sp.dma_start(w.k_st[MR:MK, :, :, 0:SKP].rearrange("p a b k -> p (a b) k"),
                                     w.bias_k[:, :].unsqueeze(1).to_broadcast([1, H, SKP])).then_inc(w.bias_placed, 16)
                        expert = attentions(w)[3]
                        for s in range(TOPK):
                            yield at("gate", 0.5) if s == 0 else at("expert 0 select", 1.0)
                            if s == 0:
                                sp.wait_ge(w.g_top, 1)
                            else:
                                sp.wait_ge(w.projected, expert.past("projected") + 3)
                                sp.wait_ge(w.biased, expert.past("biased") + 2)
                            e = sp.value_load(w.idx8[0:1, s:s + 1], min_val=0, max_val=NE - 1)
                            sp.dma_start(w.ew[:, 0:EIN], t["ew"][bass.ds(e, 1)].squeeze(0)[:, 0:EIN]).then_inc(w.e_in, 16)
                            if s:
                                yield at("mlp 0", 1.0)
                                sp.wait_ge(w.e_y2, s)
                            sp.dma_start(w.ew[:, EIN:EWN], t["ew"][bass.ds(e, 1)].squeeze(0)[:, EIN:EWN])\
                                .then_inc(w.e_rest, 16)
                            if s:
                                yield at("norm y 0", 1.0)
                                sp.wait_ge(w.e_done, s)
                            sp.dma_start(w.er[:, :, :], t["er"][bass.ds(e, 1)].squeeze(0).partition_broadcast(P))\
                                .then_inc(w.e_rest, 16)
                        yield at("store")
                        sp.wait_ge(w.x_done, 6)
                        sp.dma_start(of_batch(t["out"], n).rearrange("(t p) d -> p t d", p=P), w.x[:, :, 0:D])\
                            .then_inc(w.stored, 16)

                    by_plan(stream(0, s0), stream(1, s1))
                    for w in streams:
                        sp.wait_ge(w.stored, 16)

                @block.gpsimd
                def _(pool):
                    def stream(w):
                        npow = [0]

                        def residual(bias, ready, count, src):
                            pool.wait_ge(ready, count)
                            nc.gpsimd.tensor_tensor(w.xb[:, :, :], src, bias.unsqueeze(1).to_broadcast([P, NT, D]),
                                                    ALU.add).then_inc(w.xb_done, 1)

                        def rsqrt():
                            k = npow[0]
                            pool.wait_ge(w.var_ready, k + 1)
                            nc.gpsimd.tensor_tensor(w.rstd[:, k, :], w.var[:, k, :], half[:, :], ALU.pow)\
                                .then_inc(w.rstd_ready, 1)
                            npow[0] += 1

                        x = w.x[:, :, 0:D]
                        yield at("lin select")
                        residual(rows[:, 1, :], w.x_loaded, 32, x)
                        yield at("norm 1", 0.3)
                        rsqrt()
                        yield at("norm 1", 0.8)
                        residual(rows[:, 3, :], w.x_done, 1, x)
                        for phase in ("norm 2", "unit norm", "norm 3"):
                            yield at(phase, 0.3)
                            rsqrt()
                        yield at("norm 3", 0.8)
                        residual(rows[:, 6, :], w.x_done, 3, x)
                        yield at("norm 4", 0.3)
                        rsqrt()
                        yield at("norm 4", 0.8)
                        residual(rows[:, 5, :], w.x_done, 4, x)
                        yield at("norm 5", 0.3)
                        rsqrt()
                        for s in range(TOPK):
                            yield at(f"expert {s} select", 0.5)
                            pool.wait_ge(w.e_rest, 32 * (s + 1))
                            if s:
                                pool.wait_ge(w.e_done, s)
                            residual(w.er[:, 1, :], w.x_done, 5, x)
                            yield at(f"norm x1 {s}", 0.3)
                            rsqrt()
                            yield at(f"norm x1 {s}", 0.8)
                            residual(w.er[:, 4, :], w.e_x1, s + 1, w.x1)
                            yield at(f"norm y {s}", 0.3)
                            rsqrt()
                        yield at("norm 6", 0.3)
                        rsqrt()

                    by_plan(stream(s0), stream(s1))

                @block.tensor
                def _(pe):
                    mm, tr = nc.tensor.matmul, nc.tensor.transpose

                    def turn(w, bank, src, name):
                        for i in range(NT):
                            last = tr(bank[:, i * P:(i + 1) * P], src[:, i, 0:D], eye[:, :])
                        last.then_inc(w.turned, 1)

                    def attention(w, a):
                        bank = w.bank
                        src = w.x_T if a.self_keys else w.c_T
                        yield at(f"{a.name} select")
                        mm(bank[1][:, 0:a.nk], a.wk, src[:, 0:a.nk], start=True, stop=True).then_inc(w.projected, 1)
                        mm(bank[0], a.wq, w.x_T[:, :], start=True, stop=True).then_inc(w.projected, 1)
                        for kt in range(a.units):
                            last = mm(bank[2][:, kt * D:(kt + 1) * D], src[:, kt * P:(kt + 1) * P], a.wv,
                                      start=True, stop=True)
                        last.then_inc(w.projected, 1)
                        held_until = {"select": w.stacked, "max": w.reduced, "score": w.weighted, "out": w.normed,
                                      "turn": w.m_rows}
                        counted = {"select": "stacked", "max": "reduced", "score": "weighted", "out": "normed",
                                   "turn": "m_rows"}

                        def take_bank(what, n):
                            k, before = a.bank_of(what, n), a.bank_before(what, n)
                            if before is not None:
                                pe.wait_ge(held_until[before[0]], a.past(counted[before[0]]) + before[1] + 1)
                            elif k < 2:
                                pe.wait_ge(w.biased, a.past("biased") + 2)
                            else:
                                pe.wait_ge(w.v_ready, a.past("v_ready") + 1)
                            return k

                        def select_rows(i):
                            G, keys = i // 2, i % 2 == 0
                            if i < 2:
                                pe.wait_ge(w.split, a.past("split") + i + 1)
                            n, hi, lo, sel = (a.nk, w.k_hi, w.k_lo, select) if keys else (S, w.q_hi, w.q_lo, select_q)
                            out = bank[take_bank("select", i)][0:ST, 0:n]
                            mm(out, sel[:, 0, G, :], hi[:, 0:n], start=True, stop=False)
                            mm(out, sel[:, 1, G, :], lo[:, 0:n], start=False, stop=True).then_inc(w.selected, 1)

                        def max_step(n):
                            G, i = divmod(n, a.msteps)
                            if i == 0:
                                pe.wait_ge(w.stacked, a.past("stacked") + 2 * G + 2)
                            out = bank[take_bank("max", n)]
                            if a.self_keys:
                                qt, g = i // GH, i % GH
                                mm(out[:, 0:a.nk], w.q_st[0:ST, G, qt * P:(qt + 1) * P], w.k_st[0:ST, G, g, 0:a.nk],
                                   start=True, stop=True).then_inc(w.max_scored, 1)
                                return
                            qt, g = i // 2, 2 * (i % 2)
                            out, K = out[:, 0:2 * SKP].rearrange("p (j k) -> p j k", j=2), a.rows(False)
                            last = mm(out, w.q_st[0:K, G, qt * P:(qt + 1) * P], w.k_st[0:K, G, g:g + 2, 0:SKP],
                                      start=True, stop=a.kind == "cross_key")
                            if a.kind == "cross_full":
                                last = mm(out, bigeye[:, :], bias_q[:, qt, :].unsqueeze(1).to_broadcast([P, 2, SKP]),
                                          start=False, stop=True)
                            last.then_inc(w.max_scored, 1)

                        def turn_max(G):
                            k = take_bank("turn", G)
                            pe.wait_ge(w.m_parts_ready, a.past("m_parts") + G + 1)
                            for qt in range(NT):
                                last = tr(w.bank16[k][ST:MR, qt * P:(qt + 1) * P], w.m_parts[:, qt, :, :], eye16[:, :])
                            last.then_inc(w.m_turned, 1)

                        def score(G, tile):
                            k = take_bank("score", G * a.tiles + tile)
                            if tile == 0:
                                if a.has_max:
                                    pe.wait_ge(w.m_rows, a.past("m_rows") + G + 1)
                                else:
                                    pe.wait_ge(w.stacked, 2 * G + 2)
                                    pe.wait_ge(w.k_masked, G + 1)
                            K = a.rows(True)
                            if a.self_keys or tile < GH:
                                kt, g = divmod(tile, GH)
                                lo = kt * P if a.kind == "causal" else 0
                                out = bank[k]
                                last = mm(out[:, lo:S], w.k_st[0:K, G, g, kt * P:(kt + 1) * P], w.q_st[0:K, G, lo:S],
                                          start=True, stop=a.kind != "cross_full")
                                if a.kind == "cross_full":
                                    last = mm(out, bigeye[:, :], bias_kq[:, 0, :], start=False, stop=True)
                            else:
                                for g in range(GH):
                                    out = w.p[32 * g:32 * g + 32, k, :]
                                    last = mm(out, w.k_st[0:K, G, g, P:SKP], w.q_st[0:K, G, :], start=True,
                                              stop=a.kind != "cross_full")
                                    if a.kind == "cross_full":
                                        last = mm(out, bigeye[0:32, 0:32], bias_kq[0:32, 1, :], start=False, stop=True,
                                                  tile_position=(0, 32 * g))
                            last.then_inc(w.scored, 1)

                        def weigh(u):
                            G, kt = divmod(u, a.units)
                            done = G * a.tiles + min(GH * (kt + 1), a.tiles)
                            if a.has_max:
                                pe.wait_ge(w.weighted, a.past("weighted") + done)
                            else:
                                pe.wait_ge(w.diagonal, a.past("diagonal") + done)
                            if kt == 0 and G:
                                pe.wait_ge(w.o_out, a.past("o_out") + G)
                            if u == 0:
                                pe.wait_ge(w.v_ready, a.past("v_ready") + 1)
                                if a.expert == 0:
                                    pe.wait_ge(w.g_ready, 1)
                            rest = not a.self_keys and kt == 1
                            for g in range(GH):
                                k0, k1 = (32 * g, 32 * g + 32) if rest else (0, P)
                                lo = kt * P if a.kind == "causal" else 0
                                c = (GH * G + g) * (DH + 1)
                                last = mm(w.p[32 * g:32 * g + 32, 3, lo:S], w.v[k0:k1, kt, c:c + 32],
                                          w.pt[k0:k1, u % 2, 0 if rest else g, lo:S], start=kt == 0,
                                          stop=kt == a.units - 1 or a.kind == "causal", skip_group_check=True)
                            last.then_inc(w.pv_done, 1)

                        def turn_outputs(G):
                            k = take_bank("out", G)
                            pe.wait_ge(w.o_out, a.past("o_out") + G + 1)
                            for qt in range(NT):
                                last = tr(bank[k][:, qt * P:(qt + 1) * P], w.o_sb[:, G % 2, qt * P:(qt + 1) * P], eye[:, :])
                            last.then_inc(w.o_turned, 1)

                        if a.expert == 0:
                            yield at("expert 0 select", 0.35)
                            pe.wait_ge(w.g_weights, 1)
                            mm(bank[3][:, 8:10], ones[0:1, :], w.gw1[:, :], start=True, stop=True).then_inc(w.g_spread, 1)
                        for where, what, n in a.start():
                            yield where
                            if (what, n) == ("max", a.msteps + 1):
                                turn_max(0)
                            if what == "max":
                                max_step(n)
                            else:
                                select_rows(n)
                        for G in range(NG):
                            for tile in range(a.tiles):
                                yield at(f"{a.name} group {G}", tile / a.tiles)
                                steps = a.steps_beside(G, tile)
                                for n in steps[0:1]:
                                    max_step(n)
                                for i in a.select_beside(G, tile):
                                    select_rows(i)
                                score(G, tile)
                                yield at(f"{a.name} group {G}", (tile + 0.5) / a.tiles)
                                for n in steps[1:]:
                                    max_step(n)
                                if tile % GH == GH - 1 or tile == a.tiles - 1:
                                    u = G * a.units + tile // GH
                                    if u:
                                        weigh(u - 1)
                                if a.follows("out", G, tile):
                                    turn_outputs(G - 1)
                                if a.has_max and a.follows("turn", G, tile):
                                    turn_max(G + 1)
                        yield at(f"{a.name} tail")
                        weigh(NG * a.units - 1)
                        yield at(f"{a.name} tail", 0.2)
                        turn_outputs(NG - 1)
                        yield at(f"{a.name} tail", 0.5)
                        pe.wait_ge(w.normed, a.past("normed") + NG)
                        turn(w, bank[1], w.heads, f"heads {a.name}")
                        yield at(f"{a.name} tail", 0.7)
                        pe.wait_ge(w.turned_out, turn_no(f"heads {a.name}"))
                        if a.expert is not None:
                            pe.wait_ge(w.e_rest, 32 * (a.expert + 1))
                        for qt in range(NT):
                            last = mm(w.y[:, qt, :], w.heads_T[:, qt * P:(qt + 1) * P], a.wo, start=True, stop=True)
                        last.then_inc(w.y_ready, 1)

                    def turn_x(w, n):
                        yield at(f"norm {n}", 0.8)
                        pe.wait_ge(w.x_done, n)
                        turn(w, w.bank[0], w.x, f"x {n}")

                    def stream(w):
                        lin, cross0, cross1, *experts = attentions(w)
                        bank = w.bank
                        yield at("lin select")
                        pe.wait_ge(w.x_loaded, 32)
                        yield from attention(w, lin)
                        yield from turn_x(w, 1)
                        yield at("cross 0 select")
                        pe.wait_ge(w.ctx_loaded, 16 * 4)
                        pe.wait_ge(w.bias_placed, 16)
                        pe.wait_ge(w.turned_out, turn_no("x 1"))
                        yield from attention(w, cross0)

                        yield at("unit norm", 0.8)
                        pe.wait_ge(w.mix_normed, 1)
                        turn(w, bank[0], w.xn, "xn")
                        yield at("logits")
                        pe.wait_ge(w.turned_out, turn_no("xn"))
                        def turn_rows(which):
                            for i in range(NT):
                                last = tr(w.bank16[0][0:2, i * P:(i + 1) * P], w.nm_parts[:, which, i, :], eye16[:, :])
                            last.then_inc(w.rows_turned, 1)

                        for j in range(NT):
                            yield at("logits", j / (2 * NT))
                            mm(bank[j], w.xn_T[:, j * P:(j + 1) * P], slot_T[:, :], start=True, stop=True).then_inc(w.logits, 1)
                        yield at("logits", 0.42)
                        pe.wait_ge(w.logits_max, NT + 1)
                        turn_rows(0)
                        for j in range(NT):
                            yield at("logits", 0.5 + j / (2 * NT))
                            if j == 0:
                                pe.wait_ge(w.rows_out, 1)
                            mm(bank[j], slot_T[:, j * P:(j + 1) * P], w.xn_T[:, :], start=True, stop=True).then_inc(w.logits, 1)
                        for j in range(NT):
                            yield at("weights", j / (2 * NT))
                            pe.wait_ge(w.logits_max, NT + 2 + j)
                            mm(bank[j], scale_rows[:, :], w.nm_row[:, 0, :], start=False, stop=True,
                               skip_group_check=True).then_inc(w.rescored, 1)
                        yield at("weights", 0.5)
                        pe.wait_ge(w.logits_max, 2 * NT + 2)
                        pe.wait_ge(w.mix_weights, 1)
                        turn_rows(1)
                        for j in range(NT):
                            yield at("weights", 0.5 + j / (2 * NT))
                            k = (j + 1) % NT
                            pe.wait_ge(w.mix_weights, k + 1)
                            if k == 0:
                                pe.wait_ge(w.rows_out, 2)
                            mm(bank[k], w.xn_T[:, j * P:(j + 1) * P], slot_T[:, :], start=True, stop=False)
                            if j == 0:
                                pe.wait_ge(w.rows_out, 2)
                            mm(bank[k], scale_rows[:, :], w.nm_row[:, 1, :], start=False, stop=True).then_inc(w.rescored, 1)
                        yield at("slots")
                        pe.wait_ge(w.mix_weights, 2 * NT)
                        for j in range(NT):
                            yield at("slots", j / NT)
                            for i in range(NT):
                                last = mm(w.four[:, j // 2, j % 2, :], w.disp[:, i, j * P:(j + 1) * P], w.xn[:, i, :],
                                          start=i == 0, stop=i == NT - 1)
                            if j == NT - 1:
                                last.then_inc(w.slots_summed, 1)
                        yield at("hidden")
                        pe.wait_ge(w.slots_out, 1)
                        pe.wait_ge(w.mix_weights, 2 * NT)
                        turn(w, bank[2], w.slots, "slots")
                        yield at("hidden", 0.2)
                        pe.wait_ge(w.turned_out, turn_no("slots"))
                        for k in range(NT):
                            yield at("hidden", 0.2 + 0.2 * k)
                            mm(bank[k], w1[:, k * P:(k + 1) * P], w.slots_T[:, :], start=True, stop=True).then_inc(w.hidden, 1)
                        yield at("processed")
                        pe.wait_ge(w.hidden_out, NT)
                        for j in range(NT):
                            yield at("processed", j / NT)
                            for k in range(NT):
                                last = mm(w.y[:, j, :], w.hid[:, k, j * P:(j + 1) * P], w2[:, k, :],
                                          start=k == 0, stop=k == NT - 1)
                            if j == NT - 1:
                                last.then_inc(w.processed, 1)
                        yield at("combine")
                        pe.wait_ge(w.processed_out, 1)
                        for i in range(NT):
                            yield at("combine", i / NT)
                            for j in range(NT):
                                last = mm(w.four[:, i // 2, i % 2, :], w.comb[:, j, i * P:(i + 1) * P], w.proc[:, j, :],
                                          start=j == 0, stop=j == NT - 1)
                            if i == NT - 1:
                                last.then_inc(w.combined, 1)
                        yield from turn_x(w, 3)

                        yield at("queries")
                        pe.wait_ge(w.turned_out, turn_no("x 3"))
                        for G in range(NG):
                            yield at("queries", G / NG)
                            mm(bank[G], wqf[:, G * P:(G + 1) * P], w.x_T[:, :], start=True, stop=True).then_inc(w.f_q, 1)
                        for i in range(NT):
                            yield at("keys", i / NT)
                            pe.wait_ge(w.f_q_exp, i + 1)
                            mm(bank[i], w.x_T[:, i * P:(i + 1) * P], wkf[:, :], start=True, stop=True).then_inc(w.f_k, 1)
                        yield at("sums")
                        pe.wait_ge(w.f_k_exp, NT)
                        for G in range(NG):
                            yield at("sums", G / NG)
                            for i in range(NT):
                                last = mm(w.four[:, G // 2, G % 2, :], w.kp[:, i, G * P:(G + 1) * P], w.x[:, i, :],
                                          start=i == 0, stop=i == NT - 1)
                            if G == NG - 1:
                                last.then_inc(w.f_kx, 1)
                        yield at("scale", 0.1)
                        pe.wait_ge(w.f_kx_out, 1)
                        for G in range(NG):
                            last = mm(bank[3][0:FH, :], w.ksc[:, G, :], w.qp[:, G, :], start=G == 0, stop=G == NG - 1)
                        last.then_inc(w.f_den, 1)
                        turn(w, bank[2], w.kx, "kx")
                        yield at("scale", 0.4)
                        pe.wait_ge(w.turned_out, turn_no("kx"))
                        for h in range(FH):
                            G, g = divmod(h, GH)
                            last = mm(w.p[FF * g:FF * (g + 1), 0, G * D:(G + 1) * D], w.kx_T[:, h * FF:(h + 1) * FF],
                                      wvp[:, h, :], start=True, stop=True)
                        last.then_inc(w.f_z, 1)
                        yield at("spread")
                        pe.wait_ge(w.f_den_inv, 1)
                        for G in range(NG):
                            yield at("spread", G / NG)
                            if G == NG - 1:
                                pe.wait_ge(w.f_z_out, 1)
                            mm(bank[(G + 1) % 4], headrep[:, G, :], w.dinv, start=True, stop=True).then_inc(w.f_spread, 1)
                        yield at("features")
                        pe.wait_ge(w.f_scaled, NG)
                        for i in range(NT):
                            yield at("features", i / NT)
                            for G in range(NG):
                                last = mm(w.y[:, i, :], w.qn[:, G, i * P:(i + 1) * P], w.z[:, G, :],
                                          start=G == 0, stop=G == NG - 1)
                            if i == NT - 1:
                                last.then_inc(w.f_y, 1)
                        yield from turn_x(w, 4)
                        yield at("cross 1 select")
                        pe.wait_ge(w.turned_out, turn_no("x 4"))
                        yield from attention(w, cross1)
                        yield from turn_x(w, 5)

                        yield at("gate", 0.1)
                        pe.wait_ge(w.g_sum, 1)
                        mm(bank[3][0:1, 0:NE], w.xsum[:, :], gate_w[:, :], start=True, stop=True).then_inc(w.g_logit, 1)

                        for s in range(TOPK):
                            yield at(f"expert {s} select")
                            pe.wait_ge(w.e_in, 16 * (s + 1))
                            if s:
                                pe.wait_ge(w.e_done, s)
                            yield from attention(w, experts[s])
                            yield at(f"norm x1 {s}", 0.8)
                            pe.wait_ge(w.e_x1, s + 1)
                            turn(w, bank[0], w.x1, f"x1 {s}")
                            yield at(f"mlp {s}")
                            pe.wait_ge(w.turned_out, turn_no(f"x1 {s}"))
                            for k in range(NT):
                                yield at(f"mlp {s}", k / 8)
                                mm(bank[k], w.ew[:, E1 + k * P:E1 + (k + 1) * P], w.x1_T[:, :],
                                   start=True, stop=True).then_inc(w.hidden, 1)
                            yield at(f"mlp {s}", 0.5)
                            pe.wait_ge(w.hidden_out, NT * (s + 2))
                            for i in range(NT):
                                yield at(f"mlp {s}", 0.5 + i / 8)
                                for k in range(NT):
                                    c = E2 + k * D
                                    last = mm(w.y[:, i, :], w.hid[:, k, i * P:(i + 1) * P], w.ew[:, c:c + D],
                                              start=k == 0, stop=k == NT - 1)
                                if i == NT - 1:
                                    last.then_inc(w.e_y2, 1)

                    by_plan(stream(s0), stream(s1))

                @block.scalar
                def _(act):
                    actv, copy = nc.scalar.activation, nc.scalar.copy

                    def take(w, dst, bank, name):
                        act.wait_ge(w.turned, turn_no(name))
                        copy(dst, bank).then_inc(w.turned_out, 1)

                    def attention(w, a):
                        yield at(f"{a.name} select")
                        act.wait_ge(w.projected, a.past("projected") + 1)
                        actv(w.k_full[:, 0:a.nk], w.bank[1][:, 0:a.nk], ACT.Identity, bias=a.bk,
                             scale=a.k_scale).then_inc(w.biased, 1)
                        act.wait_ge(w.projected, a.past("projected") + 2)
                        if a.expert is not None:
                            act.wait_ge(w.e_bias, a.expert + 1)
                        actv(w.q_full, w.bank[0], ACT.Identity, bias=a.bq, scale=a.scale).then_inc(w.biased, 1)
                        def stack_rows(i):
                            G, keys = i // 2, i % 2 == 0
                            act.wait_ge(w.selected, a.past("selected") + i + 1)
                            if keys and a.kind == "causal":
                                copy(w.k_dense[0:ST, G, :], w.bank[a.bank_of("select", i)][0:ST, :]).then_inc(w.stacked, 1)
                                return
                            if not keys:
                                copy(w.q_st[0:ST, G, :], w.bank[a.bank_of("select", i)][0:ST, :]).then_inc(w.stacked, 1)
                                return
                            for g in range(GH):
                                last = actv(w.k_st[0:ST, G, g, 0:a.nk], w.bank[a.bank_of("select", i)][0:ST, 0:a.nk], ACT.Identity,
                                            scale=colmask[0:ST, g:g + 1])
                            last.then_inc(w.stacked, 1)

                        def weights(G, tile):
                            u, g = G * a.units + tile // GH, tile % GH
                            act.wait_ge(w.scored, a.past("scored") + G * a.tiles + tile + 1)
                            if a.kind == "causal" and u == 1 and g == 0:
                                act.wait_ge(w.k_masked, NG)
                            if u >= 2 and g == 0:
                                act.wait_ge(w.pv_done, a.past("pv_done") + u - 1)
                            bank = w.bank[a.bank_of("score", G * a.tiles + tile)]
                            if a.kind == "causal":
                                lo = tile // GH * P
                                copy(w.pt[:, u % 2, g, lo:S], bank[:, lo:S]).then_inc(w.weighted, 1)
                            else:
                                actv(w.pt[:, u % 2, g, :], bank, ACT.Exp).then_inc(w.weighted, 1)

                        def outputs(G):
                            act.wait_ge(w.pv_done, a.past("pv_done") + (G + 1) * a.units)
                            if G >= 2:
                                act.wait_ge(w.o_turned, a.past("o_turned") + G - 1)
                            copy(w.o_sb[:, G % 2, :], w.bank[3]).then_inc(w.o_out, 1)

                        for i in range(2 * NG):
                            if i not in a.late:
                                yield a.place_select(i)
                                stack_rows(i)
                        for G in range(NG):
                            for tile in range(a.tiles):
                                yield at(f"{a.name} group {G}", tile / a.tiles)
                                for i in a.select_beside(G, tile):
                                    stack_rows(i)
                                weights(G, tile)
                                if tile == GH - 1 and G:
                                    yield at(f"{a.name} group {G}", (tile + 0.5) / a.tiles)
                                    outputs(G - 1)
                        yield at(f"{a.name} tail")
                        outputs(NG - 1)
                        yield at(f"{a.name} tail", 0.5)
                        take(w, w.heads_T[:, :], w.bank[1], f"heads {a.name}")

                    def stream(w):
                        lin, cross0, cross1, *experts = attentions(w)
                        yield from attention(w, lin)
                        yield at("norm 1", 0.8)
                        take(w, w.x_T[:, :], w.bank[0], "x 1")
                        yield from attention(w, cross0)

                        yield at("unit norm", 0.8)
                        take(w, w.xn_T[:, :], w.bank[0], "xn")
                        def rows_out(which):
                            act.wait_ge(w.rows_turned, which + 1)
                            copy(w.nm_row[:, which, :], w.bank16[0][0:2, 0:S]).then_inc(w.rows_out, 1)

                        yield at("logits", 0.42)
                        rows_out(0)
                        for j in range(NT):
                            yield at("weights", j / (2 * NT))
                            act.wait_ge(w.rescored, j + 1)
                            actv(w.comb[:, j, :], w.bank[j], ACT.Exp).then_inc(w.mix_weights, 1)
                        yield at("weights", 0.5)
                        rows_out(1)
                        for j in range(NT):
                            yield at("weights", 0.5 + j / (2 * NT))
                            act.wait_ge(w.rescored, NT + j + 1)
                            actv(w.disp[:, j, :], w.bank[(j + 1) % NT], ACT.Exp).then_inc(w.mix_weights, 1)
                        yield at("hidden")
                        take(w, w.slots_T[:, :], w.bank[2], "slots")
                        for k in range(NT):
                            yield at("hidden", 0.2 + 0.2 * k)
                            act.wait_ge(w.hidden, k + 1)
                            actv(w.hid[:, k, :], w.bank[k], ACT.Gelu).then_inc(w.hidden_out, 1)
                        yield at("processed", 0.9)
                        act.wait_ge(w.processed, 1)
                        copy(w.proc[:, :, 0:D], w.y).then_inc(w.processed_out, 1)
                        yield at("norm 3", 0.8)
                        take(w, w.x_T[:, :], w.bank[0], "x 3")

                        for G in range(NG):
                            yield at("queries", G / NG)
                            act.wait_ge(w.f_q, G + 1)
                            actv(w.qp[:, G, :], w.bank[G], ACT.Exp, bias=bqf[:, G:G + 1]).then_inc(w.f_q_exp, 1)
                        for i in range(NT):
                            yield at("keys", (i + 0.5) / NT)
                            act.wait_ge(w.f_k_biased, i + 1)
                            actv(w.kp[:, i, :], w.kpre[:, i % 2, :], ACT.Exp).then_inc(w.f_k_exp, 1)
                        yield at("scale", 0.2)
                        take(w, w.kx_T[:, :], w.bank[2], "kx")
                        yield at("norm 4", 0.8)
                        take(w, w.x_T[:, :], w.bank[0], "x 4")
                        yield from attention(w, cross1)
                        yield at("norm 5", 0.8)
                        take(w, w.x_T[:, :], w.bank[0], "x 5")

                        yield at("gate", 0.5)
                        act.wait_ge(w.g_top, 1)
                        actv(w.gexp[0:1, 0:NE], w.gdiff[0:1, 0:NE], ACT.Exp, accum_out=w.gsum[0:1, 0:1])
                        actv(w.gexp[0:1, 4:6], w.gdiff[0:1, 4:6], ACT.Exp).then_inc(w.g_exp, 1)

                        for s in range(TOPK):
                            yield from attention(w, experts[s])
                            yield at(f"norm x1 {s}", 0.8)
                            take(w, w.x1_T[:, :], w.bank[0], f"x1 {s}")
                            for k in range(NT):
                                yield at(f"mlp {s}", k / 8)
                                act.wait_ge(w.hidden, NT * (s + 1) + k + 1)
                                actv(w.hid[:, k, :], w.bank[k], ACT.Relu, bias=w.ew[:, EB + k:EB + k + 1])\
                                    .then_inc(w.hidden_out, 1)

                    by_plan(stream(s0), stream(s1))

                @block.vector
                def _(dve):
                    V = nc.vector
                    step = [0]

                    def link(ins):
                        step[0] += 1
                        ins.then_inc(dve_step, 1)
                        dve.wait_ge(dve_step, step[0])

                    def attention(w, a):
                        for i, (full, hi, lo, n) in enumerate(((w.k_full, w.k_hi, w.k_lo, a.nk),
                                                               (w.q_full, w.q_hi, w.q_lo, S))):
                            yield at(f"{a.name} select", 0.1 + 0.05 * i)
                            dve.wait_ge(w.biased, a.past("biased") + i + 1)
                            if a.kind == "causal":
                                link(V.tensor_scalar(full[:, 0:n], full[:, 0:n], 0.0, 1e-6 * LSCALE, ALU.max, ALU.add))
                            link(V.tensor_copy(hi[:, 0:n], full[:, 0:n]))
                            V.tensor_tensor(lo[:, 0:n], full[:, 0:n], hi[:, 0:n], ALU.subtract).then_inc(w.split, 1)
                        yield at(f"{a.name} select", 0.2)
                        dve.wait_ge(w.projected, a.past("projected") + 3)
                        if a.expert is not None:
                            dve.wait_ge(w.e_rest, 32 * (a.expert + 1))
                        V.tensor_tensor(w.v[:, 0:a.units, 0:H * (DH + 1)].rearrange("p k (h c) -> p k h c", h=H)[:, :, :, 0:DH],
                                        w.bank[2][:, 0:a.units * D].rearrange("p (k h d) -> p k h d", k=a.units, h=H),
                                        a.bv.rearrange("p (h d) -> p h d", h=H).unsqueeze(1)
                                        .to_broadcast([P, a.units, H, DH]), ALU.add).then_inc(w.v_ready, 1)

                        if a.expert == 0:
                            yield at("expert 0 select", 0.25)
                            dve.wait_ge(w.g_exp, 1)
                            link(V.reciprocal(w.gsum[0:1, 1:2], w.gsum[0:1, 0:1]))
                            V.tensor_scalar(w.gw1[:, :], w.gexp[0:1, 4:6], w.gsum[0:1, 1:2], None, ALU.mult)\
                                .then_inc(w.g_weights, 1)
                            yield at("expert 0 select", 0.5)
                            dve.wait_ge(w.g_spread, 1)
                            V.tensor_copy(w.gw[:, :], w.bank[3][:, 8:10]).then_inc(w.g_ready, 1)
                        if a.kind == "causal":
                            for G in range(NG):
                                yield a.place_select(2 * G)
                                dve.wait_ge(w.stacked, 2 * G + 1)
                                for g in range(GH):
                                    last = V.tensor_scalar(w.k_st[0:ST, G, g, 0:a.nk], w.k_dense[0:ST, G, 0:a.nk],
                                                           colmask[0:ST, g:g + 1], None, ALU.mult)
                                last.then_inc(w.k_masked, 1)

                        def reduce(n):
                            G, i = divmod(n, a.msteps)
                            dve.wait_ge(w.max_scored, a.past("max_scored") + n + 1)
                            if a.self_keys:
                                qt, g = i // GH, i % GH
                                V.tensor_reduce(w.neg_max[:, G, qt, g:g + 1], w.bank[a.bank_of("max", n)][:, 0:a.nk], AX.X, ALU.max,
                                                negate=True).then_inc(w.reduced, 1)
                            else:
                                qt, g = i // 2, 2 * (i % 2)
                                V.tensor_reduce(w.neg_max[:, G, qt, g:g + 2],
                                                w.bank[a.bank_of("max", n)][:, 0:2 * SKP].rearrange("p (j k) -> p j k", j=2), AX.X,
                                                ALU.max, negate=True).then_inc(w.reduced, 1)

                        def parts(G):
                            dve.wait_ge(w.reduced, a.past("reduced") + (G + 1) * a.msteps)
                            link(V.tensor_scalar(w.m_full[:, :, :], w.neg_max[:, G, :, :], MCAP, 1.0 / MSCALE,
                                                 ALU.min, ALU.mult))
                            if G:
                                dve.wait_ge(w.m_turned, a.past("m_turned") + G)
                            link(V.tensor_copy(w.m_parts[:, :, 0, :], w.m_full[:, :, :]))
                            V.tensor_tensor(w.m_parts[:, :, 1, :], w.m_full[:, :, :], w.m_parts[:, :, 0, :], ALU.subtract)\
                                .then_inc(w.m_parts_ready, 1)

                        def m_rows(G):
                            dve.wait_ge(w.m_turned, a.past("m_turned") + G + 1)
                            V.tensor_copy(w.q_st[ST:MR, G, :], w.bank16[a.bank_of("turn", G)][ST:MR, 0:S])\
                                .then_inc(w.m_rows, 1)

                        def diagonal(G, tile):
                            u, (kt, g) = G * a.units + tile // GH, divmod(tile, GH)
                            dve.wait_ge(w.weighted, a.past("weighted") + G * a.tiles + tile + 1)
                            block_ = w.pt[:, u % 2, g, kt * P:(kt + 1) * P]
                            V.tensor_tensor(block_, block_, causal[:, :], ALU.mult).then_inc(w.diagonal, 1)

                        def normalise(G):
                            dve.wait_ge(w.o_turned, a.past("o_turned") + G + 1)
                            if G >= 2:
                                dve.wait_ge(w.normed, a.past("normed") + G - 1)
                            rden = w.rden[:, G % 2, :, :]
                            o = w.bank[a.bank_of("out", G)].rearrange("p (t g c) -> p t g c", t=NT, g=GH)
                            if a.kind in ("causal", "cross_key"):
                                link(V.tensor_scalar(rden, o[:, :, :, DH], 1e-6 * LSCALE ** 2 if a.kind == "causal" else 1e-30,
                                                     None, ALU.max))
                                link(V.reciprocal(rden, rden))
                            else:
                                link(V.reciprocal(rden, o[:, :, :, DH]))
                            c = GH * DH * G
                            V.tensor_tensor(w.heads[:, :, c:c + GH * DH].rearrange("p t (g d) -> p t g d", g=GH),
                                            o[:, :, :, 0:DH], rden.unsqueeze(3).to_broadcast([P, NT, GH, DH]),
                                            ALU.mult).then_inc(w.normed, 1)

                        for n in a.steps_first():
                            yield a.place_max(n)
                            if n == a.msteps:
                                parts(0)
                            if n == a.msteps + 1:
                                m_rows(0)
                            reduce(n)
                        for G in range(NG):
                            for tile in range(a.tiles):
                                yield at(f"{a.name} group {G}", tile / a.tiles)
                                if tile and a.has_max and a.follows("turn", G, tile - 1):
                                    m_rows(G + 1)
                                if a.kind == "causal":
                                    diagonal(G, tile)
                                for n in a.steps_beside(G, tile):
                                    if n > a.steps_beside(G, tile)[0]:
                                        yield at(f"{a.name} group {G}", (tile + 0.5) / a.tiles)
                                    reduce(n)
                                    if n == (G + 2) * a.msteps - 1:
                                        parts(G + 1)
                                yield at(f"{a.name} group {G}", (tile + 0.5) / a.tiles)
                                if a.follows("out", G, tile):
                                    normalise(G - 1)
                        yield at(f"{a.name} tail", 0.3)
                        normalise(NG - 1)

                    def rsqrt(w, npow, phase, src, eps, op=ALU.add):
                        k = npow[0]
                        V.tensor_scalar(w.var[:, k, :], src, eps, None, op).then_inc(w.var_ready, 1)
                        yield at(phase, 0.6)
                        dve.wait_ge(w.rstd_ready, k + 1)
                        npow[0] += 1

                    def layernorm(w, npow, phase, dst):
                        for i in range(NT):
                            last = V.bn_stats(w.stats[:, i, :], w.r[:, i, :])
                        link(last)
                        for i in range(NT):
                            last = V.bn_aggr(w.mv[:, i, :], w.stats[:, i, :])
                        link(last)
                        yield from rsqrt(w, npow, phase, w.mv[:, :, 1], LN_EPS)
                        for i in range(NT):
                            last = V.tensor_scalar(dst[:, i, 0:D], w.r[:, i, :], w.mv[:, i, 0:1],
                                                   w.rstd[:, npow[0] - 1, i:i + 1], ALU.subtract, ALU.mult)
                        return last

                    def stream(w):
                        lin, cross0, cross1, *experts = attentions(w)
                        npow, nxb = [0], [0]

                        def add_residual(ready, count, phase):
                            yield at(phase)
                            dve.wait_ge(ready, count)
                            nxb[0] += 1
                            dve.wait_ge(w.xb_done, nxb[0])
                            link(V.tensor_tensor(w.r[:, :, :], w.y, w.xb[:, :, :], ALU.add))

                        def new_x(phase):
                            last = yield from layernorm(w, npow, phase, w.x)
                            last.then_inc(w.x_done, 1)

                        yield at("lin select")
                        dve.wait_ge(w.mask_loaded, 16)
                        V.tensor_scalar(w.bias_k[:, :], w.mask_k[:, :], 0, -BIG, ALU.is_equal, ALU.mult)
                        V.memset(w.q_st[ST:MR, :, :], 0.0).then_inc(w.bias_ready, 1)
                        yield from attention(w, lin)
                        yield from add_residual(w.y_ready, 1, "norm 1")
                        yield from new_x("norm 1")
                        yield from attention(w, cross0)
                        yield from add_residual(w.y_ready, 2, "norm 2")
                        yield from new_x("norm 2")

                        yield at("unit norm")
                        dve.wait_ge(w.x_done, 2)
                        link(V.tensor_tensor(w.r[:, :, :], w.x[:, :, 0:D], w.x[:, :, 0:D], ALU.mult))
                        link(V.tensor_reduce(w.nmax[:, 0, :], w.r[:, :, :], AX.X, ALU.add))
                        yield from rsqrt(w, npow, "unit norm", w.nmax[:, 0, :], 1e-24, ALU.max)
                        for i in range(NT):
                            last = V.scalar_tensor_tensor(out=w.xn[:, i, 0:D], in0=w.x[:, i, 0:D],
                                                          scalar=w.rstd[:, npow[0] - 1, i:i + 1],
                                                          in1=rows[:, 7, :], op0=ALU.mult, op1=ALU.mult)
                        last.then_inc(w.mix_normed, 1)
                        for which in range(2):
                            for i in range(NT):
                                yield at("logits", 0.5 * which + i / (2 * NT))
                                dve.wait_ge(w.logits, NT * which + i + 1)
                                V.tensor_reduce(w.nmax[:, which, i:i + 1], w.bank[i], AX.X, ALU.max, negate=True)\
                                    .then_inc(w.logits_max, 1)
                            yield at("logits", 0.5 * which + 0.42)
                            dve.wait_ge(w.logits_max, (NT + 1) * which + NT)
                            link(V.tensor_scalar(w.nm_full[:, which, :], w.nmax[:, which, :], 1.0 / MSCALE, None, ALU.mult))
                            link(V.tensor_copy(w.nm_parts[:, which, :, 0], w.nm_full[:, which, :]))
                            V.tensor_tensor(w.nm_parts[:, which, :, 1], w.nm_full[:, which, :], w.nm_parts[:, which, :, 0],
                                            ALU.subtract).then_inc(w.logits_max, 1)
                        yield at("slots", 0.9)
                        dve.wait_ge(w.slots_summed, 1)
                        pairs = lambda a: a.rearrange("p (a b) -> p a b", a=2)
                        link(V.reciprocal(pairs(w.rsum[:, 0, :]), w.four[:, :, :, D]))
                        for j in range(NT):
                            last = V.tensor_scalar(w.slots[:, j, :], w.four[:, j // 2, j % 2, 0:D], w.rsum[:, 0, j:j + 1],
                                                   None, ALU.mult)
                        last.then_inc(w.slots_out, 1)
                        yield at("norm 3")
                        dve.wait_ge(w.combined, 1)
                        link(V.reciprocal(pairs(w.rsum[:, 1, :]), w.four[:, :, :, D]))
                        for j in range(NT):
                            last = V.scalar_tensor_tensor(out=w.r[:, j, :], in0=w.four[:, j // 2, j % 2, 0:D],
                                                          scalar=w.rsum[:, 1, j:j + 1], in1=w.x[:, j, 0:D],
                                                          op0=ALU.mult, op1=ALU.add)
                        link(last)
                        yield from new_x("norm 3")

                        for i in range(NT):
                            yield at("keys", i / NT)
                            dve.wait_ge(w.f_k, i + 1)
                            if i >= 2:
                                dve.wait_ge(w.f_k_exp, i - 1)
                            V.tensor_tensor(w.kpre[:, i % 2, :], w.bank[i], bkf[:, :], ALU.add).then_inc(w.f_k_biased, 1)
                        yield at("scale")
                        dve.wait_ge(w.f_kx, 1)
                        link(V.tensor_copy(pairs(w.ks[:, :]), w.four[:, :, :, D]))
                        for G in range(NG):
                            V.tensor_scalar(w.ksc[:, G, :], headmask[:, G, :], w.ks[:, G:G + 1], None, ALU.mult)
                        V.tensor_copy(w.kx[:, :, :].rearrange("p (a b) d -> p a b d", a=2), w.four[:, :, :, 0:D])\
                            .then_inc(w.f_kx_out, 1)
                        yield at("scale", 0.3)
                        dve.wait_ge(w.f_den, 1)
                        link(V.tensor_scalar(w.den, w.bank[3][0:FH, :], 1e-6, None, ALU.add))
                        V.reciprocal(w.dinv, w.den).then_inc(w.f_den_inv, 1)
                        yield at("scale", 0.9)
                        dve.wait_ge(w.f_z, 1)
                        for G in range(NG):
                            last = V.scalar_tensor_tensor(out=w.z[:, G, :], in0=bvp[:, G, :], scalar=w.ks[:, G:G + 1],
                                                          in1=w.bank[0][:, G * D:(G + 1) * D], op0=ALU.mult, op1=ALU.add)
                        last.then_inc(w.f_z_out, 1)
                        for G in range(NG):
                            yield at("spread", G / NG)
                            dve.wait_ge(w.f_spread, G + 1)
                            V.tensor_tensor(w.qn[:, G, :], w.bank[(G + 1) % 4], w.qp[:, G, :], ALU.mult)\
                                .then_inc(w.f_scaled, 1)
                        yield from add_residual(w.f_y, 1, "norm 4")
                        yield from new_x("norm 4")
                        yield from attention(w, cross1)
                        yield from add_residual(w.y_ready, 3, "norm 5")
                        yield from new_x("norm 5")

                        yield at("gate")
                        dve.wait_ge(w.turned_out, turn_no("x 5"))
                        V.tensor_reduce(w.xsum[:, :], w.x_T[:, :], AX.X, ALU.add).then_inc(w.g_sum, 1)
                        yield at("gate", 0.3)
                        dve.wait_ge(w.g_logit, 1)
                        link(V.scalar_tensor_tensor(out=w.logit8[0:1, 0:NE], in0=w.bank[3][0:1, 0:NE], scalar=1.0 / S,
                                                    in1=gate_b[:, :], op0=ALU.mult, op1=ALU.add))
                        link(V.max(w.top8[:, :], w.logit8[:, :]))
                        V.max_index(w.idx8[:, :], w.top8[:, :], w.logit8[:, :])
                        V.tensor_scalar(w.gdiff[0:1, 0:NE], w.logit8[0:1, 0:NE], w.top8[0:1, 0:1], None, ALU.subtract)
                        V.tensor_scalar(w.gdiff[0:1, 4:6], w.top8[0:1, 0:2], w.top8[0:1, 0:1], None, ALU.subtract)\
                            .then_inc(w.g_top, 1)
                        for s in range(TOPK):
                            yield at(f"expert {s} select")
                            dve.wait_ge(w.e_in, 16 * (s + 1))
                            V.tensor_scalar(w.ebq[:, s:s + 1], w.ew[:, EIN - 2:EIN - 1], DH ** -0.5, None, ALU.mult)\
                                .then_inc(w.e_bias, 1)
                            yield from attention(w, experts[s])
                            yield from add_residual(w.y_ready, s + 4, f"norm x1 {s}")
                            last = yield from layernorm(w, npow, f"norm x1 {s}", w.norm)
                            link(last)
                            wide = lambda k: w.er[:, k, :].unsqueeze(1).to_broadcast([P, NT, D])
                            link(V.tensor_tensor(w.norm, w.norm, wide(2), ALU.mult))
                            V.tensor_tensor(w.x1, w.norm, wide(3), ALU.add).then_inc(w.e_x1, 1)
                            yield from add_residual(w.e_y2, s + 1, f"norm y {s}")
                            last = yield from layernorm(w, npow, f"norm y {s}", w.norm)
                            link(last)
                            link(V.tensor_tensor(w.norm, w.norm, wide(5), ALU.mult))
                            link(V.tensor_tensor(w.norm, w.norm, wide(6), ALU.add))
                            out, prev = (w.acc, w.x[:, :, 0:D]) if s == 0 else (w.r[:, :, :], w.acc)
                            ins = V.scalar_tensor_tensor(out=out, in0=w.norm, scalar=w.gw[:, s:s + 1], in1=prev,
                                                         op0=ALU.mult, op1=ALU.add)
                            if s == 0:
                                ins.then_inc(w.e_done, 1)
                            else:
                                link(ins)
                        yield from new_x("norm 6")

                    by_plan(stream(s0), stream(s1))

            nc.all_engine_barrier()
            nc.gpsimd.sem_clear(range(sems[0].num, sems[-1].num + 1))
            nc.all_engine_barrier()


def constants():
    import numpy as np
    c32 = np.zeros((P, 2 * P + GH + NG * FH), np.float32)
    p = np.arange(P)
    c32[:, 0:P] = np.eye(P)
    c32[:, P:2 * P] = p[:, None] <= p[None, :]
    for g in range(GH):
        c32[:, 2 * P + g] = (p % 32) // DH == g
    for G in range(NG):
        for g in range(GH):
            c32[32 * g:32 * g + 32, 2 * P + GH + G * FH + GH * G + g] = 1
    headrep = np.zeros((FH, NG, P), np.float32)
    for h in range(FH):
        headrep[h, h // GH, (h % GH) * FF:(h % GH + 1) * FF] = 1
    sel = np.zeros((2, P, 2, NG, ST), np.float16)
    for G in range(NG):
        for part in range(3):
            for c in range(32):
                sel[0, 32 * G + c, int(part == 1), G, 32 * part + c] = 1
                sel[1, 32 * G + c, int(part == 2), G, 32 * part + c] = 1
    c16 = np.concatenate([np.eye(P), BIG * np.eye(P), sel[0].reshape(P, -1), sel[1].reshape(P, -1)], 1).astype(np.float16)
    krow = np.zeros((2, GH, NG, GH), np.float16)
    for g in range(GH):
        krow[:, g, :, g] = MSCALE
    krow = krow.reshape(2 * GH, NG, GH, 1)
    return {
        "c32": c32, "c16": c16, "headrep": headrep,
        "krows": np.ascontiguousarray(np.broadcast_to(krow, (2 * GH, NG, GH, S))),
        "scale_rows": np.full((2, P), MSCALE, np.float16),
        "bigrow": np.full((1, NG, S), BIG, np.float16),
    }


def layout(i):
    import numpy as np
    i = {k: np.asarray(a) for k, a in i.items()}
    cut = lambda w: w.reshape(-1, P, w.shape[1]).transpose(1, 0, 2)
    per_head = lambda w: w.reshape(FH, FD, D).transpose(1, 0, 2)
    qkv = i["L0_attn_qkv_w"].T
    kv, bkv = i["L0_xattn_Wkv"], i["L0_xattn_bkv"]
    mats = [qkv[:, 0:D], qkv[:, D:2 * D], qkv[:, 2 * D:], i["L0_attn_out_w"].T, i["L0_xattn_Wq"], kv[:, 0:D], kv[:, D:],
            i["L0_xattn_Wout"], i["L1_xattn_Wq"].T, i["L1_xattn_Wk"].T, i["L1_xattn_Wv"].T, i["L1_xattn_Wo"].T]
    qb = i["L0_attn_qkv_b"]
    ew = np.concatenate([
        i["L1_ffn_in_proj_w"].transpose(0, 2, 1),
        i["L1_ffn_in_proj_b"][:, 0:2 * D].reshape(NE, 2, D).transpose(0, 2, 1), i["L1_ffn_out_proj_w"].transpose(0, 2, 1),
        i["L1_ffn_lin1_w"].transpose(0, 2, 1),
        i["L1_ffn_lin2_w"].transpose(0, 2, 1).reshape(NE, HID // P, P, D).transpose(0, 2, 1, 3).reshape(NE, P, HID),
        i["L1_ffn_lin1_b"].reshape(NE, HID // P, P).transpose(0, 2, 1)], 2)
    er = np.stack([i["L1_ffn_in_proj_b"][:, 2 * D:], i["L1_ffn_out_proj_b"], i["L1_ffn_ln1_w"], i["L1_ffn_ln1_b"],
                   i["L1_ffn_lin2_b"], i["L1_ffn_ln2_w"], i["L1_ffn_ln2_b"]], 1)
    return {
        "x": i["x"], "x_T": i["x"].transpose(0, 2, 1), "ctx_T": i["ctx_1024"].transpose(0, 2, 1),
        "mask_k": i["mask_Bx1xS2_if1"],
        "mask_q": i["mask_1x1xSxS2_ik0"].reshape(NT, P, SK).transpose(1, 0, 2),
        "mask_kq": i["mask_1x1xSxS2_ik0"].reshape(S, SK).T,
        "w_a": np.stack(mats, 1),
        "cols": np.stack([qb[0:D], qb[D:2 * D], i["L0_xattn_bq"], bkv[0:D], i["L1_xattn_bq"], i["L1_xattn_bk"]], 1),
        "rows": np.stack([qb[2 * D:], i["L0_attn_out_b"], bkv[D:], i["L0_xattn_bout"], i["L1_xattn_bv"],
                          i["L1_xattn_bo"], i["L1_attn_bproj"], i["L0_ffn_gamma_x"], i["L0_ffn_gamma_slot"]], 0),
        "w1": i["L0_ffn_w1"], "w2": cut(i["L0_ffn_w2"]), "slots": cut(i["L0_ffn_slot_embeds"].reshape(NSLOT, D)),
        "wq_t": per_head(i["L1_attn_Wq"].T), "wk_t": per_head(i["L1_attn_Wk"].T), "wv_t": per_head(i["L1_attn_Wv"].T),
        "wp": per_head(i["L1_attn_Wproj"]), "feat": np.stack([i["L1_attn_wq_feat"], i["L1_attn_wk_feat"]], 1),
        "fbias": np.stack([i[f"L1_attn_b{n}"].reshape(FH, FD).T for n in "qkv"], 1),
        "gate_w": i["L1_ffn_gate_w"].T, "gate_b": i["L1_ffn_gate_b"].reshape(1, NE), "ew": ew, "er": er,
    }


def kernel(**inputs):
    import numpy as _np
    import concourse.bacc as _bacc
    from concourse import mybir as _mybir
    from concourse.bass_utils import run_bass_kernel_spmd as _run

    nc = _bacc.Bacc("TRN2", target_bir_lowering=False, num_devices=1)
    arrays, aps = {}, {}
    for name, a in {**layout(inputs), **constants()}.items():
        arrays[f"in_{name}"] = _np.ascontiguousarray(a)
        aps[name] = nc.dram_tensor(f"in_{name}", a.shape, _mybir.dt.from_np(a.dtype), kind="ExternalInput").ap()
    aps["out"] = nc.dram_tensor("out_0", (B, S, D), _mybir.dt.float32, kind="ExternalOutput").ap()
    build(nc, aps)
    r = _run(nc, [arrays], core_ids=[0])
    return r.results[0]["out_0"]
```
